# Optimizing a Trainium2 kernel written in Bass

```python
import numpy as np
import jax
import jax.numpy as jnp

def _softmax(x, axis=-1):
    return jax.nn.softmax(x, axis=axis)

def _gelu(x):
    return jax.nn.gelu(x, approximate=True)

def _silu(x):
    return jax.nn.silu(x)

def _sigmoid(x):
    return jax.nn.sigmoid(x)

def _layernorm(x, axis=-1, eps=1e-05):
    m = jnp.mean(x, axis=axis, keepdims=True)
    v = jnp.var(x, axis=axis, keepdims=True)
    return (x - m) / jnp.sqrt(v + eps)

def _scatter_add(tgt, idx, src, axis=0):
    return tgt.at[idx].add(src)

def _segment_sum(src, seg, n):
    return jax.ops.segment_sum(src, seg, n)
kernel_name = 'mk_seq_postln_d1_jaxref_r4_d93ed7'

def setup_inputs(seed: int=0):
    np.random.seed(seed)
    _w = jnp.asarray

    def _L0_attn_setup():
        import jax, jax.numpy as jnp
        import numpy as np
        D_MODEL = 256
        N_HEADS = 16
        HEAD_DIM = D_MODEL // N_HEADS
        N_EXPERTS = 4
        HIDDEN = 4 * D_MODEL
        B, T = (1, 512)

        def _apply_rope(x, sin, cos):
            x1, x2 = (x[..., ::2], x[..., 1::2])
            r1 = x1 * cos - x2 * sin
            r2 = x1 * sin + x2 * cos
            return jnp.stack((r1, r2), axis=-1).reshape(x.shape)
        key = jax.random.key(seed)
        ks = jax.random.split(key, 16)
        s = 0.02
        d, E, Hd = (D_MODEL, N_EXPERTS, HIDDEN)
        return {'x': jax.random.normal(ks[0], (B, T, d), dtype=jnp.float32), 'w_dw': jax.random.normal(ks[1], (d, 3), dtype=jnp.float32) * s, 'w_pw': jax.random.normal(ks[2], (d, d), dtype=jnp.float32) * s, 'w_qkv': jax.random.normal(ks[3], (3 * d, d), dtype=jnp.float32) * s, 'w_o': jax.random.normal(ks[4], (d, d), dtype=jnp.float32) * s, 'w_gate': jax.random.normal(ks[5], (d, d), dtype=jnp.float32) * s, 'b_gate': jnp.zeros((d,), dtype=jnp.float32), 'ln_g': jnp.ones((d,), dtype=jnp.float32), 'ln_b': jnp.zeros((d,), dtype=jnp.float32), 'w_moe_gate': jax.random.normal(ks[6], (E, d), dtype=jnp.float32) * s, 'w1': jax.random.normal(ks[7], (E, Hd, d), dtype=jnp.float32) * s, 'b1': jnp.zeros((E, Hd), dtype=jnp.float32), 'w2': jax.random.normal(ks[8], (E, d, Hd), dtype=jnp.float32) * s, 'b2': jnp.zeros((E, d), dtype=jnp.float32)}
    _L0_attn_in = _L0_attn_setup()

    def _L0_ffn_setup():
        import jax, jax.numpy as jnp
        import numpy as np
        N_EMBD = 256
        NUM_EXPERTS = 8
        TOP_K = 2
        D_FF = 4 * N_EMBD
        B, S = (4, 512)
        key = jax.random.key(seed)
        ks = jax.random.split(key, 7)
        scale = lambda fan_in: 1.0 / np.sqrt(fan_in)
        x = jax.random.normal(ks[0], (B, S, N_EMBD), dtype=jnp.float32)
        W_router = jax.random.normal(ks[1], (N_EMBD, NUM_EXPERTS), dtype=jnp.float32) * scale(N_EMBD)
        b_router = jnp.zeros((NUM_EXPERTS,), dtype=jnp.float32)
        W1 = jax.random.normal(ks[2], (NUM_EXPERTS, N_EMBD, D_FF), dtype=jnp.float32) * scale(N_EMBD)
        b1 = jnp.zeros((NUM_EXPERTS, D_FF), dtype=jnp.float32)
        W2 = jax.random.normal(ks[3], (NUM_EXPERTS, D_FF, N_EMBD), dtype=jnp.float32) * scale(D_FF)
        b2 = jnpp = jnp.zeros((NUM_EXPERTS, N_EMBD), dtype=jnp.float32)
        return {'x': x, 'W_router': W_router, 'b_router': b_router, 'W1': W1, 'b1': b1, 'W2': W2, 'b2': b2}
    _L0_ffn_in = _L0_ffn_setup()
    _d = {'L0_attn_x': _L0_attn_in['x'], 'L0_attn_w_dw': _L0_attn_in['w_dw'], 'L0_attn_w_pw': _L0_attn_in['w_pw'], 'L0_attn_w_qkv': _L0_attn_in['w_qkv'], 'L0_attn_w_o': _L0_attn_in['w_o'], 'L0_attn_w_gate': _L0_attn_in['w_gate'], 'L0_attn_b_gate': _L0_attn_in['b_gate'], 'L0_attn_ln_g': _L0_attn_in['ln_g'], 'L0_attn_ln_b': _L0_attn_in['ln_b'], 'L0_attn_w_moe_gate': _L0_attn_in['w_moe_gate'], 'L0_attn_w1': _L0_attn_in['w1'], 'L0_attn_b1': _L0_attn_in['b1'], 'L0_attn_w2': _L0_attn_in['w2'], 'L0_attn_b2': _L0_attn_in['b2'], 'L0_ffn_W_router': _L0_ffn_in['W_router'], 'L0_ffn_b_router': _L0_ffn_in['b_router'], 'L0_ffn_W1': _L0_ffn_in['W1'], 'L0_ffn_b1': _L0_ffn_in['b1'], 'L0_ffn_W2': _L0_ffn_in['W2'], 'L0_ffn_b2': _L0_ffn_in['b2']}
    _x0 = _d['L0_attn_x']
    _d['L0_attn_x'] = jax.random.normal(jax.random.fold_in(jax.random.key(seed), 1), (2, 2048, 256), dtype=_x0.dtype)
    del _x0
    return _d

def reference(L0_attn_x, L0_attn_w_dw, L0_attn_w_pw, L0_attn_w_qkv, L0_attn_w_o, L0_attn_w_gate, L0_attn_b_gate, L0_attn_ln_g, L0_attn_ln_b, L0_attn_w_moe_gate, L0_attn_w1, L0_attn_b1, L0_attn_w2, L0_attn_b2, L0_ffn_W_router, L0_ffn_b_router, L0_ffn_W1, L0_ffn_b1, L0_ffn_W2, L0_ffn_b2):

    def _L0_attn_ref(x, w_dw, w_pw, w_qkv, w_o, w_gate, b_gate, ln_g, ln_b, w_moe_gate, w1, b1, w2, b2):
        import jax, jax.numpy as jnp
        import numpy as np
        D_MODEL = 256
        N_HEADS = 16
        HEAD_DIM = D_MODEL // N_HEADS
        N_EXPERTS = 4
        HIDDEN = 4 * D_MODEL
        B, T = (1, 512)

        def _apply_rope(x, sin, cos):
            x1, x2 = (x[..., ::2], x[..., 1::2])
            r1 = x1 * cos - x2 * sin
            r2 = x1 * sin + x2 * cos
            return jnp.stack((r1, r2), axis=-1).reshape(x.shape)
        Bv, Tv, d = x.shape
        H, Dh = (N_HEADS, HEAD_DIM)
        dt = x.dtype
        xp = jnp.pad(x, ((0, 0), (2, 0), (0, 0)))
        y = xp[:, 0:Tv] * w_dw[:, 0] + xp[:, 1:Tv + 1] * w_dw[:, 1] + xp[:, 2:Tv + 2] * w_dw[:, 2]
        y = jnp.einsum('btd,ed->bte', y, w_pw)
        x = x + y
        qkv = jnp.einsum('btd,ed->bte', x, w_qkv).reshape(Bv, Tv, 3, H, Dh)
        q, k, v = (qkv[:, :, 0], qkv[:, :, 1], qkv[:, :, 2])
        inv_freq = 1.0 / 10000.0 ** (jnp.arange(0, Dh, 2, dtype=dt) / Dh)
        pos = jnp.arange(Tv, dtype=dt)
        theta = pos[:, None] * inv_freq[None, :]
        sin = jnp.sin(theta)[None, :, None, :]
        cos = jnp.cos(theta)[None, :, None, :]
        q = _apply_rope(q, sin, cos)
        k = _apply_rope(k, sin, cos)
        q_phi = jax.nn.elu(q) + 1.0
        k_phi = jax.nn.elu(k) + 1.0
        kv = k_phi[..., :, None] * v[..., None, :]
        kv_prefix = jnp.cumsum(kv, axis=1)
        k_prefix = jnp.cumsum(k_phi, axis=1)
        num = jnp.einsum('bthd,bthdm->bthm', q_phi, kv_prefix)
        denom = jnp.sum(q_phi * k_prefix, axis=-1, keepdims=True)
        attn = num / (denom + 1e-06)
        attn = attn.reshape(Bv, Tv, d)
        attn = jnp.einsum('btd,ed->bte', attn, w_o)
        delta = x - jnp.concatenate([x[:, :1], x[:, :-1]], axis=1)
        gate = jax.nn.sigmoid(jnp.einsum('btd,ed->bte', delta, w_gate) + b_gate)
        x = x + gate * attn
        mu = jnp.mean(x, axis=-1, keepdims=True)
        var = jnp.mean((x - mu) ** 2, axis=-1, keepdims=True)
        h = (x - mu) / jnp.sqrt(var + 1e-05) * ln_g + ln_b
        gw = jax.nn.softmax(jnp.einsum('btd,ed->bte', h, w_moe_gate), axis=-1)
        hid = jax.nn.silu(jnp.einsum('btd,efd->btef', h, w1) + b1)
        eo = jnp.einsum('btef,edf->bted', hid, w2) + b2
        ffn = jnp.einsum('bte,bted->btd', gw, eo)
        return x + ffn

    def _L0_ffn_ref(x, W_router, b_router, W1, b1, W2, b2):
        import jax, jax.numpy as jnp
        import numpy as np
        N_EMBD = 256
        NUM_EXPERTS = 8
        TOP_K = 2
        D_FF = 4 * N_EMBD
        B, S = (4, 512)
        Bv, Sv, D = x.shape
        flat_x = x.reshape(-1, D)
        T = flat_x.shape[0]
        logits = flat_x @ W_router + b_router
        top_vals, top_idx = jax.lax.top_k(logits, TOP_K)
        neg_inf = jnp.full_like(logits, -jnp.inf)
        sparse_logits = neg_inf.at[jnp.arange(T)[:, None], top_idx].set(top_vals)
        router_weights = jax.nn.softmax(sparse_logits, axis=-1)
        final_output = jnp.zeros_like(flat_x)
        for e in range(NUM_EXPERTS):
            expert_mask = jnp.any(top_idx == e, axis=-1)
            h = jax.nn.relu(flat_x @ W1[e] + b1[e])
            y = h @ W2[e] + b2[e]
            w = router_weights[:, e] * expert_mask.astype(x.dtype)
            final_output = final_output + y * w[:, None]
        return final_output.reshape(Bv, Sv, D)
    x = L0_attn_x
    x = _layernorm(x + _L0_attn_ref(x, L0_attn_w_dw, L0_attn_w_pw, L0_attn_w_qkv, L0_attn_w_o, L0_attn_w_gate, L0_attn_b_gate, L0_attn_ln_g, L0_attn_ln_b, L0_attn_w_moe_gate, L0_attn_w1, L0_attn_b1, L0_attn_w2, L0_attn_b2), axis=-1)
    x = _layernorm(x + _L0_ffn_ref(x, L0_ffn_W_router, L0_ffn_b_router, L0_ffn_W1, L0_ffn_b1, L0_ffn_W2, L0_ffn_b2), axis=-1)
    return x

_drawn_inputs = setup_inputs


def setup_inputs(seed=0):
    import zlib

    import numpy as np

    out = dict(_drawn_inputs(seed))
    spreads = {'L0_attn_b_gate': (0.0, 2.0),
     'L0_attn_ln_g': (1.0, 0.551),
     'L0_attn_ln_b': (0.0, 0.473),
     'L0_attn_b1': (0.0, 0.1),
     'L0_attn_b2': (0.0, 0.1),
     'L0_ffn_b_router': (0.0, 0.1),
     'L0_ffn_b1': (0.0, 0.1),
     'L0_ffn_b2': (0.0, 0.1)}
    factors = {'L0_attn_w_qkv': 4.662, 'L0_attn_w_o': 5.094, 'L0_attn_w_gate': 8.0}
    for name, (base, spread) in spreads.items():
        noise = np.random.default_rng([zlib.crc32(name.encode()), seed]).standard_normal(out[name].shape)
        drawn = base * np.exp(spread * noise) if base else spread * noise
        out[name] = jnp.asarray(drawn.astype(out[name].dtype))
    for name, factor in factors.items():
        out[name] = (out[name] * factor).astype(out[name].dtype)
    return out
```

```python
from contextlib import ExitStack

import numpy as np

import concourse.bass as bass
from concourse import mybir

ALU = mybir.AluOpType
ACT = mybir.ActivationFunctionType
AX = mybir.AxisListType
F32 = mybir.dt.float32
F16 = mybir.dt.float16
U32 = mybir.dt.uint32
I32 = mybir.dt.int32

P = 128
B, T, D = 2, 2048, 256
NTOK = B * T
KD = D // P
CH = P
NCH = NTOK // CH
BLK = 512
CPB = BLK // CH
NBLK = NTOK // BLK
BPB = T // BLK
H, DH = 16, 16
HE = DH + 1
E1, FF = 4, 1024
FC = FF // P
E2 = 8
W1C, W2C = KD * FF, FC * D
WC = W1C + W2C
TILE = 256
CAP = NTOK + 2 * TILE
LEAST = 2 * NTOK // TILE
MOST = LEAST + E2
SCALE = 256.0
INV = 1.0 / SCALE
NR = 8
NG = NCH // NR
EPS = 1e-5

PW, QKV, WO, WG, MG, RT = 0, 512, 2048, 2560, 3072, 3080
SMALL = 3096

F_DVE = ["conv0a", "conv0b", "conv1a", "conv1b", "conv2a", "conv2b", "ylo", "halo", "x2", "first",
         "delta", "x2lo", "dlo", "rot_cos", "rot_sin_a", "rot_sin_b", "rot", "phimin", "gz", "phi"]
F_ACT = ["yhi", "x2hi", "dhi", "vext", "x2tok", "phiexp", "gt"]
F_PE = ["pw", "qk", "v", "gate", "x2t"]
T_DVE = ["qx0", "qx1", "keep", "mask0", "mask1", "mask2", "mask3", "den", "rden", "attn", "kvt",
         "kvadd", "alo", "g2", "x3", "bn", "aggr", "h0", "hlo", "gmax", "ngmax", "rsum", "gw"]
T_ACT = ["qT", "kT", "ahi", "hhi", "gexp"]
T_PE = ["phit", "score", "av", "kv", "at", "wo", "ht", "lg"]
T_POOL = ["xres", "veps", "rstd", "hg", "hb"]
R_DVE = ["bn", "aggr", "x5", "xlo", "lg", "top", "dlt", "topi", "m1", "m2", "m12", "rank", "p1", "p2",
         "cnt", "idx", "pos"]
R_ACT = ["xhi"]
R_PE = ["xt", "rl", "rk"]
R_POOL = ["veps", "rstd", "keepx", "sent"]


def build(nc, x, xT, small, wdw, rows, moe1, moe1_b, moe2, moe2_b, b2rows, rope, masks, out):
    nc.disable_value_cache = True
    with ExitStack() as ctx:
        def sb(name, shape, dt=F32):
            return ctx.enter_context(nc.sbuf_tensor(name, shape, dt))

        def ps(name):
            return ctx.enter_context(nc.psum_tensor(name, [P, 512], F32))

        def sem(name):
            return ctx.enter_context(nc.semaphore(name))

        xg = nc.dram_tensor("expert_rows", [E2 * CAP, D], F32, kind="Internal")
        yg = nc.dram_tensor("expert_out", [(MOST + E2) * TILE, D], F32, kind="Internal")

        stage = sb("stage", [P, 2, W1C])
        small_hi, small_lo = sb("small_hi", [P, SMALL], F16), sb("small_lo", [P, SMALL], F16)
        w_hi, w_lo = sb("w_hi", [P, E1, WC], F16), sb("w_lo", [P, E1, WC], F16)
        wdw_s = sb("wdw_s", [P, KD * 3])
        rows_s = sb("rows_s", [P, 3 * D + E2])
        b1_s = sb("b1_s", [P, E1 * FC])
        b1r_s = sb("b1r_s", [P, E2 * FC])
        nb2 = (E1 + E2) * D
        e_hi, e_lo = w_hi[:, 0:2, :], w_lo[:, 0:2, :]
        b2_f = w_hi[0:2, 2:4, :].rearrange("p s c -> p (s c)").bitcast(F32)[:, 0:nb2 + 2]
        b2_h = w_lo[0:2, 2:4, :].rearrange("p s c -> p (s c)")[:, 0:nb2]
        b2_l = w_lo[0:2, 2:4, :].rearrange("p s c -> p (s c)")[:, nb2:2 * nb2]
        b2_row = sb("b2_row", [P, (E1 + E2) * D], F16)
        rope_s = sb("rope_s", [P, T // CH, 2, DH])
        masks_s = sb("masks_s", [P, masks.shape[1]])
        MO = {}
        o = 0
        for name, n in (("ident", P), ("causal", P), ("block", H // 2 * HE), ("even", 1), ("odd", 1),
                        ("keep", NCH + 1), ("new", NCH + 1), ("iota8", E2), ("base", E2)):
            MO[name] = masks_s[:, o:o + n]
            o += n
        ident, causal = MO["ident"], MO["causal"]
        before = sb("before", [P, P], F16)
        ones = sb("ones", [P, P], F16)
        mhalf = sb("mhalf", [P, 1])
        px5 = sb("px5", [P, D])
        zeros = px5

        xall = sb("xall", [P, NCH, D])
        xTb = sb("xTb", [P, 2, KD, BLK + 2])
        yT = sb("yT", [P, KD, CH])
        y_hi, y_lo = sb("y_hi", [P, KD, CH], F16), sb("y_lo", [P, KD, CH], F16)
        x2T = sb("x2T", [P, KD, CH + 1])
        x2_hi, x2_lo = sb("x2_hi", [P, KD, CH], F16), sb("x2_lo", [P, KD, CH], F16)
        dT, d_hi, d_lo = yT, y_hi, y_lo
        vext = sb("vext", [P, H, HE])
        x2tok = sb("x2tok", [P, D])
        gz, gt = sb("gz", [P, D]), sb("gt", [P, D])
        r1, r2, rq = sb("r1", [P, 2 * D]), sb("r2", [P, 2 * D]), sb("rq", [P, 2 * D])
        phm, phe = r1, r2
        phi = sb("phi", [P, 2 * D])
        kTs, qTs = (r2[:, n * D:(n + 1) * D].rearrange("p (k n) -> p k n", k=KD) for n in range(2))
        qx = r1[:, :].rearrange("p (k a n) -> p k a n", k=KD, a=2)
        sm = sb("sm", [P, 4, 4, CH])
        state, kvt = sb("state", [P, KD, H // 2 * HE]), sb("kvt", [P, KD, H // 2 * HE])
        den, rden = sb("den", [P, H]), sb("rden", [P, H])
        attn = rq[:, 0:D]
        a_hi, a_lo = sb("a_hi", [P, KD, CH], F16), sb("a_lo", [P, KD, CH], F16)
        g2, x3 = gz, sb("x3", [P, D])
        bn, mv, rstd = sb("bn", [P, 6]), sb("mv", [P, 2]), sb("rstd", [P, 1])
        h0 = sb("h0", [P, D])
        hT_hi, hT_lo = sb("hT_hi", [P, 2, KD, BLK], F16), sb("hT_lo", [P, 2, KD, BLK], F16)
        gm, gn, ge, gs, gr = sb("gm", [P, 1]), sb("gn", [P, 1]), sb("ge", [P, E1]), sb("gs", [P, 1]), sb("gr", [P, 1])
        gw = sb("gw", [P, 2, CPB, E1])
        acc = sb("acc", [P, 2, CPB, D])
        s32 = sb("s32", [P, 2, BLK])
        h_hi, h_lo = sb("h_hi", [P, 4, BLK], F16), sb("h_lo", [P, 4, BLK], F16)
        pbn, pmv, prstd = sb("pbn", [P, 6]), sb("pmv", [P, 2]), sb("prstd", [P, 1])
        px_hi, px_lo = sb("px_hi", [P, KD, CH], F16), sb("px_lo", [P, KD, CH], F16)
        plg = sb("plg", [P, E2])
        top8 = sb("top8", [P, 8])
        topi = sb("topi", [P, 8], U32)
        m1, m2, m12 = sb("m1", [P, E2]), sb("m2", [P, E2]), sb("m12", [P, E2], F16)
        rank = sb("rank", [P, E2])
        count = sb("count", [P, E2])
        junk = sb("junk", [P, 2, E2])
        posf, pos = sb("posf", [P, 2]), sb("pos", [P, NCH, 2])
        idx, idx8 = sb("idx", [P, 2], U32), sb("idx8", [P, NR, 2], U32)
        cf, ci, ct = sb("cf", [P, E2]), sb("ci", [P, E2], I32), sb("ct", [P, E2], I32)
        ctf, cum = sb("ctf", [P, E2]), sb("cum", [P, E2])
        tabf = sb("tabf", [P, 3 * E2 + 1])
        tab = sb("tab", [P, 3 * E2 + 1], I32)
        xin, ysb = acc[:, 0, 0:2, :], acc[:, 1, 0:2, :]
        xt_hi, xt_lo = hT_hi[:, 0, :, 0:TILE], hT_lo[:, 0, :, 0:TILE]
        u32t = s32[:, :, :].rearrange("p a (b n) -> p (a b) n", n=TILE)
        u_hi, u_lo = (t[:, :, :].rearrange("p a (b n) -> p (a b) n", n=TILE) for t in (h_hi, h_lo))
        shift = junk[:, 0, :]
        move, moved = (g2[:, n * 2 * NCH:(n + 1) * 2 * NCH].rearrange("p (c a) -> p c a", a=2) for n in range(2))
        posy = g2[:, 4 * NCH:6 * NCH].rearrange("p (c a) -> p c a", a=2).bitcast(U32)
        dlt, wexp, wone = sb("dlt", [P, NCH]), *(kvt[:, 1, n * NCH:(n + 1) * NCH] for n in range(2))
        wt = sb("wt", [P, 2, NCH])
        rows8 = w_hi[:, :, :].rearrange("p e c -> p (e c)").bitcast(F32)[:, 0:NR * 2 * D]\
            .rearrange("p (r n d) -> p r n d", r=NR, n=2)
        fin = w_lo[:, :, :].rearrange("p e c -> p (e c)").bitcast(F32)[:, 0:2 * NR * D]\
            .rearrange("p (g r d) -> p g r d", g=2, r=NR)
        fbn, fmv = sb("fbn", [P, NR, 6]), sb("fmv", [P, NR, 2])
        fve, frs = sb("fve", [P, NR]), sb("frs", [P, NR])
        mhalf8 = kvt[:, 0, 0:NR]

        A = [ps(f"A{i}") for i in range(4)]
        Hb = [ps(f"H{i}") for i in range(2)]
        Yb = [ps(f"Y{i}") for i in range(2)]
        U = [A[1], A[2], A[3], Hb[0]]


        l_const, l_x, l_xT = sem("l_const"), sem("l_x"), sem("l_xT")
        l_stage = [sem(f"l_stage{i}") for i in range(2)]
        whi_done = sem("whi_done")
        passed = sem("passed")
        stage_used = sem("stage_used")
        small_split = sem("small_split")
        wch = sem("wch")
        w_ready = sem("w_ready")
        cst = sem("cst")
        b2_act, b2_dve = sem("b2_act"), sem("b2_dve")
        fdve, fact, fpe = sem("fdve"), sem("fact"), sem("fpe")
        tdve, tact, tpe, tpool = sem("tdve"), sem("tact"), sem("tpe"), sem("tpool")
        rdve, ract, rpe, rpool = sem("rdve"), sem("ract"), sem("rpe"), sem("rpool")
        g1_done, silu_done, hhi_done, hlo_done, g2_done, comb_done = (
            sem(n) for n in ("g1_done", "silu_done", "hhi_done", "hlo_done", "g2_done", "comb_done"))
        z_done, scat, tail_done = sem("z_done"), sem("scat"), sem("tail_done")
        cnt_chain, tab_ready = sem("cnt_chain"), sem("tab_ready")
        l_xin, xt_done, xthi_done, xtlo_done = sem("l_xin"), sem("xt_done"), sem("xthi_done"), sem("xtlo_done")
        u1_done, relu_done, uhi_done, ulo_done, u2_done, y_done, y_out = (
            sem(n) for n in ("u1_done", "relu_done", "uhi_done", "ulo_done", "u2_done", "y_done", "y_out"))
        wexp_done = sem("wexp_done")
        l_y = [sem(f"l_y{i}") for i in range(NR)]
        sum_done, stat_done, feps, frstd, normed = (
            sem(n) for n in ("sum_done", "stat_done", "feps", "frstd", "normed"))
        idx8_done, fin_out = sem("idx8_done"), [sem(f"fin_out{n}") for n in range(2)]

        def at(steps, q, name):
            if steps in (R_DVE, R_ACT, R_PE, R_POOL):
                q = q + 1
            return q * len(steps) + (steps.index(name) + 1)

        def before_chunk(eng, q, *waits, wait=None):
            for s, steps, name in waits:
                if not (isinstance(q, int) and q == 0):
                    wait(s, at(steps, q - 1, name)) if wait else eng.wait_ge(s, at(steps, q - 1, name))

        def pairs(ap):
            return ap.rearrange("p (g two) -> p g two", two=2)

        def cols(w, off, n):
            return w[:, off:off + KD * n].rearrange("p (k n) -> p k n", k=KD)

        block = ctx.enter_context(nc.Block())

        @block.sync
        def _(sp):
            for dst, src in ((masks_s[:, :], masks), (wdw_s[:, :], wdw), (rows_s[:, :], rows.partition_broadcast(P)),
                             (b1_s[:, :], moe1_b), (b1r_s[:, :], moe2_b), (b2_f, b2rows),
                             (rope_s[:, :, :, :], rope)):
                sp.dma_start(dst, src).then_inc(l_const, 16)
            for n in range(2):
                w = W1C if n == 0 else SMALL - W1C
                sp.dma_start(stage[:, n, 0:w], small[:, n * W1C:n * W1C + w]).then_inc(l_stage[n], 16)

            def load_xT(n):
                nb = n if n < NBLK else 0
                sp.dma_start(xTb[:, n % 2, :, :], xT[:, :, nb // BPB, (nb % BPB) * BLK:(nb % BPB) * BLK + BLK + 2])\
                  .then_inc(l_xT, 16)
                sp.wait_ge(l_xT, 16 * (n + 1))

            def load_x(n):
                sp.dma_start(xall[:, n * CPB:(n + 1) * CPB, :],
                             x[n * BLK:(n + 1) * BLK, :].rearrange("(c p) d -> p c d", p=P)).then_inc(l_x, 16)
                sp.wait_ge(l_x, 16 * (n + 1))

            load_xT(0)
            load_x(0)
            load_xT(1)
            for n in range(2 * E1):
                sp.wait_ge(stage_used, n + 1)
                sp.dma_start(stage[:, n % 2, :], moe1[:, n * W1C:(n + 1) * W1C]).then_inc(l_stage[n % 2], 16)
                if n < NBLK - 1:
                    load_x(n + 1)
            sp.wait_ge(cst, 4)
            for e in range(E2):
                sp.dma_start(xg[e * CAP:e * CAP + TILE, :].rearrange("(s p) d -> p s d", p=P),
                             zeros[:, :].unsqueeze(1).broadcast_to([P, TILE // P, D])).then_inc(z_done, 16)
            for n in range(2):
                sp.wait_ge(stage_used, 2 * E1 + n + 1)
                sp.dma_start(stage[:, n % 2, :], moe2[0, :, n * W1C:(n + 1) * W1C]).then_inc(l_stage[n % 2], 16)
            for n in range(2, NBLK + 1):
                sp.wait_ge(fdve, at(F_DVE, CPB * (n - 2) + CPB - 1, "x2"))
                load_xT(n)
            sp.wait_ge(tab_ready, 1)
            sp.wait_ge(z_done, 16 * E2)
            for e in range(E2):
                first = sp.value_load(tab[0:1, 2 * E2 + e:2 * E2 + e + 1], min_val=e * CAP, max_val=e * CAP + NTOK)
                sp.dma_start(xg[bass.ds(first, TILE), :].rearrange("(s p) d -> p s d", p=P),
                             zeros[:, :].unsqueeze(1).broadcast_to([P, TILE // P, D])).then_inc(tail_done, 16)
            ng = sp.value_load(tab[0:1, 3 * E2:3 * E2 + 1], min_val=LEAST, max_val=MOST)
            sp.dma_start(yg[bass.ds(ng * TILE, E2 * TILE), :].rearrange("(s p) d -> p s d", p=P),
                         zeros[:, :].unsqueeze(1).broadcast_to([P, E2 * TILE // P, D])).then_inc(tail_done, 16)
            sp.wait_ge(tail_done, 16 * (E2 + 1))
            sp.wait_ge(scat, 32 * NCH)
            with sp.Fori(0, E2) as e:
                nt = sp.value_load(tab[0:1, bass.ds(e, 1)], min_val=1, max_val=NTOK // TILE)
                tb = sp.value_load(tab[0:1, bass.ds(e + E2, 1)], min_val=0, max_val=MOST)
                for n in range(2):
                    sp.wait_ge(stage_used, 2 * E1 + 3 + n + 2 * e)
                    sp.dma_start(stage[:, n, :], moe2[bass.ds((e + 1) % E2, 1), :, n * W1C:(n + 1) * W1C]
                                 .rearrange("a p c -> p (a c)")).then_inc(l_stage[n], 16)
                with sp.Fori(0, nt) as t:
                    sp.wait_ge(xt_done, tb + t + 1)
                    sp.dma_start(xin[:, :, :], xg[bass.ds(e * CAP + t * TILE, TILE), :]
                                 .rearrange("(s p) d -> p s d", p=P)).then_inc(l_xin, 16)
            sp.wait_ge(xt_done, ng + 1)
            sp.dma_start(xin[:, :, :], xg[0:TILE, :].rearrange("(s p) d -> p s d", p=P)).then_inc(l_xin, 16)
            for i in range(NG):
                sp.wait_ge(normed, (i + 1) * NR)
                sp.dma_start(out[i * NR * P:(i + 1) * NR * P, :].rearrange("(r p) d -> p r d", p=P), fin[:, i % 2, :, :])\
                  .then_inc(fin_out[i % 2], 16)
            for n in range(2):
                sp.wait_ge(fin_out[n], 16 * (NG // 2))

        @block.tensor
        def _(pe):
            pe.sem_inc(rpe, len(R_PE))
            pe.sem_inc(xt_done, 1)
            pe.sem_inc(u2_done, 1)
            mm = nc.tensor.matmul

            def three(outp, wl, xl, first=True, last=True):
                n = len(wl[0])
                for k in range(n):
                    for i, (a, b) in enumerate(((0, 0), (0, 1), (1, 0))):
                        ins = mm(outp, wl[a][k], xl[b][k], start=first and k == 0 and i == 0,
                                 stop=last and k == n - 1 and i == 2, skip_group_check=True)
                return ins

            def ks(t, off=0, n=None):
                return [t[:, k, off:off + n] if n else t[:, k, :] for k in range(KD)]

            def front_pw(q):
                pe.wait_ge(fact, at(F_ACT, q, "yhi"))
                pe.wait_ge(fdve, at(F_DVE, q, "ylo"))
                before_chunk(pe, q, (tdve, T_DVE, "kvt"))
                for eh in range(KD):
                    ins = three(A[1][:, eh * P:(eh + 1) * P],
                                [ks(cols(small_hi, PW, D), eh * P, P), ks(cols(small_lo, PW, D), eh * P, P)],
                                [ks(y_hi), ks(y_lo)])
                ins.then_inc(fpe, 1)

            def front_qkv(q):
                pe.wait_ge(fact, at(F_ACT, q, "dhi"))
                pe.wait_ge(fdve, at(F_DVE, q, "dlo"))
                before_chunk(pe, q, (tact, T_ACT, "ahi"), (tdve, T_DVE, "alo"))
                w = [[t[:, QKV + k * 768:QKV + k * 768 + 512] for k in range(KD)] for t in (small_hi, small_lo)]
                wv = [[t[:, QKV + k * 768 + 512:QKV + (k + 1) * 768] for k in range(KD)] for t in (small_hi, small_lo)]
                three(A[1][:, :], [ks(x2_hi), ks(x2_lo)], w).then_inc(fpe, 1)
                three(A[2][:, 0:D], [ks(x2_hi), ks(x2_lo)], wv).then_inc(fpe, 1)
                three(A[2][:, D:2 * D], [ks(d_hi), ks(d_lo)],
                      [ks(cols(small_hi, WG, D)), ks(cols(small_lo, WG, D))]).then_inc(fpe, 1)
                before_chunk(pe, q, (tdve, T_DVE, "attn"))
                if not (isinstance(q, int) and q <= 8):
                    pe.wait_ge(rdve, at(R_DVE, q - 9, "cnt"))
                for k in range(KD):
                    ins = nc.tensor.transpose(A[0][:, D + k * P:D + (k + 1) * P], x2T[:, k, 1:CH + 1], ident)
                ins.then_inc(fpe, 1)

            def phit(q):
                pe.wait_ge(fdve, at(F_DVE, q, "phi"))
                before_chunk(pe, q, (tdve, T_DVE, "gmax"), (tact, T_ACT, "gexp"))
                for n in range(4):
                    ins = nc.tensor.transpose(A[3][:, n * P:(n + 1) * P], phi[:, n * P:(n + 1) * P], ident)
                ins.then_inc(tpe, 1)

            def score(q):
                pe.wait_ge(tact, at(T_ACT, q, "kT"))
                pe.wait_ge(tdve, at(T_DVE, q, "qx1"))
                pe.wait_ge(fact, at(F_ACT, q, "x2tok"))
                for half in range(KD):
                    for j in range(4):
                        ins = mm(A[j][:, half * D:(half + 1) * D], kTs[32 * j:32 * j + 32, half, :],
                                 qx[32 * j:32 * j + 32, half, :, :], start=True, stop=True, skip_group_check=True)
                ins.then_inc(tpe, 1)

            def av(q):
                pe.wait_ge(tdve, at(T_DVE, q, "mask3"))
                for half in range(KD):
                    o = half * H // 2 * HE
                    mm(A[0][:, o:o + H // 2 * HE], qTs[:, half, :], state[:, half, :],
                       start=half == 0, stop=False, skip_group_check=True)
                    for h8 in range(H // 2):
                        ins = mm(A[0][:, o + h8 * HE:o + (h8 + 1) * HE], sm[:, h8 // 2, half * 2 + h8 % 2, :],
                                 vext[:, half * H // 2 + h8, :], start=False, stop=True, skip_group_check=True)
                ins.then_inc(tpe, 1)
                for half in range(KD):
                    ins = mm(A[1][:, half * H // 2 * HE:(half + 1) * H // 2 * HE], phi[:, D + half * P:D + (half + 1) * P],
                             vext[:, half * H // 2:(half + 1) * H // 2, :], start=True, stop=True, skip_group_check=True)
                ins.then_inc(tpe, 1)

            def at_(q):
                pe.wait_ge(tdve, at(T_DVE, q, "attn"))
                for k in range(KD):
                    ins = nc.tensor.transpose(A[2][:, k * P:(k + 1) * P], attn[:, k * P:(k + 1) * P], ident)
                ins.then_inc(tpe, 1)

            def wo(q):
                pe.wait_ge(tact, at(T_ACT, q, "ahi"))
                pe.wait_ge(tdve, at(T_DVE, q, "alo"))
                three(A[3][:, 0:D], [ks(a_hi), ks(a_lo)],
                      [ks(cols(small_hi, WO, D)), ks(cols(small_lo, WO, D))]).then_inc(tpe, 1)

            def ht(q):
                pe.wait_ge(tpool, at(T_POOL, q, "hb"))
                for k in range(KD):
                    ins = nc.tensor.transpose(A[3][:, D + k * P:D + (k + 1) * P], h0[:, k * P:(k + 1) * P], ident)
                ins.then_inc(tpe, 1)

            def lg(q, b, j):
                pe.wait_ge(tact, at(T_ACT, q, "hhi"))
                pe.wait_ge(tdve, at(T_DVE, q, "hlo"))
                s = b % 2
                three(A[3][:, 0:E1], [[t[:, s, k, j * P:(j + 1) * P] for k in range(KD)] for t in (hT_hi, hT_lo)],
                      [ks(cols(small_hi, MG, E1)), ks(cols(small_lo, MG, E1))]).then_inc(tpe, 1)

            def g1(b, n, i):
                e, c, s = n // FC, n % FC, b % 2
                u = i * E1 * FC + n
                if n == 0:
                    pe.wait_ge(tact, at(T_ACT, i * CPB + CPB - 1, "hhi"))
                    pe.wait_ge(tdve, at(T_DVE, i * CPB + CPB - 1, "hlo"))
                if b == 0 and c == 0:
                    pe.wait_ge(w_ready, 2 * (e + 1))
                if not (isinstance(u, int) and u < 2):
                    pe.wait_ge(silu_done, u - 1)
                three(Hb[n % 2][:, :], [[t[:, e, k * FF + c * P:k * FF + (c + 1) * P] for k in range(KD)] for t in (w_hi, w_lo)],
                      [ks(hT_hi[:, s]), ks(hT_lo[:, s])]).then_inc(g1_done, 1)

            def g2_(n, i):
                e, c, s = n // FC, n % FC, n % 4
                u = i * E1 * FC + n
                pe.wait_ge(hhi_done, u + 1)
                pe.wait_ge(hlo_done, u + 1)
                if c == 0:
                    pe.wait_ge(b2_dve, 3)
                    if not (isinstance(u, int) and u == 0):
                        pe.wait_ge(comb_done, (i * E1 + e) * CPB)
                    for t in range(CPB):
                        mm(Yb[t // 2][:, (t % 2) * D:(t % 2 + 1) * D], ones[:, :], b2_row[:, e * D:(e + 1) * D],
                           start=t % 2 == 0, stop=False, skip_group_check=True)
                for t in range(CPB):
                    w = [t2[:, e, W1C + c * D:W1C + (c + 1) * D] for t2 in (w_hi, w_lo)]
                    ins = three(Yb[t // 2][:, (t % 2) * D:(t % 2 + 1) * D],
                                [[h_hi[:, s, t * P:(t + 1) * P]], [h_lo[:, s, t * P:(t + 1) * P]]],
                                [[w[0]], [w[1]]], first=False, last=c == FC - 1)
                ins.then_inc(g2_done, 1)

            def post_xt(p):
                pe.wait_ge(rdve, at(R_DVE, p, "x5"))
                before_chunk(pe, p, (rdve, R_DVE, "cnt"))
                for k in range(KD):
                    ins = nc.tensor.transpose(A[0][:, k * P:(k + 1) * P], px5[:, k * P:(k + 1) * P], ident)
                ins.then_inc(rpe, 1)

            def post_rl(p):
                pe.wait_ge(ract, at(R_ACT, p, "xhi"))
                pe.wait_ge(rdve, at(R_DVE, p, "xlo"))
                three(A[0][:, D:D + E2], [ks(px_hi), ks(px_lo)],
                      [ks(cols(small_hi, RT, E2)), ks(cols(small_lo, RT, E2))]).then_inc(rpe, 1)

            def post_rk(p):
                pe.wait_ge(rdve, at(R_DVE, p, "m12"))
                mm(A[0][:, 2 * D - 2 * E2:2 * D - E2], before[:, :], m12[:, :], start=True, stop=True, skip_group_check=True)
                mm(A[0][:, 2 * D - E2:2 * D], ones[:, :], m12[:, :], start=True, stop=True, skip_group_check=True)\
                    .then_inc(rpe, 1)

            def step(b, i, j, ffn=True, att=True, post=True):
                q = (i + 1) * CPB + j
                for c in range(FC):
                    if att:
                        if c == 0: phit(q)
                        if c == 1: score(q)
                        if c == 2: av(q)
                        if c == 3: at_(q); front_pw(q + 1)
                        if c == 4: wo(q)
                    if post:
                        p = (i - 1) * CPB + j
                        if c == 4: post_xt(p)
                        if c == 5: post_rl(p)
                        if c == 6: post_rk(p)
                    if att:
                        if c == 6: ht(q); front_qkv(q + 1)
                        if c == 7: lg(q, b + 1, j)
                    if ffn:
                        g1(b, j * FC + c, i)
                        n = j * FC + c - 2
                        if n >= 0:
                            g2_(n, i)
                        elif not (isinstance(i, int) and i == 0):
                            g2_(n + E1 * FC, i - 1)

            pe.wait_ge(small_split, 4)
            pe.wait_ge(cst, 7)
            pe.wait_ge(l_const, 16 * 7)
            front_pw(0)
            front_qkv(0)
            for j in range(CPB):
                step(-1, -1, j, ffn=False, post=False)
            for j in range(CPB):
                step(0, 0, j, post=False)
            with pe.Fori(0, (NBLK - 2) // 2) as i:
                for b in (1, 2):
                    for j in range(CPB):
                        step(b, 2 * i + b, j)
            pe.wait_ge(fact, at(F_ACT, NCH, "gt"))
            for j in range(CPB):
                step(NBLK - 1, NBLK - 1, j, att=False)
            for n in (2, 1):
                g2_(E1 * FC - n, NBLK - 1)
            for j in range(CPB):
                step(NBLK, NBLK, j, ffn=False, att=False)

            def transposes(g):
                pe.wait_ge(l_xin, 16 * (g + 1))
                if not (isinstance(g, int) and g == 0):
                    pe.wait_ge(xtlo_done, g)
                for s in range(2):
                    for k in range(KD):
                        ins = nc.tensor.transpose(A[0][:, k * TILE + s * P:k * TILE + (s + 1) * P],
                                                  xin[:, s, k * P:(k + 1) * P], ident)
                ins.then_inc(xt_done, 1)

            transposes(0)
            with pe.Fori(0, E2 // 2) as ep:
                for s in range(2):
                    e = 2 * ep + s
                    nt = pe.value_load(tab[0:1, bass.ds(e, 1)], min_val=1, max_val=NTOK // TILE)
                    tb = pe.value_load(tab[0:1, bass.ds(e + E2, 1)], min_val=0, max_val=MOST)
                    pe.wait_ge(w_ready, 2 * E1 + 2 + 2 * e)
                    pe.sem_inc(passed, 1)
                    with pe.Fori(0, nt) as t:
                        g = pe.snap(tb + t)
                        pe.wait_ge(xthi_done, g + 1)
                        pe.wait_ge(xtlo_done, g + 1)
                        for n in range(FC + 4):
                            if n < FC:
                                if n >= 4:
                                    pe.wait_ge(relu_done, g * FC + n - 3)
                                three(U[n % 4][:, 0:TILE],
                                      [[w[:, s, k * FF + n * P:k * FF + (n + 1) * P] for k in range(KD)] for w in (e_hi, e_lo)],
                                      [ks(xt_hi), ks(xt_lo)]).then_inc(u1_done, 1)
                            if n == 5:
                                transposes(g + 1)
                            if n >= 4:
                                c = n - 4
                                pe.wait_ge(uhi_done, g * FC + c + 1)
                                pe.wait_ge(ulo_done, g * FC + c + 2)
                                if c == 0:
                                    pe.wait_ge(y_done, g + 1)
                                    for r in range(2):
                                        mm(Yb[0][:, r * D:(r + 1) * D], ones[:, :], b2_row[:, bass.ds((e + E1) * D, D)],
                                           start=r == 0, stop=False, skip_group_check=True)
                                w = [[t2[:, s, W1C + c * D:W1C + (c + 1) * D]] for t2 in (e_hi, e_lo)]
                                for r in range(2):
                                    ins = three(Yb[0][:, r * D:(r + 1) * D],
                                                [[u_hi[:, c, r * P:(r + 1) * P]], [u_lo[:, c, r * P:(r + 1) * P]]], w,
                                                first=False, last=c == FC - 1)
                        ins.then_inc(u2_done, 1)

        @block.vector
        def _(dve):
            dve.sem_inc(rdve, len(R_DVE))
            dve.sem_inc(ulo_done, 1)
            dve.sem_inc(y_done, 1)
            V = nc.vector

            def split_lo(out_, in_, hi, scale=1.0):
                return V.scalar_tensor_tensor(out=out_, in0=in_, scalar=scale, in1=hi, op0=ALU.mult, op1=ALU.subtract)

            def front_conv(q, b, j, i):
                xt = xTb[:, b % 2]
                if j == 0:
                    dve.wait_ge(l_xT, 16 * (i + 1))
                before_chunk(dve, q, (fact, F_ACT, "dhi"), (fdve, F_DVE, "dlo"))
                for tap in range(3):
                    for k in range(KD):
                        src, w = xt[:, k, j * CH + tap:j * CH + tap + CH], wdw_s[:, k * 3 + tap:k * 3 + tap + 1]
                        if tap == 0:
                            V.tensor_scalar(yT[:, k, :], src, w, None, ALU.mult).then_inc(fdve, 1)
                        else:
                            dve.wait_ge(fdve, at(F_DVE, q, f"conv{tap - 1}{'ab'[k]}"))
                            V.scalar_tensor_tensor(out=yT[:, k, :], in0=src, scalar=w, in1=yT[:, k, :],
                                                   op0=ALU.mult, op1=ALU.add).then_inc(fdve, 1)
                dve.wait_ge(fact, at(F_ACT, q, "yhi"))
                dve.wait_ge(fdve, at(F_DVE, q, "conv2b"))
                before_chunk(dve, q, (fpe, F_PE, "gate"))
                split_lo(y_lo[:, :, :], yT[:, :, :], y_hi[:, :, :]).then_inc(fdve, 1)

            def front_x2(q, b, j):
                xt = xTb[:, b % 2]
                before_chunk(dve, q, (fpe, F_PE, "x2t"), (fact, F_ACT, "x2hi"), (fdve, F_DVE, "delta"))
                if isinstance(q, int) and q == 0:
                    V.memset(x2T[:, :, 0:1], 0.0).then_inc(fdve, 1)
                else:
                    V.tensor_scalar(x2T[:, :, 0:1], x2T[:, :, CH:CH + 1], MO["keep"][:, bass.ds(q, 1)], None,
                                    ALU.mult).then_inc(fdve, 1)
                dve.wait_ge(fpe, at(F_PE, q, "pw"))
                dve.wait_ge(fdve, at(F_DVE, q, "halo"))
                V.scalar_tensor_tensor(out=x2T[:, :, 1:CH + 1], in0=A[1][:, 0:D].rearrange("p (k n) -> p k n", k=KD),
                                       scalar=INV, in1=xt[:, :, 2 + j * CH:2 + j * CH + CH],
                                       op0=ALU.mult, op1=ALU.add).then_inc(fdve, 1)
                dve.wait_ge(fdve, at(F_DVE, q, "x2"))
                V.scalar_tensor_tensor(out=x2T[:, :, 0:1], in0=x2T[:, :, 1:2], scalar=MO["new"][:, bass.ds(q, 1)],
                                       in1=x2T[:, :, 0:1], op0=ALU.mult, op1=ALU.add).then_inc(fdve, 1)
                dve.wait_ge(fdve, at(F_DVE, q, "first"))
                V.tensor_tensor(dT[:, :, :], x2T[:, :, 1:CH + 1], x2T[:, :, 0:CH], ALU.subtract).then_inc(fdve, 1)
                dve.wait_ge(fact, at(F_ACT, q, "x2hi"))
                before_chunk(dve, q, (fpe, F_PE, "v"))
                split_lo(x2_lo[:, :, :], x2T[:, :, 1:CH + 1], x2_hi[:, :, :]).then_inc(fdve, 1)
                dve.wait_ge(fact, at(F_ACT, q, "dhi"))
                dve.wait_ge(fdve, at(F_DVE, q, "delta"))
                split_lo(d_lo[:, :, :], dT[:, :, :], d_hi[:, :, :]).then_inc(fdve, 1)

            def front_phi(q, c):
                cos = rope_s[:, bass.ds(c, 1), 0, :].broadcast_to([P, 2 * H, DH])
                sin = rope_s[:, bass.ds(c, 1), 1, :].broadcast_to([P, 2 * H, DH])
                qk = A[1][:, :].rearrange("p (h d) -> p h d", d=DH)
                dve.wait_ge(fpe, at(F_PE, q, "qk"))
                before_chunk(dve, q, (fdve, F_DVE, "phi"), (tpe, T_PE, "at"))
                V.tensor_tensor(r1[:, :].rearrange("p (h d) -> p h d", d=DH), qk, cos, ALU.mult).then_inc(fdve, 1)
                r2v = r2[:, :].rearrange("p (h d) -> p h d", d=DH)
                V.tensor_tensor(r2v[:, :, 0:DH:2], qk[:, :, 1:DH:2], sin[:, :, 0:DH:2], ALU.mult).then_inc(fdve, 1)
                V.tensor_tensor(r2v[:, :, 1:DH:2], qk[:, :, 0:DH:2], sin[:, :, 1:DH:2], ALU.mult).then_inc(fdve, 1)
                dve.wait_ge(fdve, at(F_DVE, q, "rot_sin_b"))
                V.tensor_tensor(rq[:, :], r1[:, :], r2[:, :], ALU.add).then_inc(fdve, 1)
                dve.wait_ge(fdve, at(F_DVE, q, "rot"))
                V.tensor_scalar(phm[:, :], rq[:, :], 0.0, None, ALU.min).then_inc(fdve, 1)

            def front_phi2(q):
                dve.wait_ge(fact, at(F_ACT, q, "vext"))
                before_chunk(dve, q, (fact, F_ACT, "gt"), (tdve, T_DVE, "x3"))
                V.scalar_tensor_tensor(out=gz[:, :], in0=A[2][:, D:2 * D], scalar=INV, in1=rows_s[:, 0:D],
                                       op0=ALU.mult, op1=ALU.add).then_inc(fdve, 1)
                dve.wait_ge(fact, at(F_ACT, q, "phiexp"))
                before_chunk(dve, q, (tpe, T_PE, "kv"))
                V.scalar_tensor_tensor(out=phi[:, :], in0=rq[:, :], scalar=0.0, in1=phe[:, :],
                                       op0=ALU.max, op1=ALU.add).then_inc(fdve, 1)

            def tail_qx(q):
                dve.wait_ge(tact, at(T_ACT, q, "qT"))
                before_chunk(dve, q, (tpe, T_PE, "score"))
                for par, name in enumerate(("even", "odd")):
                    V.tensor_scalar(qx[:, :, par, :], qTs, MO[name], None, ALU.mult).then_inc(tdve, 1)
                before_chunk(dve, q, (tdve, T_DVE, "kvadd"), (tpe, T_PE, "av"))
                V.tensor_scalar(state[:, :, :], state[:, :, :], MO["keep"][:, bass.ds(q, 1)], None,
                                ALU.mult).then_inc(tdve, 1)

            def tail_mask(q):
                dve.wait_ge(tpe, at(T_PE, q, "score"))
                before_chunk(dve, q, (tpe, T_PE, "av"))
                for j in range(4):
                    V.tensor_tensor(sm[:, j, :, :], A[j][:, :].rearrange("p (m n) -> p m n", m=4),
                                    causal.unsqueeze(1).broadcast_to([P, 4, CH]), ALU.mult).then_inc(tdve, 1)

            def tail_attn(q):
                o = A[0][:, 0:H * HE].rearrange("p (h e) -> p h e", e=HE)
                dve.wait_ge(tpe, at(T_PE, q, "av"))
                before_chunk(dve, q, (tdve, T_DVE, "attn"), (tpe, T_PE, "at"))
                V.tensor_scalar(den[:, :].unsqueeze(2), o[:, :, DH:HE], 1e-6, None, ALU.add).then_inc(tdve, 1)
                dve.wait_ge(tdve, at(T_DVE, q, "den"))
                V.reciprocal(rden[:, :], den[:, :]).then_inc(tdve, 1)
                dve.wait_ge(tdve, at(T_DVE, q, "rden"))
                V.tensor_tensor(attn[:, :].rearrange("p (h d) -> p h d", d=DH), o[:, :, 0:DH],
                                rden[:, :].unsqueeze(2).broadcast_to([P, H, DH]), ALU.mult).then_inc(tdve, 1)
                dve.wait_ge(tpe, at(T_PE, q, "kv"))
                V.tensor_tensor(kvt[:, :, :], A[1][:, 0:H * HE].rearrange("p (k n) -> p k n", k=KD),
                                MO["block"].unsqueeze(1).broadcast_to([P, KD, H // 2 * HE]), ALU.mult).then_inc(tdve, 1)
                dve.wait_ge(tdve, at(T_DVE, q, "kvt"))
                V.tensor_tensor(state[:, :, :], state[:, :, :], kvt[:, :, :], ALU.add).then_inc(tdve, 1)

            def tail_alo(q):
                dve.wait_ge(tact, at(T_ACT, q, "ahi"))
                before_chunk(dve, q, (tpe, T_PE, "wo"))
                split_lo(a_lo[:, :, :], A[2][:, 0:D].rearrange("p (k n) -> p k n", k=KD), a_hi[:, :, :]).then_inc(tdve, 1)

            def norm(sem_, steps, q, bn_, mv_, src, names):
                V.bn_stats(bn_[:, :], src).then_inc(sem_, 1)
                dve.wait_ge(sem_, at(steps, q, names[0]))
                dve.sem_inc(passed, 1)
                V.bn_aggr(mv_[:, :], bn_[:, :]).then_inc(sem_, 1)

            def tail_x3(q):
                dve.wait_ge(tpe, at(T_PE, q, "wo"))
                dve.wait_ge(fact, at(F_ACT, q, "gt"))
                V.scalar_tensor_tensor(out=g2[:, :], in0=gt[:, :], scalar=1.0, in1=A[3][:, 0:D],
                                       op0=ALU.add, op1=ALU.mult).then_inc(tdve, 1)
                dve.wait_ge(tdve, at(T_DVE, q, "g2"))
                dve.wait_ge(fact, at(F_ACT, q, "x2tok"))
                before_chunk(dve, q, (tpool, T_POOL, "rstd"))
                V.scalar_tensor_tensor(out=x3[:, :], in0=g2[:, :], scalar=0.5 * INV, in1=x2tok[:, :],
                                       op0=ALU.mult, op1=ALU.add).then_inc(tdve, 1)
                dve.wait_ge(tdve, at(T_DVE, q, "x3"))
                norm(tdve, T_DVE, q, bn, mv, x3[:, :], ("bn",))

            def tail_h0(q):
                dve.wait_ge(tpool, at(T_POOL, q, "rstd"))
                dve.wait_ge(tdve, at(T_DVE, q, "aggr"))
                before_chunk(dve, q, (tpe, T_PE, "ht"))
                V.tensor_scalar(h0[:, :], x3[:, :], mv[:, 0:1], rstd[:, 0:1], ALU.subtract, ALU.mult).then_inc(tdve, 1)

            def tail_hlo(q, b, j):
                dve.wait_ge(tact, at(T_ACT, q, "hhi"))
                split_lo(hT_lo[:, b % 2, :, j * CH:(j + 1) * CH], A[3][:, D:2 * D].rearrange("p (k n) -> p k n", k=KD),
                         hT_hi[:, b % 2, :, j * CH:(j + 1) * CH]).then_inc(tdve, 1)

            def tail_gmax(q):
                dve.wait_ge(tpe, at(T_PE, q, "lg"))
                before_chunk(dve, q, (tdve, T_DVE, "gw"), (tact, T_ACT, "gexp"))
                V.tensor_reduce(gm[:, :], A[3][:, 0:E1], AX.X, ALU.max).then_inc(tdve, 1)
                dve.wait_ge(tdve, at(T_DVE, q, "gmax"))
                V.tensor_scalar(gn[:, :], gm[:, :], -INV, None, ALU.mult).then_inc(tdve, 1)

            def tail_gate(q, b, j):
                dve.wait_ge(tact, at(T_ACT, q, "gexp"))
                V.reciprocal(gr[:, :], gs[:, :]).then_inc(tdve, 1)
                dve.wait_ge(tdve, at(T_DVE, q, "rsum"))
                V.tensor_scalar(gw[:, b % 2, j, :], ge[:, :], gr[:, 0:1], INV, ALU.mult, ALU.mult).then_inc(tdve, 1)

            def split_half_lo(n):
                dve.wait_ge(whi_done, n + 1)
                split_lo(w_lo[:, n // 2, (n % 2) * W1C:(n % 2 + 1) * W1C], stage[:, n % 2, :],
                         w_hi[:, n // 2, (n % 2) * W1C:(n % 2 + 1) * W1C], SCALE).then_inc(w_ready, 1)

            def hlo(n, i):
                u = i * E1 * FC + n
                dve.wait_ge(hhi_done, u + 1)
                if not (isinstance(u, int) and u < 4):
                    dve.wait_ge(g2_done, u - 3)
                V.tensor_tensor(h_lo[:, n % 4, :], s32[:, n % 2, :], h_hi[:, n % 4, :], ALU.subtract).then_inc(hlo_done, 1)

            def comb(e, b, i):
                dve.wait_ge(g2_done, (i * E1 + e + 1) * FC)
                for t in range(CPB):
                    if e == 0:
                        dve.wait_ge(tpool, at(T_POOL, i * CPB + t, "xres"))
                        dve.wait_ge(tdve, at(T_DVE, i * CPB + t, "gw"))
                    else:
                        dve.wait_ge(comb_done, (i * E1 + e - 1) * CPB + t + 1)
                    a = acc[:, b % 2, t, :]
                    V.scalar_tensor_tensor(out=a, in0=Yb[t // 2][:, (t % 2) * D:(t % 2 + 1) * D],
                                           scalar=gw[:, b % 2, t, e:e + 1], in1=a,
                                           op0=ALU.mult, op1=ALU.add).then_inc(comb_done, 1)

            def post_norm(p, b, j, i):
                dve.wait_ge(comb_done, (i * E1 + E1 - 1) * CPB + j + 1)
                before_chunk(dve, p, (rdve, R_DVE, "x5"), (rpool, R_POOL, "veps"))
                norm(rdve, R_DVE, p, pbn, pmv, acc[:, b % 2, j, :], ("bn",))

            def post_x5(p, b, j):
                dve.wait_ge(rpool, at(R_POOL, p, "rstd"))
                dve.wait_ge(rdve, at(R_DVE, p, "aggr"))
                before_chunk(dve, p, (rpe, R_PE, "xt"), (rpool, R_POOL, "sent"))
                V.tensor_scalar(px5[:, :], acc[:, b % 2, j, :],
                                pmv[:, 0:1], prstd[:, 0:1], ALU.subtract, ALU.mult).then_inc(rdve, 1)

            def post_xlo(p):
                dve.wait_ge(ract, at(R_ACT, p, "xhi"))
                before_chunk(dve, p, (rpe, R_PE, "rl"))
                split_lo(px_lo[:, :, :], A[0][:, 0:D].rearrange("p (k n) -> p k n", k=KD), px_hi[:, :, :]).then_inc(rdve, 1)

            def post_route(p):
                dve.wait_ge(rpe, at(R_PE, p, "rl"))
                before_chunk(dve, p, (rdve, R_DVE, "pos"))
                V.scalar_tensor_tensor(out=plg[:, :], in0=A[0][:, D:D + E2], scalar=INV, in1=rows_s[:, 3 * D:3 * D + E2],
                                       op0=ALU.mult, op1=ALU.add).then_inc(rdve, 1)
                dve.wait_ge(rdve, at(R_DVE, p, "lg"))
                dve.sem_inc(passed, 1)
                V.max(top8[:, :], plg[:, :]).then_inc(rdve, 1)
                dve.wait_ge(rdve, at(R_DVE, p, "top"))
                dve.sem_inc(passed, 1)
                V.tensor_tensor(dlt[:, bass.ds(p, 1)], top8[:, 1:2], top8[:, 0:1], ALU.subtract).then_inc(rdve, 1)
                V.max_index(topi[:, :], top8[:, :], plg[:, :]).then_inc(rdve, 1)
                dve.wait_ge(rdve, at(R_DVE, p, "topi"))
                V.tensor_scalar(m1[:, :], MO["iota8"], topi[:, 0:1], None, ALU.is_equal).then_inc(rdve, 1)
                V.tensor_scalar(m2[:, :], MO["iota8"], topi[:, 1:2], None, ALU.is_equal).then_inc(rdve, 1)
                dve.wait_ge(rdve, at(R_DVE, p, "m2"))
                before_chunk(dve, p, (rpe, R_PE, "rk"))
                V.tensor_tensor(m12[:, :], m1[:, :], m2[:, :], ALU.add).then_inc(rdve, 1)

            def post_rank(p):
                dve.wait_ge(rpe, at(R_PE, p, "rk"))
                before_chunk(dve, p, (rdve, R_DVE, "cnt"))
                V.tensor_tensor(rank[:, :], A[0][:, 2 * D - 2 * E2:2 * D - E2], count[:, :], ALU.add).then_inc(rdve, 1)
                dve.wait_ge(rdve, at(R_DVE, p, "rank"))
                for n, m in enumerate((m1, m2)):
                    V.tensor_tensor_reduce(junk[:, n, :], m[:, :], rank[:, :], 1.0, 0.0, ALU.mult, ALU.add,
                                           posf[:, n:n + 1]).then_inc(rdve, 1)
                V.tensor_tensor(count[:, :], count[:, :], A[0][:, 2 * D - E2:2 * D], ALU.add).then_inc(rdve, 1)
                dve.wait_ge(rdve, at(R_DVE, p, "p2"))
                V.tensor_copy(idx[:, :], posf[:, :]).then_inc(rdve, 1)
                V.tensor_copy(pos[:, bass.ds(p, 1), :].rearrange("p a d -> p (a d)"), posf[:, :]).then_inc(rdve, 1)

            def step(b, i, j, ffn=True, att=True, post=True, w_split=False):
                q = (i + 1) * CPB + j
                nb, nj = b + 1 + (j == CPB - 1), (j + 1) % CPB
                p = (i - 1) * CPB + j
                for c in range(FC):
                    if ffn and c == 2:
                        if j > 0:
                            comb(j - 1, b, i)
                        elif not (isinstance(i, int) and i == 0):
                            comb(E1 - 1, b - 1, i - 1)
                    if att:
                        if c == 0: tail_qx(q); front_conv(q + 1, nb, nj, i + 1 + (j == CPB - 1))
                        if c == 1: tail_mask(q)
                        if c == 2: tail_attn(q)
                        if c == 3: tail_alo(q); front_x2(q + 1, nb, nj)
                        if c == 4: tail_x3(q)
                        if c == 5: tail_h0(q)
                    if post:
                        if c == 2: post_norm(p, b - 1, j, i - 1)
                        if c == 3: post_x5(p, b - 1, j)
                        if c == 4: post_xlo(p)
                        if c == 5: post_route(p)
                        if c == 6: post_rank(p)
                    if att:
                        if c == 6: tail_hlo(q, b + 1, j); front_phi(q + 1, row_chunk(q + 1))
                        if c == 7: tail_gmax(q); front_phi2(q + 1); tail_gate(q, b + 1, j)
                    if w_split:
                        if c == 1: split_half_lo(2 * j)
                        if c == 4: split_half_lo(2 * j + 1)
                    if ffn:
                        hlo(j * FC + c, i)

            def row_chunk(q):
                return q % (T // CH)

            V.memset(ones[:, :], 1.0).then_inc(cst, 1)
            V.memset(mhalf[:, :], -0.5).then_inc(cst, 1)
            V.memset(state[:, :, :], 0.0).then_inc(cst, 1)
            V.memset(zeros[:, :], 0.0).then_inc(cst, 1)
            V.memset(b2_row[:, :], 0.0).then_inc(cst, 1)
            dve.wait_ge(l_const, 16 * 7)
            V.tensor_tensor(before[:, :], causal, ident, ALU.subtract).then_inc(cst, 1)
            V.tensor_copy(count[:, :], MO["base"]).then_inc(cst, 1)
            dve.wait_ge(cst, 7)
            for n in range(2):
                w = W1C if n == 0 else SMALL - W1C
                dve.wait_ge(small_split, n * 2 + 1)
                split_lo(small_lo[:, n * W1C:n * W1C + w], stage[:, n, 0:w], small_hi[:, n * W1C:n * W1C + w], SCALE)\
                    .then_inc(small_split, 1)
            nb = (E1 + E2) * D
            dve.wait_ge(b2_act, 1)
            split_lo(b2_l, b2_f[:, 0:nb], b2_h, SCALE).then_inc(b2_dve, 1)
            dve.wait_ge(b2_dve, 1)
            V.tensor_scalar(b2_h, b2_h, b2_f[:, nb:nb + 1], None, ALU.mult).then_inc(b2_dve, 1)
            dve.wait_ge(b2_dve, 2)
            V.scalar_tensor_tensor(out=b2_row[0:2, :], in0=b2_l, scalar=b2_f[:, nb + 1:nb + 2], in1=b2_h,
                                   op0=ALU.mult, op1=ALU.add).then_inc(b2_dve, 1)

            front_conv(0, 0, 0, 0)
            front_x2(0, 0, 0)
            front_phi(0, 0)
            front_phi2(0)
            for j in range(CPB):
                step(-1, -1, j, ffn=False, post=False, w_split=True)
            for j in range(CPB):
                step(0, 0, j, post=False)
            dve.wait_ge(z_done, 16 * E2)
            with dve.Fori(0, (NBLK - 2) // 2) as i:
                for b in (1, 2):
                    for j in range(CPB):
                        step(b, 2 * i + b, j)
            for j in range(CPB):
                step(NBLK - 1, NBLK - 1, j, att=False)
            comb(E1 - 1, NBLK - 1, NBLK - 1)
            for j in range(CPB):
                step(NBLK, NBLK, j, ffn=False, att=False)

            chain = [0]

            def link(ins):
                chain[0] += 1
                ins.then_inc(cnt_chain, 1)
                dve.wait_ge(cnt_chain, chain[0])

            dve.wait_ge(rdve, at(R_DVE, NCH - 1, "pos"))
            link(V.tensor_tensor(cf[:, :], count[:, :], MO["base"], ALU.subtract))
            link(V.tensor_scalar(cf[:, :], cf[:, :], float(TILE - 1), None, ALU.add))
            link(V.tensor_copy(ci[:, :], cf[:, :]))
            link(V.tensor_scalar(ct[:, :], ci[:, :], TILE.bit_length() - 1, None, ALU.arith_shift_right))
            link(V.tensor_copy(ctf[:, :], ct[:, :]))
            link(V.tensor_scalar(tabf[:, 0:E2], ctf[:, :], 1.0, None, ALU.max))
            link(V.memset(cf[:, :], 0.0))
            link(V.tensor_tensor_scan(cum[:, :], tabf[:, 0:E2], cf[:, :], 0.0, ALU.add, ALU.add))
            link(V.tensor_tensor(tabf[:, E2:2 * E2], cum[:, :], tabf[:, 0:E2], ALU.subtract))
            link(V.tensor_copy(tabf[:, 2 * E2:3 * E2], count[:, :]))
            link(V.tensor_copy(tabf[:, 3 * E2:3 * E2 + 1], cum[:, E2 - 1:E2]))
            link(V.tensor_scalar(shift[:, :], tabf[:, E2:2 * E2], float(TILE), None, ALU.mult))
            link(V.tensor_tensor(shift[:, :], shift[:, :], MO["base"], ALU.subtract))
            link(V.memset(move[:, :, :], 0.0))
            for e in range(1, E2):
                link(V.tensor_tensor(cf[:, 0:1], shift[:, e:e + 1], shift[:, e - 1:e], ALU.subtract))
                link(V.tensor_scalar(moved[:, :, :], pos[:, :, :], float(e * CAP), cf[:, 0:1], ALU.is_ge, ALU.mult))
                link(V.tensor_tensor(move[:, :, :], move[:, :, :], moved[:, :, :], ALU.add))
            link(V.tensor_tensor(posy[:, :, :], pos[:, :, :], move[:, :, :], ALU.add))
            dve.wait_ge(rpool, at(R_POOL, NCH - 1, "sent"))
            link(V.memset(zeros[:, :], 0.0))
            V.tensor_copy(tab[:, :], tabf[:, :]).then_inc(tab_ready, 1)

            def tile_lo(g):
                dve.wait_ge(xthi_done, g + 1)
                split_lo(xt_lo[:, :, :], A[0][:, :].rearrange("p (k n) -> p k n", k=KD), xt_hi[:, :, :])\
                    .then_inc(xtlo_done, 1)

            dve.wait_ge(tab_ready, 1)
            tile_lo(0)
            with dve.Fori(0, E2) as e:
                nt = dve.value_load(tab[0:1, bass.ds(e, 1)], min_val=1, max_val=NTOK // TILE)
                tb = dve.value_load(tab[0:1, bass.ds(e + E2, 1)], min_val=0, max_val=MOST)
                with dve.Fori(0, nt) as t:
                    g = dve.snap(tb + t)
                    for c in range(FC):
                        dve.wait_ge(uhi_done, g * FC + c + 1)
                        V.tensor_tensor(u_lo[:, c, :], u32t[:, c % 4, :], u_hi[:, c, :], ALU.subtract).then_inc(ulo_done, 1)
                    tile_lo(g + 1)
                    dve.wait_ge(u2_done, g + 2)
                    dve.wait_ge(y_out, 16 * (g + 1))
                    V.tensor_scalar(ysb[:, :, :], Yb[0][:, :].rearrange("p (s d) -> p s d", s=2), INV, None, ALU.mult)\
                        .then_inc(y_done, 1)

            dve.wait_ge(wexp_done, 1)
            link(V.tensor_scalar(wone[:, :], wexp[:, :], 1.0, None, ALU.add))
            link(V.reciprocal(wt[:, 0, :], wone[:, :]))
            link(V.tensor_tensor(wt[:, 1, :], wt[:, 0, :], wexp[:, :], ALU.mult))

            def sums(i):
                for r in range(NR):
                    n = i * NR + r
                    xr = xall[:, bass.ds(n, 1), :].rearrange("p a d -> p (a d)")
                    dve.wait_ge(l_y[r], 32 * (i + 1))
                    for a in range(2):
                        V.scalar_tensor_tensor(out=xr, in0=rows8[:, r, a, :], scalar=wt[:, a, bass.ds(n, 1)], in1=xr,
                                               op0=ALU.mult, op1=ALU.add).then_inc(sum_done, 1)
                        dve.wait_ge(sum_done, 2 * n + a + 1)
                    V.bn_stats(fbn[:, r, :], xr).then_inc(stat_done, 1)
                for r in range(NR):
                    dve.wait_ge(stat_done, i * 2 * NR + r + 1)
                    V.bn_aggr(fmv[:, r, :], fbn[:, r, :]).then_inc(stat_done, 1)

            def norms(i, g):
                for r in range(NR):
                    n = i * NR + r
                    V.tensor_scalar(fin[:, g, r, :], xall[:, bass.ds(n, 1), :].rearrange("p a d -> p (a d)"),
                                    fmv[:, r, 0:1], frs[:, r:r + 1], ALU.subtract, ALU.mult).then_inc(normed, 1)

            for i in range(NG):
                sums(i)
                dve.wait_ge(frstd, i + 1)
                if i >= 2:
                    dve.wait_ge(fin_out[i % 2], 16 * (i // 2))
                norms(i, i % 2)

        @block.scalar
        def _(act):
            act.sem_inc(ract, len(R_ACT))
            act.sem_inc(y_out, 16)
            S = nc.scalar

            def copy(out_, in_, scale=1.0):
                return S.activation(out_, in_, ACT.Copy, scale=scale)

            def front_yhi(q):
                act.wait_ge(fdve, at(F_DVE, q, "conv2b"))
                before_chunk(act, q, (fpe, F_PE, "gate"), (fdve, F_DVE, "dlo"))
                copy(y_hi[:, :, :], yT[:, :, :]).then_inc(fact, 1)

            def front_x2(q):
                act.wait_ge(fdve, at(F_DVE, q, "x2"))
                before_chunk(act, q, (fpe, F_PE, "gate"))
                copy(x2_hi[:, :, :], x2T[:, :, 1:CH + 1]).then_inc(fact, 1)
                act.wait_ge(fdve, at(F_DVE, q, "delta"))
                copy(d_hi[:, :, :], dT[:, :, :]).then_inc(fact, 1)

            def front_evac(q):
                act.wait_ge(fpe, at(F_PE, q, "x2t"))
                before_chunk(act, q, (tpe, T_PE, "kv"), (tdve, T_DVE, "x3"))
                copy(vext[:, :, 0:DH], A[2][:, 0:D].rearrange("p (h d) -> p h d", d=DH), INV).then_inc(fact, 1)
                copy(x2tok[:, :], A[0][:, D:2 * D]).then_inc(fact, 1)

            def front_exp(q):
                act.wait_ge(fdve, at(F_DVE, q, "phimin"))
                before_chunk(act, q, (fdve, F_DVE, "phi"))
                S.activation(phe[:, :], phm[:, :], ACT.Exp).then_inc(fact, 1)

            def front_gt(q):
                act.wait_ge(fdve, at(F_DVE, q, "gz"))
                before_chunk(act, q, (tdve, T_DVE, "g2"))
                S.activation(gt[:, :], gz[:, :], ACT.Tanh, scale=0.5).then_inc(fact, 1)

            def tail_T(q):
                act.wait_ge(tpe, at(T_PE, q, "phit"))
                before_chunk(act, q, (tpe, T_PE, "av"))
                copy(qTs[:, :, :], A[3][:, 0:D].rearrange("p (k n) -> p k n", k=KD)).then_inc(tact, 1)
                copy(kTs[:, :, :], A[3][:, D:2 * D].rearrange("p (k n) -> p k n", k=KD)).then_inc(tact, 1)

            def tail_ahi(q):
                act.wait_ge(tpe, at(T_PE, q, "at"))
                before_chunk(act, q, (tpe, T_PE, "wo"), (tdve, T_DVE, "alo"))
                copy(a_hi[:, :, :], A[2][:, 0:D].rearrange("p (k n) -> p k n", k=KD)).then_inc(tact, 1)

            def tail_hhi(q, b, j):
                act.wait_ge(tpe, at(T_PE, q, "ht"))
                copy(hT_hi[:, b % 2, :, j * CH:(j + 1) * CH],
                     A[3][:, D:2 * D].rearrange("p (k n) -> p k n", k=KD)).then_inc(tact, 1)

            def tail_gexp(q):
                act.wait_ge(tdve, at(T_DVE, q, "ngmax"))
                act.wait_ge(tpe, at(T_PE, q, "lg"))
                S.activation(ge[:, :], A[3][:, 0:E1], ACT.Exp, bias=gn[:, 0:1], scale=INV, accum_out=gs[:, 0:1])\
                    .then_inc(tact, 1)

            def silu(n, i):
                e, c = n // FC, n % FC
                u = i * E1 * FC + n
                act.wait_ge(g1_done, u + 1)
                if not (isinstance(u, int) and u < 2):
                    act.wait_ge(hlo_done, u - 1)
                S.activation(s32[:, n % 2, :], Hb[n % 2][:, :], ACT.Silu, bias=b1_s[:, e * FC + c:e * FC + c + 1],
                             scale=INV).then_inc(silu_done, 1)
                act.wait_ge(silu_done, u + 1)
                if not (isinstance(u, int) and u < 4):
                    act.wait_ge(g2_done, u - 3)
                copy(h_hi[:, n % 4, :], s32[:, n % 2, :]).then_inc(hhi_done, 1)

            def post_xhi(p):
                act.wait_ge(rpe, at(R_PE, p, "xt"))
                before_chunk(act, p, (rpe, R_PE, "rl"))
                copy(px_hi[:, :, :], A[0][:, 0:D].rearrange("p (k n) -> p k n", k=KD)).then_inc(ract, 1)

            def step(b, i, j, ffn=True, att=True, post=True, w_split=False):
                q = (i + 1) * CPB + j
                for c in range(FC):
                    if att:
                        if c == 0: tail_T(q)
                        if c == 3: tail_ahi(q); front_x2(q + 1)
                        if c == 6: tail_hhi(q, b + 1, j); front_evac(q + 1)
                        if c == 7: front_exp(q + 1); tail_gexp(q); front_gt(q + 1)
                    if post and c == 4:
                        post_xhi((i - 1) * CPB + j)
                    if ffn:
                        silu(j * FC + c, i)
                    if att and c == 0: front_yhi(q + 1)
                    if w_split:
                        if c == 1: split_half_hi(2 * j)
                        if c == 4: split_half_hi(2 * j + 1)

            def split_half_hi(n):
                act.wait_ge(l_stage[n % 2], 16 * (n // 2 + 2))
                if n == 4:
                    act.wait_ge(b2_dve, 3)
                copy(w_hi[:, n // 2, (n % 2) * W1C:(n % 2 + 1) * W1C], stage[:, n % 2, :], SCALE).then_inc(whi_done, 1)

            for n in range(2):
                w = W1C if n == 0 else SMALL - W1C
                act.wait_ge(l_stage[n], 16)
                if n:
                    act.wait_ge(small_split, 2)
                copy(small_hi[:, n * W1C:n * W1C + w], stage[:, n, 0:w], SCALE).then_inc(small_split, 1)
            act.wait_ge(l_const, 16 * 7)
            copy(b2_h, b2_f[:, 0:(E1 + E2) * D], SCALE).then_inc(b2_act, 1)
            front_yhi(0)
            front_x2(0)
            act.wait_ge(cst, 1)
            copy(vext[:, :, DH:HE], ones[:, 0:H].unsqueeze(2)).then_inc(b2_act, 1)
            front_evac(0)
            front_exp(0)
            front_gt(0)
            for j in range(CPB):
                step(-1, -1, j, ffn=False, post=False, w_split=True)
            for j in range(CPB):
                step(0, 0, j, post=False)
            with act.Fori(0, (NBLK - 2) // 2) as i:
                for b in (1, 2):
                    for j in range(CPB):
                        step(b, 2 * i + b, j)
            for j in range(CPB):
                step(NBLK - 1, NBLK - 1, j, att=False)
            for j in range(CPB):
                step(NBLK, NBLK, j, ffn=False, att=False)

            act.wait_ge(rdve, at(R_DVE, NCH - 1, "dlt"))
            S.activation(wexp[:, :], dlt[:, :], ACT.Exp).then_inc(wexp_done, 1)

            def tile_hi(g):
                act.wait_ge(xt_done, g + 2)
                if not (isinstance(g, int) and g == 0):
                    act.wait_ge(u1_done, g * FC)
                copy(xt_hi[:, :, :], A[0][:, :].rearrange("p (k n) -> p k n", k=KD)).then_inc(xthi_done, 1)

            act.wait_ge(tab_ready, 1)
            tile_hi(0)
            with act.Fori(0, E2) as e:
                nt = act.value_load(tab[0:1, bass.ds(e, 1)], min_val=1, max_val=NTOK // TILE)
                tb = act.value_load(tab[0:1, bass.ds(e + E2, 1)], min_val=0, max_val=MOST)
                with act.Fori(0, nt) as t:
                    g = act.snap(tb + t)
                    for c in range(FC):
                        act.wait_ge(u1_done, g * FC + c + 1)
                        if c >= 4:
                            act.wait_ge(ulo_done, g * FC + c - 2)
                        else:
                            act.wait_ge(ulo_done, g * FC + 1)
                        S.activation(u32t[:, c % 4, :], U[c % 4][:, 0:TILE], ACT.Relu,
                                     bias=b1r_s[:, bass.ds(e * FC + c, 1)], scale=INV).then_inc(relu_done, 1)
                        act.wait_ge(relu_done, g * FC + c + 1)
                        if c == 0:
                            act.wait_ge(u2_done, g + 1)
                        copy(u_hi[:, c, :], u32t[:, c % 4, :]).then_inc(uhi_done, 1)
                    tile_hi(g + 1)
                    act.wait_ge(y_done, g + 2)
                    act.dma_start(yg[bass.ds(g.with_bounds(min_val=0, max_val=MOST - 1) * TILE, TILE), :].rearrange("(s p) d -> p s d", p=P),
                                  ysb[:, :, :]).then_inc(y_out, 16)

        @block.gpsimd
        def _(pool):
            pool.sem_inc(rpool, len(R_POOL))

            G = nc.gpsimd

            def wait(s, value):
                pool.wait_ge(s, value)
                pool.sem_inc(passed, 1)


            def split(src, hi, lo, waits):
                k = 3 * (waits - 2 * E1)
                G.tensor_scalar(src, src, SCALE, 1.0, ALU.mult, ALU.mult).then_inc(wch, 1)
                wait(wch, k + 1)
                G.tensor_copy(hi, src).then_inc(wch, 1)
                wait(wch, k + 2)
                G.tensor_tensor(lo, src, hi, ALU.subtract).then_inc(wch, 1)
                wait(wch, k + 3)
                pool.sem_inc(stage_used, 1)
                pool.sem_inc(w_ready, 1)

            def tail(q, b, j):
                wait(tdve, at(T_DVE, q, "x3"))
                if not (isinstance(q, int) and q < 2 * CPB):
                    wait(rdve, at(R_DVE, q - 2 * CPB, "x5"))
                G.tensor_tensor(acc[:, b % 2, j, :], xall[:, bass.ds(q, 1), :].rearrange("p a d -> p (a d)"), x3[:, :],
                                ALU.add).then_inc(tpool, 1)
                wait(tdve, at(T_DVE, q, "aggr"))
                before_chunk(pool, q, (tdve, T_DVE, "h0"), wait=wait)
                G.tensor_scalar(rstd[:, :], mv[:, 1:2], EPS, 1.0, ALU.add, ALU.mult).then_inc(tpool, 1)
                wait(tpool, at(T_POOL, q, "veps"))
                G.tensor_tensor(rstd[:, :], rstd[:, :], mhalf[:, :], ALU.pow).then_inc(tpool, 1)
                wait(tdve, at(T_DVE, q, "h0"))
                G.tensor_tensor(h0[:, :], h0[:, :], rows_s[:, D:2 * D], ALU.mult).then_inc(tpool, 1)
                wait(tpool, at(T_POOL, q, "hg"))
                G.tensor_tensor(h0[:, :], h0[:, :], rows_s[:, 2 * D:3 * D], ALU.add).then_inc(tpool, 1)

            def post_rstd(p):
                wait(rdve, at(R_DVE, p, "aggr"))
                before_chunk(pool, p, (rdve, R_DVE, "x5"), wait=wait)
                G.tensor_scalar(prstd[:, :], pmv[:, 1:2], EPS, 1.0, ALU.add, ALU.mult).then_inc(rpool, 1)
                wait(rpool, at(R_POOL, p, "veps"))
                G.tensor_tensor(prstd[:, :], prstd[:, :], mhalf[:, :], ALU.pow).then_inc(rpool, 1)

            def post_keep(p):
                wait(rdve, at(R_DVE, p, "x5"))
                G.tensor_copy(xall[:, bass.ds(p, 1), :].rearrange("p a d -> p (a d)"), px5[:, :]).then_inc(rpool, 1)

            def post_scatter(p):
                wait(rdve, at(R_DVE, p, "idx"))
                for n in range(2):
                    G.indirect_dma_start(xg[:, :], bass.IndirectOffsetOnAxis(idx[:, n:n + 1], 0), px5[:, :], None)\
                        .then_inc(scat, 16)
                wait(scat, 32 * (p + 1))
                pool.sem_inc(rpool, 1)

            def step(b, i, j, ffn=True, att=True, post=True):
                if post:
                    post_rstd((i - 1) * CPB + j)
                    post_keep((i - 1) * CPB + j)
                if att:
                    if j == 0:
                        wait(l_x, 16 * (i + 2))
                    tail((i + 1) * CPB + j, b + 1, j)
                if post:
                    post_scatter((i - 1) * CPB + j)

            def split_half(n):
                wait(l_stage[n % 2], 16 * (n // 2 + 2))
                hi, lo = (w[:, 0, (n % 2) * W1C:(n % 2 + 1) * W1C] for w in (e_hi, e_lo))
                split(stage[:, n % 2, :], hi, lo, n)

            for n in range(2):
                wait(small_split, 2 * (n + 1))
                pool.sem_inc(stage_used, 1)
            wait(cst, 2)
            for j in range(CPB):
                step(-1, -1, j, ffn=False, post=False)
                for n in range(2):
                    wait(w_ready, 2 * j + n + 1)
                    pool.sem_inc(stage_used, 1)
            for j in range(CPB):
                step(0, 0, j, post=False)
            wait(z_done, 16 * E2)
            with pool.Fori(0, (NBLK - 2) // 2) as i:
                for b in (1, 2):
                    for j in range(CPB):
                        step(b, 2 * i + b, j)
            for j in range(CPB):
                step(NBLK - 1, NBLK - 1, j, att=False)
                if j >= 2:
                    wait(g2_done, ((NBLK - 1) * E1 + 1) * FC)
                    split_half(2 * E1 + j - 2)
            for j in range(CPB):
                step(NBLK, NBLK, j, ffn=False, att=False)

            wait(tab_ready, 1)
            with pool.Fori(0, E2 // 2) as ep:
                for s in range(2):
                    e = 2 * ep + s
                    tb = pool.value_load(tab[0:1, bass.ds(e + E2, 1)], min_val=0, max_val=MOST)
                    wait(u2_done, tb + 1)
                    if s == 0:
                        wait(g2_done, NBLK * E1 * FC)
                    for n in range(2):
                        wait(l_stage[n], 16 * (E1 + 3 + e))
                        split(stage[:, n, :], *(w[:, 1 - s, n * W1C:(n + 1) * W1C] for w in (e_hi, e_lo)),
                              2 * E1 + 2 + 2 * e + n)

            ng = pool.value_load(tab[0:1, 3 * E2:3 * E2 + 1], min_val=1, max_val=MOST)
            wait(y_out, 16 * (ng + 1))
            G.memset(mhalf8, -0.5).then_inc(feps, 1)
            for i in range(NG):
                if i:
                    for r in range(NR):
                        wait(l_y[r], 32 * i)
                G.tensor_copy(idx8[:, :, :], posy[:, i * NR:(i + 1) * NR, :]).then_inc(idx8_done, 1)
                wait(idx8_done, i + 1)
                for r in range(NR):
                    if i:
                        wait(sum_done, 2 * ((i - 1) * NR + r + 1))
                    for n in range(2):
                        G.indirect_dma_start(rows8[:, r, n, :], None, yg[0:MOST * TILE, :],
                                             bass.IndirectOffsetOnAxis(idx8[:, r, n:n + 1], 0)).then_inc(l_y[r], 16)
                wait(stat_done, 2 * NR * (i + 1))
                G.tensor_scalar(fve[:, :], fmv[:, :, 1], EPS, 1.0, ALU.add, ALU.mult).then_inc(feps, 1)
                wait(feps, i + 2)
                G.tensor_tensor(frs[:, :], fve[:, :], mhalf8[:, :], ALU.pow).then_inc(frstd, 1)


def _layout(a):
    f = {k: np.ascontiguousarray(np.asarray(v)) for k, v in a.items()}
    part = lambda m: m.reshape(KD, P, -1).transpose(1, 0, 2).reshape(P, -1)
    at, ff = "L0_attn_", "L0_ffn_"
    x = f[at + "x"]
    xpad = np.concatenate([np.zeros((B, 2, D), x.dtype), x], axis=1)
    xT = np.ascontiguousarray(xpad.transpose(2, 0, 1).reshape(KD, P, B, T + 2).transpose(1, 0, 2, 3))
    small = np.concatenate([part(f[at + n].T) for n in ("w_pw", "w_qkv", "w_o", "w_gate", "w_moe_gate")]
                           + [part(f[ff + "W_router"])], axis=1)
    wdw = f[at + "w_dw"].reshape(KD, P, 3).transpose(1, 0, 2).reshape(P, -1)
    rows = np.concatenate([f[at + "b_gate"], f[at + "ln_g"], f[at + "ln_b"], f[ff + "b_router"]])
    moe1 = np.concatenate([np.concatenate([part(f[at + "w1"][e].T),
                                           f[at + "w2"][e].T.reshape(FC, P, D).transpose(1, 0, 2).reshape(P, -1)], axis=1)
                           for e in range(E1)], axis=1)
    moe1_b = f[at + "b1"].reshape(E1 * FC, P).T
    moe2 = np.stack([np.concatenate([part(f[ff + "W1"][e]),
                                     f[ff + "W2"][e].reshape(FC, P, D).transpose(1, 0, 2).reshape(P, -1)], axis=1)
                     for e in range(E2)])
    moe2_b = f[ff + "b1"].reshape(E2 * FC, P).T
    b2 = np.concatenate([f[at + "b2"].reshape(-1), f[ff + "b2"].reshape(-1)])
    b2rows = np.concatenate([np.stack([b2, b2]), np.eye(2, dtype=np.float32)], axis=1)
    inv_freq = (1.0 / np.float32(10000.0) ** (np.arange(0, DH, 2, dtype=np.float32) / np.float32(DH))).astype(np.float32)
    theta = np.arange(T, dtype=np.float32)[:, None] * inv_freq[None, :]
    cos, sin = np.cos(theta), np.sin(theta)
    rope = np.stack([np.repeat(cos, 2, axis=1), np.stack([-sin, sin], axis=-1).reshape(T, DH)], axis=1) * INV
    rope = rope.astype(np.float32).reshape(T // P, P, 2, DH).transpose(1, 0, 2, 3)
    p = np.arange(P)
    chunks = np.arange(NCH + 1)
    keep = (chunks % (T // CH) != 0).astype(np.float32)
    masks = np.concatenate([
        np.eye(P), p[:, None] <= p[None, :], (p[:, None] // DH) == (np.arange(H // 2 * HE)[None, :] // HE),
        (p[:, None] // DH) % 2 == 0, (p[:, None] // DH) % 2 == 1,
        np.tile(keep, (P, 1)), np.tile(1 - keep, (P, 1)), np.tile(np.arange(E2), (P, 1)),
        np.tile(np.arange(E2) * CAP, (P, 1))], axis=1).astype(np.float32)
    arrays = dict(x=x.reshape(NTOK, D), xT=xT, small=small, wdw=wdw, rows=rows, moe1=moe1, moe1_b=moe1_b, moe2=moe2,
                  moe2_b=moe2_b, b2rows=b2rows, rope=rope, masks=masks)
    return {k: np.ascontiguousarray(v) for k, v in arrays.items()}


def kernel(**inputs):
    import concourse.bacc as bacc
    from concourse.bass_utils import run_bass_kernel_spmd

    nc = bacc.Bacc("TRN2", target_bir_lowering=False, num_devices=1)
    arrays = _layout(inputs)
    args = {k: nc.dram_tensor("in_" + k, a.shape, mybir.dt.from_np(a.dtype), kind="ExternalInput").ap()
            for k, a in arrays.items()}
    out = nc.dram_tensor("out_0", (NTOK, D), F32, kind="ExternalOutput").ap()
    build(nc, out=out, **args)
    r = run_bass_kernel_spmd(nc, [{"in_" + k: a for k, a in arrays.items()}], core_ids=[0])
    return r.results[0]["out_0"].reshape(B, T, D)
```

```python
from contextlib import ExitStack

import numpy as np

import concourse.bass as bass
from concourse import mybir

ALU = mybir.AluOpType
ACT = mybir.ActivationFunctionType
AX = mybir.AxisListType
F32 = mybir.dt.float32
F16 = mybir.dt.float16
U32 = mybir.dt.uint32
I32 = mybir.dt.int32

P = 128
B, T, D = 2, 2048, 256
NTOK = B * T
KD = D // P
CH = P
NCH = NTOK // CH
BLK = 512
CPB = BLK // CH
NBLK = NTOK // BLK
BPB = T // BLK
H, DH = 16, 16
NP = 4 * H * DH
HE = DH + 1
E1, FF = 4, 1024
FC = FF // P
E2 = 8
W1C, W2C = KD * FF, FC * D
WC = W1C + W2C
TILE = 256
CAP = NTOK + 2 * TILE
LEAST = 2 * NTOK // TILE
MOST = LEAST + E2
SCALE = 256.0
INV = 1.0 / SCALE
NR = 8
NG = NCH // NR
EPS = 1e-5

PW, QKV, WO, WG, MG, RT = 0, 512, 2048, 2560, 3072, 3080
SMALL = 3096

F_DVE = ["conv0a", "conv0b", "conv1a", "conv1b", "conv2a", "conv2b", "ylo", "halo", "x2", "first",
         "delta", "x2lo", "dlo", "rot_cos", "rot_sin_a", "rot_sin_b", "rot", "phimin", "gz", "phi",
         "qlo", "klo"]
F_ACT = ["yhi", "x2hi", "dhi", "vext", "x2tok", "phiexp", "gt", "qhi", "khi"]
F_PE = ["pw", "qk", "v", "gate", "x2t"]
T_DVE = ["kS", "keep", "mask0", "mask1", "mask2", "mask3", "den", "rden", "attn", "kvt",
         "kvadd", "alo", "g2", "x3", "bn", "aggr", "h0", "hlo", "gmax", "ngmax", "rsum", "gw"]
T_ACT = ["qS", "qT", "ahi", "hhi", "gexp"]
T_PE = ["phit", "score", "av", "kv", "at", "wo", "ht", "lg"]
T_POOL = ["clear", "xres", "veps", "rstd", "hg", "hb"]
R_DVE = ["bn", "aggr", "x5", "xlo", "lg", "top", "dlt", "topi", "m1", "m2", "m12", "rank", "p1", "p2",
         "cnt", "idx", "pos"]
R_ACT = ["xhi"]
R_PE = ["xt", "rl", "rk"]
R_POOL = ["veps", "rstd", "keepx", "sent"]


def build(nc, x, xT, small, wdw, rows, moe1, moe1_b, moe2, moe2_b, b2rows, rope, masks, out):
    nc.disable_value_cache = True
    with ExitStack() as ctx:
        def sb(name, shape, dt=F32):
            return ctx.enter_context(nc.sbuf_tensor(name, shape, dt))

        def ps(name):
            return ctx.enter_context(nc.psum_tensor(name, [P, 512], F32))

        def sem(name):
            return ctx.enter_context(nc.semaphore(name))

        xg = nc.dram_tensor("expert_rows", [E2 * CAP, D], F32, kind="Internal")
        yg = nc.dram_tensor("expert_out", [(MOST + E2) * TILE, D], F32, kind="Internal")

        stage = sb("stage", [P, 2, W1C])
        small_hi, small_lo = sb("small_hi", [P, SMALL], F16), sb("small_lo", [P, SMALL], F16)
        w_hi, w_lo = sb("w_hi", [P, E1, WC], F16), sb("w_lo", [P, E1, WC], F16)
        wdw_s = sb("wdw_s", [P, KD * 3])
        rows_s = sb("rows_s", [P, 3 * D + E2])
        b1_s = sb("b1_s", [P, E1 * FC])
        b1r_s = sb("b1r_s", [P, E2 * FC])
        nb2 = (E1 + E2) * D
        e_hi, e_lo = w_hi[:, 0:2, :], w_lo[:, 0:2, :]
        b2_f = w_hi[0:2, 2:4, :].rearrange("p s c -> p (s c)").bitcast(F32)[:, 0:nb2 + 2]
        b2_h = w_lo[0:2, 2:4, :].rearrange("p s c -> p (s c)")[:, 0:nb2]
        b2_l = w_lo[0:2, 2:4, :].rearrange("p s c -> p (s c)")[:, nb2:2 * nb2]
        b2_row = sb("b2_row", [P, (E1 + E2) * D], F16)
        rope_s = sb("rope_s", [P, T // CH, 2, DH])
        masks_s = sb("masks_s", [P, masks.shape[1]])
        MO = {}
        o = 0
        for name, n in (("ident", P), ("causal", P), ("block", H // 2 * HE), ("even", 1), ("odd", 1),
                        ("keep", NCH + 1), ("new", NCH + 1), ("iota8", E2), ("base", E2)):
            MO[name] = masks_s[:, o:o + n]
            o += n
        ident, causal = MO["ident"], MO["causal"]
        ident16 = sb("ident16", [P, P], F16)
        before = sb("before", [P, P], F16)
        ones = sb("ones", [P, P], F16)
        mhalf = sb("mhalf", [P, 1])
        px5 = sb("px5", [P, D])
        zeros = px5

        xall = sb("xall", [P, NCH, D])
        xTb = sb("xTb", [P, 2, KD, BLK + 2])
        yT = sb("yT", [P, KD, CH])
        y_hi, y_lo = sb("y_hi", [P, KD, CH], F16), sb("y_lo", [P, KD, CH], F16)
        x2T = sb("x2T", [P, KD, CH + 1])
        x2_hi, x2_lo = sb("x2_hi", [P, KD, CH], F16), sb("x2_lo", [P, KD, CH], F16)
        dT, d_hi, d_lo = yT, y_hi, y_lo
        vext = sb("vext", [P, H, HE])
        x2tok = sb("x2tok", [P, D])
        gz, gt = sb("gz", [P, D]), sb("gt", [P, D])
        r1, r2, rq = sb("r1", [P, 2 * D]), sb("r2", [P, 2 * D]), sb("rq", [P, 2 * D])
        phm, phe = r1, r2
        phi = sb("phi", [P, 2 * D])
        qTs = r2[:, D:2 * D].rearrange("p (k n) -> p k n", k=KD)
        sm = sb("sm", [P, 4, 4, CH])
        parts = sm[:, :, :, :].rearrange("p a b n -> p (a b n)").bitcast(F16)
        qp, kp = (parts[:, n * NP:(n + 1) * NP].rearrange("p (h c d) -> p h c d", c=4, d=DH) for n in range(2))
        qS, kS = (parts[:, n * NP:(n + 1) * NP].rearrange("p (g n) -> p g n", n=CH) for n in (2, 3))
        state, kvt = sb("state", [P, KD, H // 2 * HE]), sb("kvt", [P, KD, H // 2 * HE])
        den, rden = sb("den", [P, H]), sb("rden", [P, H])
        attn = rq[:, 0:D]
        a_hi, a_lo = sb("a_hi", [P, KD, CH], F16), sb("a_lo", [P, KD, CH], F16)
        g2, x3 = gz, sb("x3", [P, D])
        bn, mv, rstd = sb("bn", [P, 6]), sb("mv", [P, 2]), sb("rstd", [P, 1])
        h0 = sb("h0", [P, D])
        hT_hi, hT_lo = sb("hT_hi", [P, 2, KD, BLK], F16), sb("hT_lo", [P, 2, KD, BLK], F16)
        gm, gn, ge, gs, gr = sb("gm", [P, 1]), sb("gn", [P, 1]), sb("ge", [P, E1]), sb("gs", [P, 1]), sb("gr", [P, 1])
        gw = sb("gw", [P, 2, CPB, E1])
        acc = sb("acc", [P, 2, CPB, D])
        s32 = sb("s32", [P, 2, BLK])
        h_hi, h_lo = sb("h_hi", [P, 4, BLK], F16), sb("h_lo", [P, 4, BLK], F16)
        pbn, pmv, prstd = sb("pbn", [P, 6]), sb("pmv", [P, 2]), sb("prstd", [P, 1])
        px_hi, px_lo = sb("px_hi", [P, KD, CH], F16), sb("px_lo", [P, KD, CH], F16)
        plg = sb("plg", [P, E2])
        top8 = sb("top8", [P, 8])
        topi = sb("topi", [P, 8], U32)
        m1, m2, m12 = sb("m1", [P, E2]), sb("m2", [P, E2]), sb("m12", [P, E2], F16)
        rank = sb("rank", [P, E2])
        count = sb("count", [P, E2])
        junk = sb("junk", [P, 2, E2])
        posf, pos = sb("posf", [P, 2]), sb("pos", [P, NCH, 2])
        idx, idx8 = sb("idx", [P, 2], U32), sb("idx8", [P, NR, 2], U32)
        cf, ci, ct = sb("cf", [P, E2]), sb("ci", [P, E2], I32), sb("ct", [P, E2], I32)
        ctf, cum = sb("ctf", [P, E2]), sb("cum", [P, E2])
        tabf = sb("tabf", [P, 3 * E2 + 1])
        tab = sb("tab", [P, 3 * E2 + 1], I32)
        xin, ysb = acc[:, 0, 0:2, :], acc[:, 1, 0:2, :]
        xt_hi, xt_lo = hT_hi[:, 0, :, 0:TILE], hT_lo[:, 0, :, 0:TILE]
        u32t = s32[:, :, :].rearrange("p a (b n) -> p (a b) n", n=TILE)
        u_hi, u_lo = (t[:, :, :].rearrange("p a (b n) -> p (a b) n", n=TILE) for t in (h_hi, h_lo))
        shift = junk[:, 0, :]
        move, moved = (g2[:, n * 2 * NCH:(n + 1) * 2 * NCH].rearrange("p (c a) -> p c a", a=2) for n in range(2))
        posy = g2[:, 4 * NCH:6 * NCH].rearrange("p (c a) -> p c a", a=2).bitcast(U32)
        dlt, wexp, wone = sb("dlt", [P, NCH]), *(kvt[:, 1, n * NCH:(n + 1) * NCH] for n in range(2))
        wt = sb("wt", [P, 2, NCH])
        rows8 = w_hi[:, :, :].rearrange("p e c -> p (e c)").bitcast(F32)[:, 0:NR * 2 * D]\
            .rearrange("p (r n d) -> p r n d", r=NR, n=2)
        fin = w_lo[:, :, :].rearrange("p e c -> p (e c)").bitcast(F32)[:, 0:2 * NR * D]\
            .rearrange("p (g r d) -> p g r d", g=2, r=NR)
        fbn, fmv = sb("fbn", [P, NR, 6]), sb("fmv", [P, NR, 2])
        fve, frs = sb("fve", [P, NR]), sb("frs", [P, NR])
        mhalf8 = kvt[:, 0, 0:NR]

        A = [ps(f"A{i}") for i in range(4)]
        Hb = [ps(f"H{i}") for i in range(2)]
        Yb = [ps(f"Y{i}") for i in range(2)]
        U = [A[1], A[2], A[3], Hb[0]]


        l_const, l_x, l_xT = sem("l_const"), sem("l_x"), sem("l_xT")
        l_stage = [sem(f"l_stage{i}") for i in range(2)]
        whi_done = sem("whi_done")
        passed = sem("passed")
        stage_used = sem("stage_used")
        small_split = sem("small_split")
        wch = sem("wch")
        w_ready = sem("w_ready")
        cst = sem("cst")
        b2_act, b2_dve = sem("b2_act"), sem("b2_dve")
        fdve, fact, fpe = sem("fdve"), sem("fact"), sem("fpe")
        tdve, tact, tpe, tpool = sem("tdve"), sem("tact"), sem("tpe"), sem("tpool")
        rdve, ract, rpe, rpool = sem("rdve"), sem("ract"), sem("rpe"), sem("rpool")
        g1_done, silu_done, hhi_done, hlo_done, g2_done, comb_done = (
            sem(n) for n in ("g1_done", "silu_done", "hhi_done", "hlo_done", "g2_done", "comb_done"))
        z_done, scat, tail_done = sem("z_done"), sem("scat"), sem("tail_done")
        cnt_chain, tab_ready = sem("cnt_chain"), sem("tab_ready")
        l_xin, xt_done, xthi_done, xtlo_done = sem("l_xin"), sem("xt_done"), sem("xthi_done"), sem("xtlo_done")
        u1_done, relu_done, uhi_done, ulo_done, u2_done, y_done, y_out = (
            sem(n) for n in ("u1_done", "relu_done", "uhi_done", "ulo_done", "u2_done", "y_done", "y_out"))
        wexp_done = sem("wexp_done")
        l_y = [sem(f"l_y{i}") for i in range(NR)]
        sum_done, stat_done, feps, frstd, normed = (
            sem(n) for n in ("sum_done", "stat_done", "feps", "frstd", "normed"))
        idx8_done, fin_out = sem("idx8_done"), [sem(f"fin_out{n}") for n in range(2)]

        def at(steps, q, name):
            if steps in (R_DVE, R_ACT, R_PE, R_POOL):
                q = q + 1
            return q * len(steps) + (steps.index(name) + 1)

        def before_chunk(eng, q, *waits, wait=None):
            for s, steps, name in waits:
                if not (isinstance(q, int) and q == 0):
                    wait(s, at(steps, q - 1, name)) if wait else eng.wait_ge(s, at(steps, q - 1, name))

        def pairs(ap):
            return ap.rearrange("p (g two) -> p g two", two=2)

        def cols(w, off, n):
            return w[:, off:off + KD * n].rearrange("p (k n) -> p k n", k=KD)

        block = ctx.enter_context(nc.Block())

        @block.sync
        def _(sp):
            for dst, src in ((masks_s[:, :], masks), (wdw_s[:, :], wdw), (rows_s[:, :], rows.partition_broadcast(P)),
                             (b1_s[:, :], moe1_b), (b1r_s[:, :], moe2_b), (b2_f, b2rows),
                             (rope_s[:, :, :, :], rope)):
                sp.dma_start(dst, src).then_inc(l_const, 16)
            for n in range(2):
                w = W1C if n == 0 else SMALL - W1C
                sp.dma_start(stage[:, n, 0:w], small[:, n * W1C:n * W1C + w]).then_inc(l_stage[n], 16)

            def load_xT(n):
                nb = n if n < NBLK else 0
                sp.dma_start(xTb[:, n % 2, :, :], xT[:, :, nb // BPB, (nb % BPB) * BLK:(nb % BPB) * BLK + BLK + 2])\
                  .then_inc(l_xT, 16)
                sp.wait_ge(l_xT, 16 * (n + 1))

            def load_x(n):
                sp.dma_start(xall[:, n * CPB:(n + 1) * CPB, :],
                             x[n * BLK:(n + 1) * BLK, :].rearrange("(c p) d -> p c d", p=P)).then_inc(l_x, 16)
                sp.wait_ge(l_x, 16 * (n + 1))

            load_xT(0)
            load_x(0)
            load_xT(1)
            for n in range(2 * E1):
                sp.wait_ge(stage_used, n + 1)
                sp.dma_start(stage[:, n % 2, :], moe1[:, n * W1C:(n + 1) * W1C]).then_inc(l_stage[n % 2], 16)
                if n < NBLK - 1:
                    load_x(n + 1)
            sp.wait_ge(cst, 4)
            for e in range(E2):
                sp.dma_start(xg[e * CAP:e * CAP + TILE, :].rearrange("(s p) d -> p s d", p=P),
                             zeros[:, :].unsqueeze(1).broadcast_to([P, TILE // P, D])).then_inc(z_done, 16)
            for n in range(2):
                sp.wait_ge(stage_used, 2 * E1 + n + 1)
                sp.dma_start(stage[:, n % 2, :], moe2[0, :, n * W1C:(n + 1) * W1C]).then_inc(l_stage[n % 2], 16)
            for n in range(2, NBLK + 1):
                sp.wait_ge(fdve, at(F_DVE, CPB * (n - 2) + CPB - 1, "x2"))
                load_xT(n)
            sp.wait_ge(tab_ready, 1)
            sp.wait_ge(z_done, 16 * E2)
            for e in range(E2):
                first = sp.value_load(tab[0:1, 2 * E2 + e:2 * E2 + e + 1], min_val=e * CAP, max_val=e * CAP + NTOK)
                sp.dma_start(xg[bass.ds(first, TILE), :].rearrange("(s p) d -> p s d", p=P),
                             zeros[:, :].unsqueeze(1).broadcast_to([P, TILE // P, D])).then_inc(tail_done, 16)
            ng = sp.value_load(tab[0:1, 3 * E2:3 * E2 + 1], min_val=LEAST, max_val=MOST)
            sp.dma_start(yg[bass.ds(ng * TILE, E2 * TILE), :].rearrange("(s p) d -> p s d", p=P),
                         zeros[:, :].unsqueeze(1).broadcast_to([P, E2 * TILE // P, D])).then_inc(tail_done, 16)
            sp.wait_ge(tail_done, 16 * (E2 + 1))
            sp.wait_ge(scat, 32 * NCH)
            with sp.Fori(0, E2) as e:
                nt = sp.value_load(tab[0:1, bass.ds(e, 1)], min_val=1, max_val=NTOK // TILE)
                tb = sp.value_load(tab[0:1, bass.ds(e + E2, 1)], min_val=0, max_val=MOST)
                for n in range(2):
                    sp.wait_ge(stage_used, 2 * E1 + 3 + n + 2 * e)
                    sp.dma_start(stage[:, n, :], moe2[bass.ds((e + 1) % E2, 1), :, n * W1C:(n + 1) * W1C]
                                 .rearrange("a p c -> p (a c)")).then_inc(l_stage[n], 16)
                with sp.Fori(0, nt) as t:
                    sp.wait_ge(xt_done, tb + t + 1)
                    sp.dma_start(xin[:, :, :], xg[bass.ds(e * CAP + t * TILE, TILE), :]
                                 .rearrange("(s p) d -> p s d", p=P)).then_inc(l_xin, 16)
            sp.wait_ge(xt_done, ng + 1)
            sp.dma_start(xin[:, :, :], xg[0:TILE, :].rearrange("(s p) d -> p s d", p=P)).then_inc(l_xin, 16)
            for i in range(NG):
                sp.wait_ge(normed, (i + 1) * NR)
                sp.dma_start(out[i * NR * P:(i + 1) * NR * P, :].rearrange("(r p) d -> p r d", p=P), fin[:, i % 2, :, :])\
                  .then_inc(fin_out[i % 2], 16)
            for n in range(2):
                sp.wait_ge(fin_out[n], 16 * (NG // 2))

        @block.tensor
        def _(pe):
            pe.sem_inc(rpe, len(R_PE))
            pe.sem_inc(xt_done, 1)
            pe.sem_inc(u2_done, 1)
            mm = nc.tensor.matmul

            def three(outp, wl, xl, first=True, last=True):
                n = len(wl[0])
                for k in range(n):
                    for i, (a, b) in enumerate(((0, 0), (0, 1), (1, 0))):
                        ins = mm(outp, wl[a][k], xl[b][k], start=first and k == 0 and i == 0,
                                 stop=last and k == n - 1 and i == 2, skip_group_check=True)
                return ins

            def ks(t, off=0, n=None):
                return [t[:, k, off:off + n] if n else t[:, k, :] for k in range(KD)]

            def front_pw(q):
                pe.wait_ge(fdve, at(F_DVE, q, "ylo"))
                before_chunk(pe, q, (tdve, T_DVE, "kvt"))
                for eh in range(KD):
                    ins = three(A[1][:, eh * P:(eh + 1) * P],
                                [ks(cols(small_hi, PW, D), eh * P, P), ks(cols(small_lo, PW, D), eh * P, P)],
                                [ks(y_hi), ks(y_lo)])
                ins.then_inc(fpe, 1)

            def front_qkv(q):
                pe.wait_ge(fdve, at(F_DVE, q, "dlo"))
                w = [[t[:, QKV + k * 768:QKV + k * 768 + 512] for k in range(KD)] for t in (small_hi, small_lo)]
                wv = [[t[:, QKV + k * 768 + 512:QKV + (k + 1) * 768] for k in range(KD)] for t in (small_hi, small_lo)]
                three(A[1][:, :], [ks(x2_hi), ks(x2_lo)], w).then_inc(fpe, 1)
                three(A[2][:, 0:D], [ks(x2_hi), ks(x2_lo)], wv).then_inc(fpe, 1)
                three(A[2][:, D:2 * D], [ks(d_hi), ks(d_lo)],
                      [ks(cols(small_hi, WG, D)), ks(cols(small_lo, WG, D))]).then_inc(fpe, 1)
                if not (isinstance(q, int) and q <= 8):
                    pe.wait_ge(rdve, at(R_DVE, q - 9, "cnt"))
                for k in range(KD):
                    ins = nc.tensor.transpose(A[0][:, D + k * P:D + (k + 1) * P], x2T[:, k, 1:CH + 1], ident)
                ins.then_inc(fpe, 1)

            def phit(q):
                pe.wait_ge(fdve, at(F_DVE, q, "klo"))
                before_chunk(pe, q, (tpool, T_POOL, "clear"))
                for src, bank in ((parts[:, 0:NP], A[1]), (parts[:, NP:2 * NP], A[2])):
                    for g in range(H // 2):
                        nc.tensor.transpose(bank[:, :].bitcast(F16)[:, g * P:(g + 1) * P], src[:, g * P:(g + 1) * P],
                                            ident16[:, :])
                for n in range(KD):
                    ins = nc.tensor.transpose(A[3][:, n * P:(n + 1) * P], phi[:, n * P:(n + 1) * P], ident)
                ins.then_inc(tpe, 1)

            def score(q):
                pe.wait_ge(tact, at(T_ACT, q, "qT"))
                pe.wait_ge(tdve, at(T_DVE, q, "kS"))
                for h in range(H):
                    bank, o, r = (h % 2) * 2 + h // 8, (h % 8) // 2 * CH, (h % 2) * 64
                    ins = mm(A[bank][:, o:o + CH], kS[r:r + 3 * DH, h // 2, :], qS[r:r + 3 * DH, h // 2, :],
                             start=True, stop=True, skip_group_check=True)
                ins.then_inc(tpe, 1)

            def av(q, between):
                pe.wait_ge(tdve, at(T_DVE, q, "mask3"))
                for half in range(KD):
                    o = half * H // 2 * HE
                    mm(A[0][:, o:o + H // 2 * HE], qTs[:, half, :], state[:, half, :],
                       start=half == 0, stop=False, skip_group_check=True)
                    for h8 in range(H // 2):
                        if between and h8 in (1, 4, 7):
                            next(between)
                        ins = mm(A[0][:, o + h8 * HE:o + (h8 + 1) * HE], sm[:, (h8 % 2) * 2 + half, h8 // 2, :],
                                 vext[:, half * H // 2 + h8, :], start=False, stop=True, skip_group_check=True)
                ins.then_inc(tpe, 1)
                for half in range(KD):
                    ins = mm(A[1][:, half * H // 2 * HE:(half + 1) * H // 2 * HE], phi[:, D + half * P:D + (half + 1) * P],
                             vext[:, half * H // 2:(half + 1) * H // 2, :], start=True, stop=True, skip_group_check=True)
                ins.then_inc(tpe, 1)

            def at_(q):
                pe.wait_ge(tdve, at(T_DVE, q, "attn"))
                for k in range(KD):
                    ins = nc.tensor.transpose(A[2][:, k * P:(k + 1) * P], attn[:, k * P:(k + 1) * P], ident)
                ins.then_inc(tpe, 1)

            def wo(q):
                pe.wait_ge(tdve, at(T_DVE, q, "alo"))
                three(A[3][:, 0:D], [ks(a_hi), ks(a_lo)],
                      [ks(cols(small_hi, WO, D)), ks(cols(small_lo, WO, D))]).then_inc(tpe, 1)

            def ht(q):
                pe.wait_ge(tpool, at(T_POOL, q, "hb"))
                for k in range(KD):
                    ins = nc.tensor.transpose(A[3][:, D + k * P:D + (k + 1) * P], h0[:, k * P:(k + 1) * P], ident)
                ins.then_inc(tpe, 1)

            def lg(q, b, j):
                pe.wait_ge(tdve, at(T_DVE, q, "hlo"))
                s = b % 2
                three(A[3][:, 0:E1], [[t[:, s, k, j * P:(j + 1) * P] for k in range(KD)] for t in (hT_hi, hT_lo)],
                      [ks(cols(small_hi, MG, E1)), ks(cols(small_lo, MG, E1))]).then_inc(tpe, 1)

            def g1(b, n, i):
                e, c, s = n // FC, n % FC, b % 2
                u = i * E1 * FC + n
                if n == 0:
                    pe.wait_ge(tdve, at(T_DVE, i * CPB + CPB - 1, "hlo"))
                if b == 0 and c == 0:
                    pe.wait_ge(w_ready, 2 * (e + 1))
                if not (isinstance(u, int) and u < 2):
                    pe.wait_ge(silu_done, u - 1)
                ws = [[t[:, e, k * FF + c * P:k * FF + (c + 1) * P] for k in range(KD)] for t in (w_hi, w_lo)]
                xs = [ks(hT_hi[:, s]), ks(hT_lo[:, s])]
                for k in range(KD):
                    for m, (a, x_) in enumerate(((0, 0), (0, 1), (1, 0))):
                        ins = mm(Hb[n % 2][:, :], ws[a][k], xs[x_][k], start=k == 0 and m == 0,
                                 stop=k == KD - 1 and m == 2, skip_group_check=True)
                        if k == KD - 1 and m == 2:
                            ins.then_inc(g1_done, 1)
                        yield

            def g2_(n, i):
                e, c, s = n // FC, n % FC, n % 4
                u = i * E1 * FC + n
                pe.wait_ge(hlo_done, u + 1)
                if c == 0:
                    pe.wait_ge(b2_dve, 3)
                    if not (isinstance(u, int) and u == 0):
                        pe.wait_ge(comb_done, (i * E1 + e) * CPB)
                    for t in range(CPB):
                        mm(Yb[t // 2][:, (t % 2) * D:(t % 2 + 1) * D], ones[:, :], b2_row[:, e * D:(e + 1) * D],
                           start=t % 2 == 0, stop=False, skip_group_check=True)
                for t in range(CPB):
                    w = [t2[:, e, W1C + c * D:W1C + (c + 1) * D] for t2 in (w_hi, w_lo)]
                    ins = three(Yb[t // 2][:, (t % 2) * D:(t % 2 + 1) * D],
                                [[h_hi[:, s, t * P:(t + 1) * P]], [h_lo[:, s, t * P:(t + 1) * P]]],
                                [[w[0]], [w[1]]], first=False, last=c == FC - 1)
                ins.then_inc(g2_done, 1)

            def post_xt(p):
                pe.wait_ge(rdve, at(R_DVE, p, "x5"))
                for k in range(KD):
                    ins = nc.tensor.transpose(A[0][:, k * P:(k + 1) * P], px5[:, k * P:(k + 1) * P], ident)
                ins.then_inc(rpe, 1)

            def post_rl(p):
                pe.wait_ge(rdve, at(R_DVE, p, "xlo"))
                three(A[0][:, D:D + E2], [ks(px_hi), ks(px_lo)],
                      [ks(cols(small_hi, RT, E2)), ks(cols(small_lo, RT, E2))]).then_inc(rpe, 1)

            def post_rk(p):
                pe.wait_ge(rdve, at(R_DVE, p, "m12"))
                mm(A[0][:, 2 * D - 2 * E2:2 * D - E2], before[:, :], m12[:, :], start=True, stop=True, skip_group_check=True)
                mm(A[0][:, 2 * D - E2:2 * D], ones[:, :], m12[:, :], start=True, stop=True, skip_group_check=True)\
                    .then_inc(rpe, 1)

            def step(b, i, j, ffn=True, att=True, post=True):
                q = (i + 1) * CPB + j
                p = (i - 1) * CPB + j
                for c in range(FC):
                    if att:
                        if c == 0: phit(q)
                        if c == 1: score(q)
                        if c == 2: av(q, g1(b, j * FC + c, i) if ffn else None)
                        if c == 3: at_(q); front_pw(q + 1)
                    if post:
                        if c == 3: post_xt(p)
                        if c == 4: post_rl(p)
                        if c == 5: post_rk(p)
                    if att:
                        if c == 5: front_qkv(q + 1)
                    if ffn and not (att and c == 2):
                        for _ in g1(b, j * FC + c, i):
                            pass
                    if att:
                        if c == 3: wo(q)
                        if c == 5: ht(q)
                        if c == 6: lg(q, b + 1, j)
                    if ffn:
                        n = j * FC + c - 2
                        if n >= 0:
                            g2_(n, i)
                        elif not (isinstance(i, int) and i == 0):
                            g2_(n + E1 * FC, i - 1)

            pe.wait_ge(small_split, 4)
            pe.wait_ge(cst, 9)
            pe.wait_ge(l_const, 16 * 7)
            front_pw(0)
            front_qkv(0)
            for j in range(CPB):
                step(-1, -1, j, ffn=False, post=False)
            for j in range(CPB):
                step(0, 0, j, post=False)
            with pe.Fori(0, (NBLK - 2) // 2) as i:
                for b in (1, 2):
                    for j in range(CPB):
                        step(b, 2 * i + b, j)
            pe.wait_ge(fact, at(F_ACT, NCH, "gt"))
            for j in range(CPB):
                step(NBLK - 1, NBLK - 1, j, att=False)
            for n in (2, 1):
                g2_(E1 * FC - n, NBLK - 1)
            for j in range(CPB):
                step(NBLK, NBLK, j, ffn=False, att=False)

            def transposes(g):
                pe.wait_ge(l_xin, 16 * (g + 1))
                if not (isinstance(g, int) and g == 0):
                    pe.wait_ge(xtlo_done, g)
                for s in range(2):
                    for k in range(KD):
                        ins = nc.tensor.transpose(A[0][:, k * TILE + s * P:k * TILE + (s + 1) * P],
                                                  xin[:, s, k * P:(k + 1) * P], ident)
                ins.then_inc(xt_done, 1)

            transposes(0)
            with pe.Fori(0, E2 // 2) as ep:
                for s in range(2):
                    e = 2 * ep + s
                    nt = pe.value_load(tab[0:1, bass.ds(e, 1)], min_val=1, max_val=NTOK // TILE)
                    tb = pe.value_load(tab[0:1, bass.ds(e + E2, 1)], min_val=0, max_val=MOST)
                    pe.wait_ge(w_ready, 2 * E1 + 2 + 2 * e)
                    pe.sem_inc(passed, 1)
                    with pe.Fori(0, nt) as t:
                        g = pe.snap(tb + t)
                        pe.wait_ge(xthi_done, g + 1)
                        pe.wait_ge(xtlo_done, g + 1)
                        for n in range(FC + 4):
                            if n < FC:
                                if n >= 4:
                                    pe.wait_ge(relu_done, g * FC + n - 3)
                                three(U[n % 4][:, 0:TILE],
                                      [[w[:, s, k * FF + n * P:k * FF + (n + 1) * P] for k in range(KD)] for w in (e_hi, e_lo)],
                                      [ks(xt_hi), ks(xt_lo)]).then_inc(u1_done, 1)
                            if n == 5:
                                transposes(g + 1)
                            if n >= 4:
                                c = n - 4
                                pe.wait_ge(uhi_done, g * FC + c + 1)
                                pe.wait_ge(ulo_done, g * FC + c + 2)
                                if c == 0:
                                    pe.wait_ge(y_done, g + 1)
                                    for r in range(2):
                                        mm(Yb[0][:, r * D:(r + 1) * D], ones[:, :], b2_row[:, bass.ds((e + E1) * D, D)],
                                           start=r == 0, stop=False, skip_group_check=True)
                                w = [[t2[:, s, W1C + c * D:W1C + (c + 1) * D]] for t2 in (e_hi, e_lo)]
                                for r in range(2):
                                    ins = three(Yb[0][:, r * D:(r + 1) * D],
                                                [[u_hi[:, c, r * P:(r + 1) * P]], [u_lo[:, c, r * P:(r + 1) * P]]], w,
                                                first=False, last=c == FC - 1)
                        ins.then_inc(u2_done, 1)

        @block.vector
        def _(dve):
            dve.sem_inc(rdve, len(R_DVE))
            dve.sem_inc(ulo_done, 1)
            dve.sem_inc(y_done, 1)
            V = nc.vector

            def split_lo(out_, in_, hi, scale=1.0):
                return V.scalar_tensor_tensor(out=out_, in0=in_, scalar=scale, in1=hi, op0=ALU.mult, op1=ALU.subtract)

            def front_conv(q, b, j, i):
                xt = xTb[:, b % 2]
                if j == 0:
                    dve.wait_ge(l_xT, 16 * (i + 1))
                for tap in range(3):
                    for k in range(KD):
                        src, w = xt[:, k, j * CH + tap:j * CH + tap + CH], wdw_s[:, k * 3 + tap:k * 3 + tap + 1]
                        if tap == 0:
                            V.tensor_scalar(yT[:, k, :], src, w, None, ALU.mult).then_inc(fdve, 1)
                        else:
                            dve.wait_ge(fdve, at(F_DVE, q, f"conv{tap - 1}{'ab'[k]}"))
                            V.scalar_tensor_tensor(out=yT[:, k, :], in0=src, scalar=w, in1=yT[:, k, :],
                                                   op0=ALU.mult, op1=ALU.add).then_inc(fdve, 1)

            def front_ylo(q):
                dve.wait_ge(fact, at(F_ACT, q, "yhi"))
                split_lo(y_lo[:, :, :], yT[:, :, :], y_hi[:, :, :]).then_inc(fdve, 1)

            def front_x2(q, b, j):
                xt = xTb[:, b % 2]
                if isinstance(q, int) and q == 0:
                    V.memset(x2T[:, :, 0:1], 0.0).then_inc(fdve, 1)
                else:
                    V.tensor_scalar(x2T[:, :, 0:1], x2T[:, :, CH:CH + 1], MO["keep"][:, bass.ds(q, 1)], None,
                                    ALU.mult).then_inc(fdve, 1)
                dve.wait_ge(fpe, at(F_PE, q, "pw"))
                dve.wait_ge(fdve, at(F_DVE, q, "halo"))
                V.scalar_tensor_tensor(out=x2T[:, :, 1:CH + 1], in0=A[1][:, 0:D].rearrange("p (k n) -> p k n", k=KD),
                                       scalar=INV, in1=xt[:, :, 2 + j * CH:2 + j * CH + CH],
                                       op0=ALU.mult, op1=ALU.add).then_inc(fdve, 1)
                dve.wait_ge(fdve, at(F_DVE, q, "x2"))
                V.scalar_tensor_tensor(out=x2T[:, :, 0:1], in0=x2T[:, :, 1:2], scalar=MO["new"][:, bass.ds(q, 1)],
                                       in1=x2T[:, :, 0:1], op0=ALU.mult, op1=ALU.add).then_inc(fdve, 1)
                dve.wait_ge(fdve, at(F_DVE, q, "first"))
                V.tensor_tensor(dT[:, :, :], x2T[:, :, 1:CH + 1], x2T[:, :, 0:CH], ALU.subtract).then_inc(fdve, 1)
                dve.wait_ge(fact, at(F_ACT, q, "x2hi"))
                split_lo(x2_lo[:, :, :], x2T[:, :, 1:CH + 1], x2_hi[:, :, :]).then_inc(fdve, 1)
                dve.wait_ge(fact, at(F_ACT, q, "dhi"))
                split_lo(d_lo[:, :, :], dT[:, :, :], d_hi[:, :, :]).then_inc(fdve, 1)

            def front_phi(q, c):
                cos = rope_s[:, bass.ds(c, 1), 0, :].broadcast_to([P, 2 * H, DH])
                sin = rope_s[:, bass.ds(c, 1), 1, :].broadcast_to([P, 2 * H, DH])
                qk = A[1][:, :].rearrange("p (h d) -> p h d", d=DH)
                dve.wait_ge(fpe, at(F_PE, q, "qk"))
                V.tensor_tensor(r1[:, :].rearrange("p (h d) -> p h d", d=DH), qk, cos, ALU.mult).then_inc(fdve, 1)
                r2v = r2[:, :].rearrange("p (h d) -> p h d", d=DH)
                V.tensor_tensor(r2v[:, :, 0:DH:2], qk[:, :, 1:DH:2], sin[:, :, 0:DH:2], ALU.mult).then_inc(fdve, 1)
                V.tensor_tensor(r2v[:, :, 1:DH:2], qk[:, :, 0:DH:2], sin[:, :, 1:DH:2], ALU.mult).then_inc(fdve, 1)
                dve.wait_ge(fdve, at(F_DVE, q, "rot_sin_b"))
                V.tensor_tensor(rq[:, :], r1[:, :], r2[:, :], ALU.add).then_inc(fdve, 1)
                dve.wait_ge(fdve, at(F_DVE, q, "rot"))
                V.tensor_scalar(phm[:, :], rq[:, :], 0.0, None, ALU.min).then_inc(fdve, 1)

            def front_phi2(q):
                dve.wait_ge(fact, at(F_ACT, q, "vext"))
                V.scalar_tensor_tensor(out=gz[:, :], in0=A[2][:, D:2 * D], scalar=INV, in1=rows_s[:, 0:D],
                                       op0=ALU.mult, op1=ALU.add).then_inc(fdve, 1)
                dve.wait_ge(fact, at(F_ACT, q, "phiexp"))
                V.scalar_tensor_tensor(out=phi[:, :], in0=rq[:, :], scalar=0.0, in1=phe[:, :],
                                       op0=ALU.max, op1=ALU.add).then_inc(fdve, 1)

            def front_lo(q):
                dve.wait_ge(fact, at(F_ACT, q, "khi"))
                for n, (t, lo) in enumerate(((qp, 2), (kp, 1))):
                    split_lo(t[:, :, lo, :], phi[:, n * D:(n + 1) * D].rearrange("p (h d) -> p h d", d=DH), t[:, :, 0, :])\
                        .then_inc(fdve, 1)

            def tail_kS(q):
                dve.wait_ge(tpe, at(T_PE, q, "phit"))
                V.tensor_copy(kS, A[2][:, :].bitcast(F16).rearrange("p (g n) -> p g n", n=CH)).then_inc(tdve, 1)
                V.tensor_scalar(state[:, :, :], state[:, :, :], MO["keep"][:, bass.ds(q, 1)], None,
                                ALU.mult).then_inc(tdve, 1)

            def tail_mask(q):
                dve.wait_ge(tpe, at(T_PE, q, "score"))
                for j in range(4):
                    V.tensor_tensor(sm[:, j, :, :], A[j][:, :].rearrange("p (m n) -> p m n", m=4),
                                    causal.unsqueeze(1).broadcast_to([P, 4, CH]), ALU.mult).then_inc(tdve, 1)

            def tail_attn(q):
                o = A[0][:, 0:H * HE].rearrange("p (h e) -> p h e", e=HE)
                dve.wait_ge(tpe, at(T_PE, q, "av"))
                V.tensor_scalar(den[:, :].unsqueeze(2), o[:, :, DH:HE], 1e-6, None, ALU.add).then_inc(tdve, 1)
                dve.wait_ge(tdve, at(T_DVE, q, "den"))
                V.reciprocal(rden[:, :], den[:, :]).then_inc(tdve, 1)
                dve.wait_ge(tdve, at(T_DVE, q, "rden"))
                V.tensor_tensor(attn[:, :].rearrange("p (h d) -> p h d", d=DH), o[:, :, 0:DH],
                                rden[:, :].unsqueeze(2).broadcast_to([P, H, DH]), ALU.mult).then_inc(tdve, 1)
                dve.wait_ge(tpe, at(T_PE, q, "kv"))
                V.tensor_tensor(kvt[:, :, :], A[1][:, 0:H * HE].rearrange("p (k n) -> p k n", k=KD),
                                MO["block"].unsqueeze(1).broadcast_to([P, KD, H // 2 * HE]), ALU.mult).then_inc(tdve, 1)
                dve.wait_ge(tdve, at(T_DVE, q, "kvt"))
                V.tensor_tensor(state[:, :, :], state[:, :, :], kvt[:, :, :], ALU.add).then_inc(tdve, 1)

            def tail_alo(q):
                dve.wait_ge(tact, at(T_ACT, q, "ahi"))
                split_lo(a_lo[:, :, :], A[2][:, 0:D].rearrange("p (k n) -> p k n", k=KD), a_hi[:, :, :]).then_inc(tdve, 1)

            def norm(sem_, steps, q, bn_, mv_, src, names):
                V.bn_stats(bn_[:, :], src).then_inc(sem_, 1)
                dve.wait_ge(sem_, at(steps, q, names[0]))
                dve.sem_inc(passed, 1)
                V.bn_aggr(mv_[:, :], bn_[:, :]).then_inc(sem_, 1)

            def tail_x3(q):
                dve.wait_ge(tpe, at(T_PE, q, "wo"))
                V.scalar_tensor_tensor(out=g2[:, :], in0=gt[:, :], scalar=1.0, in1=A[3][:, 0:D],
                                       op0=ALU.add, op1=ALU.mult).then_inc(tdve, 1)
                dve.wait_ge(tdve, at(T_DVE, q, "g2"))
                V.scalar_tensor_tensor(out=x3[:, :], in0=g2[:, :], scalar=0.5 * INV, in1=x2tok[:, :],
                                       op0=ALU.mult, op1=ALU.add).then_inc(tdve, 1)
                dve.wait_ge(tdve, at(T_DVE, q, "x3"))
                norm(tdve, T_DVE, q, bn, mv, x3[:, :], ("bn",))

            def tail_h0(q):
                dve.wait_ge(tpool, at(T_POOL, q, "rstd"))
                V.tensor_scalar(h0[:, :], x3[:, :], mv[:, 0:1], rstd[:, 0:1], ALU.subtract, ALU.mult).then_inc(tdve, 1)

            def tail_hlo(q, b, j):
                dve.wait_ge(tact, at(T_ACT, q, "hhi"))
                split_lo(hT_lo[:, b % 2, :, j * CH:(j + 1) * CH], A[3][:, D:2 * D].rearrange("p (k n) -> p k n", k=KD),
                         hT_hi[:, b % 2, :, j * CH:(j + 1) * CH]).then_inc(tdve, 1)

            def tail_gmax(q):
                dve.wait_ge(tpe, at(T_PE, q, "lg"))
                V.tensor_reduce(gm[:, :], A[3][:, 0:E1], AX.X, ALU.max).then_inc(tdve, 1)
                dve.wait_ge(tdve, at(T_DVE, q, "gmax"))
                V.tensor_scalar(gn[:, :], gm[:, :], -INV, None, ALU.mult).then_inc(tdve, 1)

            def tail_gate(q, b, j):
                dve.wait_ge(tact, at(T_ACT, q, "gexp"))
                V.reciprocal(gr[:, :], gs[:, :]).then_inc(tdve, 1)
                dve.wait_ge(tdve, at(T_DVE, q, "rsum"))
                V.tensor_scalar(gw[:, b % 2, j, :], ge[:, :], gr[:, 0:1], INV, ALU.mult, ALU.mult).then_inc(tdve, 1)

            def split_half_lo(n):
                dve.wait_ge(whi_done, n + 1)
                split_lo(w_lo[:, n // 2, (n % 2) * W1C:(n % 2 + 1) * W1C], stage[:, n % 2, :],
                         w_hi[:, n // 2, (n % 2) * W1C:(n % 2 + 1) * W1C], SCALE).then_inc(w_ready, 1)

            def hlo(n, i):
                u = i * E1 * FC + n
                dve.wait_ge(hhi_done, u + 1)
                V.tensor_tensor(h_lo[:, n % 4, :], s32[:, n % 2, :], h_hi[:, n % 4, :], ALU.subtract).then_inc(hlo_done, 1)

            def comb(e, b, i):
                dve.wait_ge(g2_done, (i * E1 + e + 1) * FC)
                if e == 0:
                    dve.wait_ge(tpool, at(T_POOL, i * CPB + CPB - 1, "xres"))
                    dve.wait_ge(tdve, at(T_DVE, i * CPB + CPB - 1, "gw"))
                else:
                    dve.wait_ge(comb_done, (i * E1 + e) * CPB)
                for t in range(CPB):
                    a = acc[:, b % 2, t, :]
                    V.scalar_tensor_tensor(out=a, in0=Yb[t // 2][:, (t % 2) * D:(t % 2 + 1) * D],
                                           scalar=gw[:, b % 2, t, e:e + 1], in1=a,
                                           op0=ALU.mult, op1=ALU.add).then_inc(comb_done, 1)

            def post_norm(p, b, j, i):
                dve.wait_ge(comb_done, (i * E1 + E1 - 1) * CPB + j + 1)
                norm(rdve, R_DVE, p, pbn, pmv, acc[:, b % 2, j, :], ("bn",))

            def post_x5(p, b, j):
                dve.wait_ge(rpool, at(R_POOL, p, "rstd"))
                before_chunk(dve, p, (rpool, R_POOL, "sent"))
                V.tensor_scalar(px5[:, :], acc[:, b % 2, j, :],
                                pmv[:, 0:1], prstd[:, 0:1], ALU.subtract, ALU.mult).then_inc(rdve, 1)

            def post_xlo(p):
                dve.wait_ge(ract, at(R_ACT, p, "xhi"))
                split_lo(px_lo[:, :, :], A[0][:, 0:D].rearrange("p (k n) -> p k n", k=KD), px_hi[:, :, :]).then_inc(rdve, 1)

            def post_route(p):
                dve.wait_ge(rpe, at(R_PE, p, "rl"))
                V.scalar_tensor_tensor(out=plg[:, :], in0=A[0][:, D:D + E2], scalar=INV, in1=rows_s[:, 3 * D:3 * D + E2],
                                       op0=ALU.mult, op1=ALU.add).then_inc(rdve, 1)
                dve.wait_ge(rdve, at(R_DVE, p, "lg"))
                dve.sem_inc(passed, 1)
                V.max(top8[:, :], plg[:, :]).then_inc(rdve, 1)
                dve.wait_ge(rdve, at(R_DVE, p, "top"))
                dve.sem_inc(passed, 1)
                V.tensor_tensor(dlt[:, bass.ds(p, 1)], top8[:, 1:2], top8[:, 0:1], ALU.subtract).then_inc(rdve, 1)
                V.max_index(topi[:, :], top8[:, :], plg[:, :]).then_inc(rdve, 1)
                dve.wait_ge(rdve, at(R_DVE, p, "topi"))
                V.tensor_scalar(m1[:, :], MO["iota8"], topi[:, 0:1], None, ALU.is_equal).then_inc(rdve, 1)
                V.tensor_scalar(m2[:, :], MO["iota8"], topi[:, 1:2], None, ALU.is_equal).then_inc(rdve, 1)
                dve.wait_ge(rdve, at(R_DVE, p, "m2"))
                V.tensor_tensor(m12[:, :], m1[:, :], m2[:, :], ALU.add).then_inc(rdve, 1)

            def post_rank(p):
                dve.wait_ge(rpe, at(R_PE, p, "rk"))
                V.tensor_tensor(rank[:, :], A[0][:, 2 * D - 2 * E2:2 * D - E2], count[:, :], ALU.add).then_inc(rdve, 1)
                dve.wait_ge(rdve, at(R_DVE, p, "rank"))
                for n, m in enumerate((m1, m2)):
                    V.tensor_tensor_reduce(junk[:, n, :], m[:, :], rank[:, :], 1.0, 0.0, ALU.mult, ALU.add,
                                           posf[:, n:n + 1]).then_inc(rdve, 1)
                V.tensor_tensor(count[:, :], count[:, :], A[0][:, 2 * D - E2:2 * D], ALU.add).then_inc(rdve, 1)
                dve.wait_ge(rdve, at(R_DVE, p, "p2"))
                V.tensor_copy(idx[:, :], posf[:, :]).then_inc(rdve, 1)
                V.tensor_copy(pos[:, bass.ds(p, 1), :].rearrange("p a d -> p (a d)"), posf[:, :]).then_inc(rdve, 1)

            def step(b, i, j, ffn=True, att=True, post=True, w_split=False):
                q = (i + 1) * CPB + j
                nb, nj = b + 1 + (j == CPB - 1), (j + 1) % CPB
                p = (i - 1) * CPB + j
                for c in range(FC):
                    if att:
                        if c == 0: tail_kS(q)
                    if ffn and c == 0:
                        if j > 0:
                            hlo(j * FC - 1, i)
                        elif not (isinstance(i, int) and i == 0):
                            hlo(E1 * FC - 1, i - 1)
                    if att:
                        if c == 1: tail_mask(q)
                    if ffn and c == 1:
                        hlo(j * FC, i)
                    if att:
                        if c == 2: front_ylo(q + 1)
                    if ffn and c == 2:
                        if j > 0:
                            comb(j - 1, b, i)
                        elif not (isinstance(i, int) and i == 0):
                            comb(E1 - 1, b - 1, i - 1)
                    if post and c == 2:
                        post_norm(p, b - 1, j, i - 1)
                        post_x5(p, b - 1, j)
                    if att:
                        if c == 2: tail_attn(q)
                        if c == 3: tail_alo(q); front_x2(q + 1, nb, nj)
                    if post and c == 3:
                        post_xlo(p)
                    if att and c == 3:
                        tail_x3(q)
                    if post and c == 4:
                        post_route(p)
                    if ffn and c == 4:
                        hlo(j * FC + c - 1, i)
                    if att and c == 4:
                        tail_h0(q)
                    if post and c == 5:
                        post_rank(p)
                    if att:
                        if c == 5: front_phi(q + 1, row_chunk(q + 1)); tail_hlo(q, b + 1, j)
                        if c == 6:
                            tail_gmax(q)
                            front_phi2(q + 1)
                            front_lo(q + 1)
                            front_conv(q + 2, b + 1 + (j >= CPB - 2), (j + 2) % CPB, i + 1 + (j >= CPB - 2))
                        if c == 7: tail_gate(q, b + 1, j)
                    if w_split:
                        if c == 1: split_half_lo(2 * j)
                        if c == 4: split_half_lo(2 * j + 1)
                    if ffn and c not in (0, 3, FC - 1):
                        hlo(j * FC + c, i)

            def row_chunk(q):
                return q % (T // CH)

            V.memset(ones[:, :], 1.0).then_inc(cst, 1)
            V.memset(mhalf[:, :], -0.5).then_inc(cst, 1)
            V.memset(state[:, :, :], 0.0).then_inc(cst, 1)
            V.memset(zeros[:, :], 0.0).then_inc(cst, 1)
            V.memset(b2_row[:, :], 0.0).then_inc(cst, 1)
            V.memset(parts, 0.0).then_inc(cst, 1)
            dve.wait_ge(l_const, 16 * 7)
            V.tensor_tensor(before[:, :], causal, ident, ALU.subtract).then_inc(cst, 1)
            V.tensor_copy(count[:, :], MO["base"]).then_inc(cst, 1)
            V.tensor_copy(ident16[:, :], ident).then_inc(cst, 1)
            dve.wait_ge(cst, 9)
            for n in range(2):
                w = W1C if n == 0 else SMALL - W1C
                dve.wait_ge(small_split, n * 2 + 1)
                split_lo(small_lo[:, n * W1C:n * W1C + w], stage[:, n, 0:w], small_hi[:, n * W1C:n * W1C + w], SCALE)\
                    .then_inc(small_split, 1)
            nb = (E1 + E2) * D
            dve.wait_ge(b2_act, 1)
            split_lo(b2_l, b2_f[:, 0:nb], b2_h, SCALE).then_inc(b2_dve, 1)
            dve.wait_ge(b2_dve, 1)
            V.tensor_scalar(b2_h, b2_h, b2_f[:, nb:nb + 1], None, ALU.mult).then_inc(b2_dve, 1)
            dve.wait_ge(b2_dve, 2)
            V.scalar_tensor_tensor(out=b2_row[0:2, :], in0=b2_l, scalar=b2_f[:, nb + 1:nb + 2], in1=b2_h,
                                   op0=ALU.mult, op1=ALU.add).then_inc(b2_dve, 1)

            front_conv(0, 0, 0, 0)
            front_ylo(0)
            front_x2(0, 0, 0)
            front_phi(0, 0)
            front_phi2(0)
            front_lo(0)
            front_conv(1, 0, 1, 0)
            for j in range(CPB):
                step(-1, -1, j, ffn=False, post=False, w_split=True)
            for j in range(CPB):
                step(0, 0, j, post=False)
            dve.wait_ge(z_done, 16 * E2)
            with dve.Fori(0, (NBLK - 2) // 2) as i:
                for b in (1, 2):
                    for j in range(CPB):
                        step(b, 2 * i + b, j)
            for j in range(CPB):
                step(NBLK - 1, NBLK - 1, j, att=False)
            hlo(E1 * FC - 1, NBLK - 1)
            comb(E1 - 1, NBLK - 1, NBLK - 1)
            for j in range(CPB):
                step(NBLK, NBLK, j, ffn=False, att=False)

            chain = [0]

            def link(ins):
                chain[0] += 1
                ins.then_inc(cnt_chain, 1)
                dve.wait_ge(cnt_chain, chain[0])

            dve.wait_ge(rdve, at(R_DVE, NCH - 1, "pos"))
            link(V.tensor_tensor(cf[:, :], count[:, :], MO["base"], ALU.subtract))
            link(V.tensor_scalar(cf[:, :], cf[:, :], float(TILE - 1), None, ALU.add))
            link(V.tensor_copy(ci[:, :], cf[:, :]))
            link(V.tensor_scalar(ct[:, :], ci[:, :], TILE.bit_length() - 1, None, ALU.arith_shift_right))
            link(V.tensor_copy(ctf[:, :], ct[:, :]))
            link(V.tensor_scalar(tabf[:, 0:E2], ctf[:, :], 1.0, None, ALU.max))
            link(V.memset(cf[:, :], 0.0))
            link(V.tensor_tensor_scan(cum[:, :], tabf[:, 0:E2], cf[:, :], 0.0, ALU.add, ALU.add))
            link(V.tensor_tensor(tabf[:, E2:2 * E2], cum[:, :], tabf[:, 0:E2], ALU.subtract))
            link(V.tensor_copy(tabf[:, 2 * E2:3 * E2], count[:, :]))
            link(V.tensor_copy(tabf[:, 3 * E2:3 * E2 + 1], cum[:, E2 - 1:E2]))
            link(V.tensor_scalar(shift[:, :], tabf[:, E2:2 * E2], float(TILE), None, ALU.mult))
            link(V.tensor_tensor(shift[:, :], shift[:, :], MO["base"], ALU.subtract))
            link(V.memset(move[:, :, :], 0.0))
            for e in range(1, E2):
                link(V.tensor_tensor(cf[:, 0:1], shift[:, e:e + 1], shift[:, e - 1:e], ALU.subtract))
                link(V.tensor_scalar(moved[:, :, :], pos[:, :, :], float(e * CAP), cf[:, 0:1], ALU.is_ge, ALU.mult))
                link(V.tensor_tensor(move[:, :, :], move[:, :, :], moved[:, :, :], ALU.add))
            link(V.tensor_tensor(posy[:, :, :], pos[:, :, :], move[:, :, :], ALU.add))
            dve.wait_ge(rpool, at(R_POOL, NCH - 1, "sent"))
            link(V.memset(zeros[:, :], 0.0))
            V.tensor_copy(tab[:, :], tabf[:, :]).then_inc(tab_ready, 1)

            def tile_lo(g):
                dve.wait_ge(xthi_done, g + 1)
                split_lo(xt_lo[:, :, :], A[0][:, :].rearrange("p (k n) -> p k n", k=KD), xt_hi[:, :, :])\
                    .then_inc(xtlo_done, 1)

            dve.wait_ge(tab_ready, 1)
            tile_lo(0)
            with dve.Fori(0, E2) as e:
                nt = dve.value_load(tab[0:1, bass.ds(e, 1)], min_val=1, max_val=NTOK // TILE)
                tb = dve.value_load(tab[0:1, bass.ds(e + E2, 1)], min_val=0, max_val=MOST)
                with dve.Fori(0, nt) as t:
                    g = dve.snap(tb + t)
                    for c in range(FC):
                        dve.wait_ge(uhi_done, g * FC + c + 1)
                        V.tensor_tensor(u_lo[:, c, :], u32t[:, c % 4, :], u_hi[:, c, :], ALU.subtract).then_inc(ulo_done, 1)
                    tile_lo(g + 1)
                    dve.wait_ge(u2_done, g + 2)
                    dve.wait_ge(y_out, 16 * (g + 1))
                    V.tensor_scalar(ysb[:, :, :], Yb[0][:, :].rearrange("p (s d) -> p s d", s=2), INV, None, ALU.mult)\
                        .then_inc(y_done, 1)

            dve.wait_ge(wexp_done, 1)
            link(V.tensor_scalar(wone[:, :], wexp[:, :], 1.0, None, ALU.add))
            link(V.reciprocal(wt[:, 0, :], wone[:, :]))
            link(V.tensor_tensor(wt[:, 1, :], wt[:, 0, :], wexp[:, :], ALU.mult))

            def sums(i):
                for r in range(NR):
                    n = i * NR + r
                    xr = xall[:, bass.ds(n, 1), :].rearrange("p a d -> p (a d)")
                    dve.wait_ge(l_y[r], 32 * (i + 1))
                    for a in range(2):
                        V.scalar_tensor_tensor(out=xr, in0=rows8[:, r, a, :], scalar=wt[:, a, bass.ds(n, 1)], in1=xr,
                                               op0=ALU.mult, op1=ALU.add).then_inc(sum_done, 1)
                        dve.wait_ge(sum_done, 2 * n + a + 1)
                    V.bn_stats(fbn[:, r, :], xr).then_inc(stat_done, 1)
                for r in range(NR):
                    dve.wait_ge(stat_done, i * 2 * NR + r + 1)
                    V.bn_aggr(fmv[:, r, :], fbn[:, r, :]).then_inc(stat_done, 1)

            def norms(i, g):
                for r in range(NR):
                    n = i * NR + r
                    V.tensor_scalar(fin[:, g, r, :], xall[:, bass.ds(n, 1), :].rearrange("p a d -> p (a d)"),
                                    fmv[:, r, 0:1], frs[:, r:r + 1], ALU.subtract, ALU.mult).then_inc(normed, 1)

            for i in range(NG):
                sums(i)
                dve.wait_ge(frstd, i + 1)
                if i >= 2:
                    dve.wait_ge(fin_out[i % 2], 16 * (i // 2))
                norms(i, i % 2)

        @block.scalar
        def _(act):
            act.sem_inc(ract, len(R_ACT))
            act.sem_inc(y_out, 16)
            S = nc.scalar

            def copy(out_, in_, scale=1.0):
                return S.activation(out_, in_, ACT.Copy, scale=scale)

            def front_yhi(q):
                act.wait_ge(fdve, at(F_DVE, q, "conv2b"))
                copy(y_hi[:, :, :], yT[:, :, :]).then_inc(fact, 1)

            def front_x2(q):
                act.wait_ge(fdve, at(F_DVE, q, "x2"))
                copy(x2_hi[:, :, :], x2T[:, :, 1:CH + 1]).then_inc(fact, 1)
                act.wait_ge(fdve, at(F_DVE, q, "delta"))
                copy(d_hi[:, :, :], dT[:, :, :]).then_inc(fact, 1)

            def front_evac(q):
                act.wait_ge(fpe, at(F_PE, q, "x2t"))
                before_chunk(act, q, (tdve, T_DVE, "x3"))
                copy(vext[:, :, 0:DH], A[2][:, 0:D].rearrange("p (h d) -> p h d", d=DH), INV).then_inc(fact, 1)
                copy(x2tok[:, :], A[0][:, D:2 * D]).then_inc(fact, 1)

            def front_exp(q):
                act.wait_ge(fdve, at(F_DVE, q, "phimin"))
                S.activation(phe[:, :], phm[:, :], ACT.Exp).then_inc(fact, 1)

            def front_gt(q):
                act.wait_ge(fdve, at(F_DVE, q, "gz"))
                S.activation(gt[:, :], gz[:, :], ACT.Tanh, scale=0.5).then_inc(fact, 1)

            def front_hi(q):
                act.wait_ge(fdve, at(F_DVE, q, "phi"))
                for n, to in enumerate((qp[:, :, 0:2, :], kp[:, :, 0:3:2, :])):
                    copy(to, phi[:, n * D:(n + 1) * D].rearrange("p (h d) -> p h d", d=DH).unsqueeze(2)
                         .broadcast_to([P, H, 2, DH])).then_inc(fact, 1)

            def tail_T(q):
                act.wait_ge(tpe, at(T_PE, q, "phit"))
                copy(qS, A[1][:, :].bitcast(F16).rearrange("p (g n) -> p g n", n=CH)).then_inc(tact, 1)
                copy(qTs[:, :, :], A[3][:, 0:D].rearrange("p (k n) -> p k n", k=KD)).then_inc(tact, 1)

            def tail_ahi(q):
                act.wait_ge(tpe, at(T_PE, q, "at"))
                copy(a_hi[:, :, :], A[2][:, 0:D].rearrange("p (k n) -> p k n", k=KD)).then_inc(tact, 1)

            def tail_hhi(q, b, j):
                act.wait_ge(tpe, at(T_PE, q, "ht"))
                copy(hT_hi[:, b % 2, :, j * CH:(j + 1) * CH],
                     A[3][:, D:2 * D].rearrange("p (k n) -> p k n", k=KD)).then_inc(tact, 1)

            def tail_gexp(q):
                act.wait_ge(tdve, at(T_DVE, q, "ngmax"))
                S.activation(ge[:, :], A[3][:, 0:E1], ACT.Exp, bias=gn[:, 0:1], scale=INV, accum_out=gs[:, 0:1])\
                    .then_inc(tact, 1)

            def silu(n, i):
                e, c = n // FC, n % FC
                u = i * E1 * FC + n
                act.wait_ge(g1_done, u + 1)
                if not (isinstance(u, int) and u < 2):
                    act.wait_ge(hlo_done, u - 1)
                S.activation(s32[:, n % 2, :], Hb[n % 2][:, :], ACT.Silu, bias=b1_s[:, e * FC + c:e * FC + c + 1],
                             scale=INV).then_inc(silu_done, 1)
                act.wait_ge(silu_done, u + 1)
                if not (isinstance(u, int) and u < 4):
                    act.wait_ge(g2_done, u - 3)
                copy(h_hi[:, n % 4, :], s32[:, n % 2, :]).then_inc(hhi_done, 1)

            def post_xhi(p):
                act.wait_ge(rpe, at(R_PE, p, "xt"))
                copy(px_hi[:, :, :], A[0][:, 0:D].rearrange("p (k n) -> p k n", k=KD)).then_inc(ract, 1)

            def step(b, i, j, ffn=True, att=True, post=True, w_split=False):
                q = (i + 1) * CPB + j
                for c in range(FC):
                    if att:
                        if c == 0: tail_T(q)
                        if c == 3: tail_ahi(q); front_x2(q + 1)
                        if c == 5: front_evac(q + 1)
                        if c == 6: tail_hhi(q, b + 1, j); front_exp(q + 1); tail_gexp(q); front_gt(q + 1); front_hi(q + 1)
                    if post and c == 3:
                        post_xhi((i - 1) * CPB + j)
                    if ffn and c == 0:
                        if j > 0:
                            silu(j * FC - 1, i)
                        elif not (isinstance(i, int) and i == 0):
                            silu(E1 * FC - 1, i - 1)
                    if ffn and c < FC - 1:
                        silu(j * FC + c, i)
                    if att:
                        if c == 7: front_yhi(q + 2)
                    if w_split:
                        if c == 1: split_half_hi(2 * j)
                        if c == 4: split_half_hi(2 * j + 1)

            def split_half_hi(n):
                act.wait_ge(l_stage[n % 2], 16 * (n // 2 + 2))
                if n == 4:
                    act.wait_ge(b2_dve, 3)
                copy(w_hi[:, n // 2, (n % 2) * W1C:(n % 2 + 1) * W1C], stage[:, n % 2, :], SCALE).then_inc(whi_done, 1)

            for n in range(2):
                w = W1C if n == 0 else SMALL - W1C
                act.wait_ge(l_stage[n], 16)
                if n:
                    act.wait_ge(small_split, 2)
                copy(small_hi[:, n * W1C:n * W1C + w], stage[:, n, 0:w], SCALE).then_inc(small_split, 1)
            act.wait_ge(l_const, 16 * 7)
            copy(b2_h, b2_f[:, 0:(E1 + E2) * D], SCALE).then_inc(b2_act, 1)
            front_yhi(0)
            front_x2(0)
            act.wait_ge(cst, 1)
            copy(vext[:, :, DH:HE], ones[:, 0:H].unsqueeze(2)).then_inc(b2_act, 1)
            front_evac(0)
            front_exp(0)
            front_gt(0)
            front_hi(0)
            front_yhi(1)
            for j in range(CPB):
                step(-1, -1, j, ffn=False, post=False, w_split=True)
            for j in range(CPB):
                step(0, 0, j, post=False)
            with act.Fori(0, (NBLK - 2) // 2) as i:
                for b in (1, 2):
                    for j in range(CPB):
                        step(b, 2 * i + b, j)
            for j in range(CPB):
                step(NBLK - 1, NBLK - 1, j, att=False)
            silu(E1 * FC - 1, NBLK - 1)
            for j in range(CPB):
                step(NBLK, NBLK, j, ffn=False, att=False)

            act.wait_ge(rdve, at(R_DVE, NCH - 1, "dlt"))
            S.activation(wexp[:, :], dlt[:, :], ACT.Exp).then_inc(wexp_done, 1)

            def tile_hi(g):
                act.wait_ge(xt_done, g + 2)
                if not (isinstance(g, int) and g == 0):
                    act.wait_ge(u1_done, g * FC)
                copy(xt_hi[:, :, :], A[0][:, :].rearrange("p (k n) -> p k n", k=KD)).then_inc(xthi_done, 1)

            act.wait_ge(tab_ready, 1)
            tile_hi(0)
            with act.Fori(0, E2) as e:
                nt = act.value_load(tab[0:1, bass.ds(e, 1)], min_val=1, max_val=NTOK // TILE)
                tb = act.value_load(tab[0:1, bass.ds(e + E2, 1)], min_val=0, max_val=MOST)
                with act.Fori(0, nt) as t:
                    g = act.snap(tb + t)
                    for c in range(FC):
                        act.wait_ge(u1_done, g * FC + c + 1)
                        if c >= 4:
                            act.wait_ge(ulo_done, g * FC + c - 2)
                        else:
                            act.wait_ge(ulo_done, g * FC + 1)
                        S.activation(u32t[:, c % 4, :], U[c % 4][:, 0:TILE], ACT.Relu,
                                     bias=b1r_s[:, bass.ds(e * FC + c, 1)], scale=INV).then_inc(relu_done, 1)
                        act.wait_ge(relu_done, g * FC + c + 1)
                        if c == 0:
                            act.wait_ge(u2_done, g + 1)
                        copy(u_hi[:, c, :], u32t[:, c % 4, :]).then_inc(uhi_done, 1)
                    tile_hi(g + 1)
                    act.wait_ge(y_done, g + 2)
                    act.dma_start(yg[bass.ds(g.with_bounds(min_val=0, max_val=MOST - 1) * TILE, TILE), :].rearrange("(s p) d -> p s d", p=P),
                                  ysb[:, :, :]).then_inc(y_out, 16)

        @block.gpsimd
        def _(pool):
            pool.sem_inc(rpool, len(R_POOL))

            G = nc.gpsimd

            def wait(s, value):
                pool.wait_ge(s, value)
                pool.sem_inc(passed, 1)


            def split(src, hi, lo, waits):
                k = 3 * (waits - 2 * E1)
                G.tensor_scalar(src, src, SCALE, 1.0, ALU.mult, ALU.mult).then_inc(wch, 1)
                wait(wch, k + 1)
                G.tensor_copy(hi, src).then_inc(wch, 1)
                wait(wch, k + 2)
                G.tensor_tensor(lo, src, hi, ALU.subtract).then_inc(wch, 1)
                wait(wch, k + 3)
                pool.sem_inc(stage_used, 1)
                pool.sem_inc(w_ready, 1)

            def tail(q, b, j):
                wait(tpe, at(T_PE, q, "av"))
                G.memset(parts[:, 0:2 * NP].rearrange("p (h c d) -> p h c d", c=4, d=DH)[:, :, 3, :], 0.0)\
                    .then_inc(tpool, 1)
                wait(tdve, at(T_DVE, q, "x3"))
                G.tensor_tensor(acc[:, b % 2, j, :], xall[:, bass.ds(q, 1), :].rearrange("p a d -> p (a d)"), x3[:, :],
                                ALU.add).then_inc(tpool, 1)
                wait(tdve, at(T_DVE, q, "aggr"))
                G.tensor_scalar(rstd[:, :], mv[:, 1:2], EPS, 1.0, ALU.add, ALU.mult).then_inc(tpool, 1)
                wait(tpool, at(T_POOL, q, "veps"))
                G.tensor_tensor(rstd[:, :], rstd[:, :], mhalf[:, :], ALU.pow).then_inc(tpool, 1)
                wait(tdve, at(T_DVE, q, "h0"))
                G.tensor_tensor(h0[:, :], h0[:, :], rows_s[:, D:2 * D], ALU.mult).then_inc(tpool, 1)
                wait(tpool, at(T_POOL, q, "hg"))
                G.tensor_tensor(h0[:, :], h0[:, :], rows_s[:, 2 * D:3 * D], ALU.add).then_inc(tpool, 1)

            def post_rstd(p):
                wait(rdve, at(R_DVE, p, "aggr"))
                G.tensor_scalar(prstd[:, :], pmv[:, 1:2], EPS, 1.0, ALU.add, ALU.mult).then_inc(rpool, 1)
                wait(rpool, at(R_POOL, p, "veps"))
                G.tensor_tensor(prstd[:, :], prstd[:, :], mhalf[:, :], ALU.pow).then_inc(rpool, 1)

            def post_keep(p):
                wait(rdve, at(R_DVE, p, "x5"))
                G.tensor_copy(xall[:, bass.ds(p, 1), :].rearrange("p a d -> p (a d)"), px5[:, :]).then_inc(rpool, 1)

            def post_scatter(p):
                wait(rdve, at(R_DVE, p, "idx"))
                for n in range(2):
                    G.indirect_dma_start(xg[:, :], bass.IndirectOffsetOnAxis(idx[:, n:n + 1], 0), px5[:, :], None)\
                        .then_inc(scat, 16)
                wait(scat, 32 * (p + 1))
                pool.sem_inc(rpool, 1)

            def step(b, i, j, ffn=True, att=True, post=True):
                if post:
                    post_rstd((i - 1) * CPB + j)
                    post_keep((i - 1) * CPB + j)
                if att:
                    if j == 0:
                        wait(l_x, 16 * (i + 2))
                    tail((i + 1) * CPB + j, b + 1, j)
                if post:
                    post_scatter((i - 1) * CPB + j)

            def split_half(n):
                wait(l_stage[n % 2], 16 * (n // 2 + 2))
                hi, lo = (w[:, 0, (n % 2) * W1C:(n % 2 + 1) * W1C] for w in (e_hi, e_lo))
                split(stage[:, n % 2, :], hi, lo, n)

            for n in range(2):
                wait(small_split, 2 * (n + 1))
                pool.sem_inc(stage_used, 1)
            wait(cst, 2)
            for j in range(CPB):
                step(-1, -1, j, ffn=False, post=False)
                for n in range(2):
                    wait(w_ready, 2 * j + n + 1)
                    pool.sem_inc(stage_used, 1)
            for j in range(CPB):
                step(0, 0, j, post=False)
            wait(z_done, 16 * E2)
            with pool.Fori(0, (NBLK - 2) // 2) as i:
                for b in (1, 2):
                    for j in range(CPB):
                        step(b, 2 * i + b, j)
            for j in range(CPB):
                step(NBLK - 1, NBLK - 1, j, att=False)
                if j >= 2:
                    wait(g2_done, ((NBLK - 1) * E1 + 1) * FC)
                    split_half(2 * E1 + j - 2)
            for j in range(CPB):
                step(NBLK, NBLK, j, ffn=False, att=False)

            wait(tab_ready, 1)
            with pool.Fori(0, E2 // 2) as ep:
                for s in range(2):
                    e = 2 * ep + s
                    tb = pool.value_load(tab[0:1, bass.ds(e + E2, 1)], min_val=0, max_val=MOST)
                    wait(u2_done, tb + 1)
                    if s == 0:
                        wait(g2_done, NBLK * E1 * FC)
                    for n in range(2):
                        wait(l_stage[n], 16 * (E1 + 3 + e))
                        split(stage[:, n, :], *(w[:, 1 - s, n * W1C:(n + 1) * W1C] for w in (e_hi, e_lo)),
                              2 * E1 + 2 + 2 * e + n)

            ng = pool.value_load(tab[0:1, 3 * E2:3 * E2 + 1], min_val=1, max_val=MOST)
            wait(y_out, 16 * (ng + 1))
            G.memset(mhalf8, -0.5).then_inc(feps, 1)
            for i in range(NG):
                if i:
                    for r in range(NR):
                        wait(l_y[r], 32 * i)
                G.tensor_copy(idx8[:, :, :], posy[:, i * NR:(i + 1) * NR, :]).then_inc(idx8_done, 1)
                wait(idx8_done, i + 1)
                for r in range(NR):
                    if i:
                        wait(sum_done, 2 * ((i - 1) * NR + r + 1))
                    for n in range(2):
                        G.indirect_dma_start(rows8[:, r, n, :], None, yg[0:MOST * TILE, :],
                                             bass.IndirectOffsetOnAxis(idx8[:, r, n:n + 1], 0)).then_inc(l_y[r], 16)
                wait(stat_done, 2 * NR * (i + 1))
                G.tensor_scalar(fve[:, :], fmv[:, :, 1], EPS, 1.0, ALU.add, ALU.mult).then_inc(feps, 1)
                wait(feps, i + 2)
                G.tensor_tensor(frs[:, :], fve[:, :], mhalf8[:, :], ALU.pow).then_inc(frstd, 1)


def _layout(a):
    f = {k: np.ascontiguousarray(np.asarray(v)) for k, v in a.items()}
    part = lambda m: m.reshape(KD, P, -1).transpose(1, 0, 2).reshape(P, -1)
    at, ff = "L0_attn_", "L0_ffn_"
    x = f[at + "x"]
    xpad = np.concatenate([np.zeros((B, 2, D), x.dtype), x], axis=1)
    xT = np.ascontiguousarray(xpad.transpose(2, 0, 1).reshape(KD, P, B, T + 2).transpose(1, 0, 2, 3))
    small = np.concatenate([part(f[at + n].T) for n in ("w_pw", "w_qkv", "w_o", "w_gate", "w_moe_gate")]
                           + [part(f[ff + "W_router"])], axis=1)
    wdw = f[at + "w_dw"].reshape(KD, P, 3).transpose(1, 0, 2).reshape(P, -1)
    rows = np.concatenate([f[at + "b_gate"], f[at + "ln_g"], f[at + "ln_b"], f[ff + "b_router"]])
    moe1 = np.concatenate([np.concatenate([part(f[at + "w1"][e].T),
                                           f[at + "w2"][e].T.reshape(FC, P, D).transpose(1, 0, 2).reshape(P, -1)], axis=1)
                           for e in range(E1)], axis=1)
    moe1_b = f[at + "b1"].reshape(E1 * FC, P).T
    moe2 = np.stack([np.concatenate([part(f[ff + "W1"][e]),
                                     f[ff + "W2"][e].reshape(FC, P, D).transpose(1, 0, 2).reshape(P, -1)], axis=1)
                     for e in range(E2)])
    moe2_b = f[ff + "b1"].reshape(E2 * FC, P).T
    b2 = np.concatenate([f[at + "b2"].reshape(-1), f[ff + "b2"].reshape(-1)])
    b2rows = np.concatenate([np.stack([b2, b2]), np.eye(2, dtype=np.float32)], axis=1)
    inv_freq = (1.0 / np.float32(10000.0) ** (np.arange(0, DH, 2, dtype=np.float32) / np.float32(DH))).astype(np.float32)
    theta = np.arange(T, dtype=np.float32)[:, None] * inv_freq[None, :]
    cos, sin = np.cos(theta), np.sin(theta)
    rope = np.stack([np.repeat(cos, 2, axis=1), np.stack([-sin, sin], axis=-1).reshape(T, DH)], axis=1) * INV
    rope = rope.astype(np.float32).reshape(T // P, P, 2, DH).transpose(1, 0, 2, 3)
    p = np.arange(P)
    chunks = np.arange(NCH + 1)
    keep = (chunks % (T // CH) != 0).astype(np.float32)
    masks = np.concatenate([
        np.eye(P), p[:, None] <= p[None, :], (p[:, None] // DH) == (np.arange(H // 2 * HE)[None, :] // HE),
        (p[:, None] // DH) % 2 == 0, (p[:, None] // DH) % 2 == 1,
        np.tile(keep, (P, 1)), np.tile(1 - keep, (P, 1)), np.tile(np.arange(E2), (P, 1)),
        np.tile(np.arange(E2) * CAP, (P, 1))], axis=1).astype(np.float32)
    arrays = dict(x=x.reshape(NTOK, D), xT=xT, small=small, wdw=wdw, rows=rows, moe1=moe1, moe1_b=moe1_b, moe2=moe2,
                  moe2_b=moe2_b, b2rows=b2rows, rope=rope, masks=masks)
    return {k: np.ascontiguousarray(v) for k, v in arrays.items()}


def kernel(**inputs):
    import concourse.bacc as bacc
    from concourse.bass_utils import run_bass_kernel_spmd

    nc = bacc.Bacc("TRN2", target_bir_lowering=False, num_devices=1)
    arrays = _layout(inputs)
    args = {k: nc.dram_tensor("in_" + k, a.shape, mybir.dt.from_np(a.dtype), kind="ExternalInput").ap()
            for k, a in arrays.items()}
    out = nc.dram_tensor("out_0", (NTOK, D), F32, kind="ExternalOutput").ap()
    build(nc, out=out, **args)
    r = run_bass_kernel_spmd(nc, [{"in_" + k: a for k, a in arrays.items()}], core_ids=[0])
    return r.results[0]["out_0"].reshape(B, T, D)
```

```python
from contextlib import ExitStack

import numpy as np

import concourse.bass as bass
from concourse import mybir

ALU = mybir.AluOpType
ACT = mybir.ActivationFunctionType
AX = mybir.AxisListType
F32 = mybir.dt.float32
F16 = mybir.dt.float16
U32 = mybir.dt.uint32
I32 = mybir.dt.int32

P = 128
B, T, D = 2, 2048, 256
NTOK = B * T
KD = D // P
CH = P
NCH = NTOK // CH
BLK = 512
CPB = BLK // CH
NBLK = NTOK // BLK
BPB = T // BLK
H, DH = 16, 16
NP = 4 * H * DH
HE = DH + 1
E1, FF = 4, 1024
FC = FF // P
E2 = 8
W1C, W2C = KD * FF, FC * D
WC = W1C + W2C
TILE = 256
CAP = NTOK + 2 * TILE
LEAST = 2 * NTOK // TILE
MOST = LEAST + E2
SCALE = 256.0
INV = 1.0 / SCALE
NR = 8
GROUPS = [(n, min(n + NR, NCH)) for n in range(0, NCH - NR, NR)] + [(NCH - NR, NCH - 3), (NCH - 3, NCH)]
EPS = 1e-5

PW, QKV, WO, WG, MG, RT = 0, 512, 2048, 2560, 3072, 3080
SMALL = 3096

F_DVE = ["conv0a", "conv0b", "conv1a", "conv1b", "conv2a", "conv2b", "ylo", "halo", "x2", "first",
         "delta", "x2lo", "dlo", "rot_cos", "rot_sin_a", "rot_sin_b", "rot", "phimin", "gz", "phi",
         "qlo", "klo"]
F_ACT = ["yhi", "x2hi", "dhi", "vext", "x2tok", "phiexp", "gt", "qhi", "khi"]
F_PE = ["pw", "qk", "v", "gate", "x2t"]
T_DVE = ["kS", "keep", "mask0", "mask2", "mask1", "mask3", "den", "rden", "attn", "kvt",
         "kvadd", "alo", "g2", "x3", "bn", "aggr", "h0", "hlo", "gmax", "ngmax", "rsum", "gw"]
T_ACT = ["qS", "qT", "ahi", "hhi", "gexp"]
T_PE = ["phit", "score", "av", "kv", "at", "wo", "ht", "lg"]
T_POOL = ["clear", "xres", "veps", "rstd", "hg", "hb"]
R_DVE = ["bn", "aggr", "x5", "xlo", "lg", "top", "dlt", "topi", "m1", "m2", "m12", "rank", "p1", "p2",
         "cnt", "idx", "pos"]
R_ACT = ["xhi"]
R_PE = ["xt", "rl", "rk"]
R_POOL = ["veps", "rstd", "keepx", "sent"]

L_DVE = ["bn", "aggr", "x5", "xlo0", "xlo1", "lg", "top", "dlt", "topi", "m", "m12", "rank", "pos4", "cnt", "idx", "pos"]
L_ACT = ["xhi0", "xhi1"]
L_PE = ["xt", "rl", "rk"]
L_POOL = ["veps", "rstd"]


def build(nc, x, xT, small, wdw, rows, moe1, moe1_b, moe2, moe2_b, b2rows, rope, masks, out):
    nc.disable_value_cache = True
    with ExitStack() as ctx:
        def sb(name, shape, dt=F32):
            return ctx.enter_context(nc.sbuf_tensor(name, shape, dt))

        def ps(name):
            return ctx.enter_context(nc.psum_tensor(name, [P, 512], F32))

        def sem(name):
            return ctx.enter_context(nc.semaphore(name))

        xg = nc.dram_tensor("expert_rows", [E2 * CAP, D], F32, kind="Internal")
        yg = nc.dram_tensor("expert_out", [(MOST + E2) * TILE, D], F32, kind="Internal")

        stage = sb("stage", [P, 2, W1C])
        small_hi, small_lo = sb("small_hi", [P, SMALL], F16), sb("small_lo", [P, SMALL], F16)
        w_hi, w_lo = sb("w_hi", [P, E1, WC], F16), sb("w_lo", [P, E1, WC], F16)
        wdw_s = sb("wdw_s", [P, KD * 3])
        rows_s = sb("rows_s", [P, 3 * D + E2])
        b1_s = sb("b1_s", [P, E1 * FC])
        b1r_s = sb("b1r_s", [P, E2 * FC])
        nb2 = (E1 + E2) * D
        e_hi, e_lo = w_hi[:, 0:2, :], w_lo[:, 0:2, :]
        b2_f = w_hi[0:2, 2:4, :].rearrange("p s c -> p (s c)").bitcast(F32)[:, 0:nb2 + 2]
        b2_h = w_lo[0:2, 2:4, :].rearrange("p s c -> p (s c)")[:, 0:nb2]
        b2_l = w_lo[0:2, 2:4, :].rearrange("p s c -> p (s c)")[:, nb2:2 * nb2]
        b2_row = sb("b2_row", [P, (E1 + E2) * D], F16)
        rope_s = sb("rope_s", [P, T // CH, 2, DH])
        masks_s = sb("masks_s", [P, masks.shape[1]])
        MO = {}
        o = 0
        for name, n in (("ident", P), ("causal", P), ("block", H // 2 * HE),
                        ("keep", NCH + 1), ("new", NCH + 1), ("iota8", E2), ("base", E2)):
            MO[name] = masks_s[:, o:o + n]
            o += n
        ident, causal = MO["ident"], MO["causal"]
        ident16 = sb("ident16", [P, P], F16)
        before = sb("before", [P, P], F16)
        ones = sb("ones", [P, P], F16)
        mhalves = sb("mhalves", [P, NR])
        mhalf = mhalves[:, 0:1]
        px5 = sb("px5", [P, D])
        zeros = px5

        xall = sb("xall", [P, NCH, D])
        xTb = sb("xTb", [P, 2, KD, BLK + 2])
        yT = sb("yT", [P, KD, CH])
        y_hi, y_lo = sb("y_hi", [P, KD, CH], F16), sb("y_lo", [P, KD, CH], F16)
        x2T = sb("x2T", [P, KD, CH + 1])
        x2_hi, x2_lo = sb("x2_hi", [P, KD, CH], F16), sb("x2_lo", [P, KD, CH], F16)
        dT, d_hi, d_lo = yT, y_hi, y_lo
        vext = sb("vext", [P, H, HE])
        x2tok = sb("x2tok", [P, D])
        gz, gt = sb("gz", [P, D]), sb("gt", [P, D])
        r1, r2, rq = sb("r1", [P, 2 * D]), sb("r2", [P, 2 * D]), sb("rq", [P, 2 * D])
        phm, phe = r1, r2
        phi = sb("phi", [P, 2 * D])
        qTs = r2[:, D:2 * D].rearrange("p (k n) -> p k n", k=KD)
        sm = sb("sm", [P, 4, 4, CH])
        parts = sm[:, :, :, :].rearrange("p a b n -> p (a b n)").bitcast(F16)
        qp, kp = (parts[:, n * NP:(n + 1) * NP].rearrange("p (h c d) -> p h c d", c=4, d=DH) for n in range(2))
        qS, kS = (parts[:, n * NP:(n + 1) * NP].rearrange("p (g n) -> p g n", n=CH) for n in (2, 3))
        state, kvt = sb("state", [P, KD, H // 2 * HE]), sb("kvt", [P, KD, H // 2 * HE])
        den, rden = sb("den", [P, H]), sb("rden", [P, H])
        attn = rq[:, 0:D]
        g2, x3 = gz, sb("x3", [P, D])
        bn, mv, rstd = sb("bn", [P, 6]), sb("mv", [P, 2]), sb("rstd", [P, 1])
        h0 = sb("h0", [P, D])
        a_hi, a_lo = (h0[:, n * P:(n + 1) * P].bitcast(F16).rearrange("p (k n) -> p k n", k=KD) for n in range(2))
        hT_hi, hT_lo = sb("hT_hi", [P, 2, KD, BLK], F16), sb("hT_lo", [P, 2, KD, BLK], F16)
        gm, gn, ge, gs, gr = sb("gm", [P, 1]), sb("gn", [P, 1]), sb("ge", [P, E1]), sb("gs", [P, 1]), sb("gr", [P, 1])
        gw = sb("gw", [P, 2, CPB, E1])
        acc = sb("acc", [P, 2, CPB, D])
        s32 = sb("s32", [P, 2, BLK])
        h_hi, h_lo = sb("h_hi", [P, 4, BLK], F16), sb("h_lo", [P, 4, BLK], F16)
        pbn, pmv, prstd = sb("pbn", [P, 6]), sb("pmv", [P, 2]), sb("prstd", [P, 1])
        px_hi, px_lo = sb("px_hi", [P, KD, CH], F16), sb("px_lo", [P, KD, CH], F16)
        plg = sb("plg", [P, E2])
        top8 = sb("top8", [P, 8])
        topi = sb("topi", [P, 8], U32)
        m1, m2, m12 = sb("m1", [P, E2]), sb("m2", [P, E2]), sb("m12", [P, E2], F16)
        rank = sb("rank", [P, E2])
        count = sb("count", [P, E2])
        junk = sb("junk", [P, 2, E2])
        posf, pos = sb("posf", [P, 2]), sb("pos", [P, NCH, 2])
        idx = sb("idx", [P, 2], U32)
        cf, ci, ct = sb("cf", [P, E2]), sb("ci", [P, E2], I32), sb("ct", [P, E2], I32)
        ctf, cum = sb("ctf", [P, E2]), sb("cum", [P, E2])
        tabf = sb("tabf", [P, 3 * E2 + 1])
        tab = sb("tab", [P, 3 * E2 + 1], I32)
        p_last = NCH - CPB
        o4 = [0]

        def cut4(n):
            o4[0] += CPB * n
            return r1[:, o4[0] - CPB * n:o4[0]].rearrange("p (j n) -> p j n", n=n)

        bn4, mv4, rstd4, lg4, top4, topi4 = cut4(6), cut4(2), cut4(1), cut4(E2), cut4(8), cut4(8).bitcast(U32)
        m4, rank4, junk4, pos4, idx4 = [cut4(E2), cut4(E2)], cut4(E2), [cut4(E2), cut4(E2)], cut4(2), cut4(2).bitcast(U32)
        m12_4 = cut4(E2 // 2).bitcast(F16)
        xhi4, xlo4 = (parts[:, n * CPB * D:(n + 1) * CPB * D].rearrange("p (j k n) -> p j k n", j=CPB, k=KD)
                      for n in range(2))
        xin, ysb = acc[:, 0, 0:2, :], acc[:, 1, 0:2, :]
        xt_hi, xt_lo = hT_hi[:, 0, :, 0:TILE], hT_lo[:, 0, :, 0:TILE]
        u32t = s32[:, :, :].rearrange("p a (b n) -> p (a b) n", n=TILE)
        u_hi, u_lo = (t[:, :, :].rearrange("p a (b n) -> p (a b) n", n=TILE) for t in (h_hi, h_lo))
        shift = junk[:, 0, :]
        move, moved = (g2[:, n * 2 * NCH:(n + 1) * 2 * NCH].rearrange("p (c a) -> p c a", a=2) for n in range(2))
        posy = g2[:, 4 * NCH:6 * NCH].rearrange("p (c a) -> p c a", a=2).bitcast(U32)
        dlt, wexp, wone = sb("dlt", [P, NCH]), *(kvt[:, 1, n * NCH:(n + 1) * NCH] for n in range(2))
        wt = sb("wt", [P, 2, NCH])
        rows8 = w_hi[:, :, :].rearrange("p e c -> p (e c)").bitcast(F32)[:, 0:NR * 2 * D]\
            .rearrange("p (r n d) -> p r n d", r=NR, n=2)
        fin = w_lo[:, :, :].rearrange("p e c -> p (e c)").bitcast(F32)[:, 0:2 * NR * D]\
            .rearrange("p (g r d) -> p g r d", g=2, r=NR)
        fbn, fmv = sb("fbn", [P, NR, 6]), sb("fmv", [P, 2, NR, 2])
        frs = sb("frs", [P, 2, NR])

        A = [ps(f"A{i}") for i in range(4)]
        Hb = [ps(f"H{i}") for i in range(2)]
        Yb = [ps(f"Y{i}") for i in range(2)]
        U = [A[1], A[2], A[3], Hb[0]]


        l_const, l_x, l_xT = sem("l_const"), sem("l_x"), sem("l_xT")
        l_stage = [sem(f"l_stage{i}") for i in range(2)]
        whi_done = sem("whi_done")
        passed = sem("passed")
        stage_used = sem("stage_used")
        small_split = sem("small_split")
        wch = sem("wch")
        w_ready = sem("w_ready")
        cst = sem("cst")
        b2_act, b2_dve = sem("b2_act"), sem("b2_dve")
        fdve, fact, fpe = sem("fdve"), sem("fact"), sem("fpe")
        tdve, tact, tpe, tpool = sem("tdve"), sem("tact"), sem("tpe"), sem("tpool")
        rdve, ract, rpe, rpool = sem("rdve"), sem("ract"), sem("rpe"), sem("rpool")
        g1_done, silu_done, hhi_done, hlo_done, g2_done, comb_done = (
            sem(n) for n in ("g1_done", "silu_done", "hhi_done", "hlo_done", "g2_done", "comb_done"))
        ldve, lact, lpe, lpool = sem("ldve"), sem("lact"), sem("lpe"), sem("lpool")
        z_done, scat, tail_done = sem("z_done"), sem("scat"), sem("tail_done")
        cnt_chain, tab_ready = sem("cnt_chain"), sem("tab_ready")
        l_xin, xt_done, xthi_done, xtlo_done = sem("l_xin"), sem("xt_done"), sem("xthi_done"), sem("xtlo_done")
        u1_done, relu_done, uhi_done, ulo_done, u2_done, y_done, y_out = (
            sem(n) for n in ("u1_done", "relu_done", "uhi_done", "ulo_done", "u2_done", "y_done", "y_out"))
        wexp_done = sem("wexp_done")
        l_y = [sem(f"l_y{i}") for i in range(NR)]
        sum_done, stat_done, feps, frstd, normed = (
            sem(n) for n in ("sum_done", "stat_done", "feps", "frstd", "normed"))
        fin_out = [sem(f"fin_out{n}") for n in range(2)]

        def at(steps, q, name):
            if steps in (R_DVE, R_ACT, R_PE, R_POOL):
                q = q + 1
            return q * len(steps) + (steps.index(name) + 1)

        def last(steps, name):
            return steps.index(name) + 1

        def before_chunk(eng, q, *waits, wait=None):
            for s, steps, name in waits:
                if not (isinstance(q, int) and q == 0):
                    wait(s, at(steps, q - 1, name)) if wait else eng.wait_ge(s, at(steps, q - 1, name))

        def cols(w, off, n):
            return w[:, off:off + KD * n].rearrange("p (k n) -> p k n", k=KD)

        block = ctx.enter_context(nc.Block())

        @block.sync
        def _(sp):
            for dst, src in ((masks_s[:, :], masks), (wdw_s[:, :], wdw), (rows_s[:, :], rows.partition_broadcast(P)),
                             (b1_s[:, :], moe1_b), (b1r_s[:, :], moe2_b), (b2_f, b2rows),
                             (rope_s[:, :, :, :], rope)):
                sp.dma_start(dst, src).then_inc(l_const, 16)
            for n in range(2):
                w = W1C if n == 0 else SMALL - W1C
                sp.dma_start(stage[:, n, 0:w], small[:, n * W1C:n * W1C + w]).then_inc(l_stage[n], 16)

            def load_xT(n):
                nb = n if n < NBLK else 0
                sp.dma_start(xTb[:, n % 2, :, :], xT[:, :, nb // BPB, (nb % BPB) * BLK:(nb % BPB) * BLK + BLK + 2])\
                  .then_inc(l_xT, 16)
                sp.wait_ge(l_xT, 16 * (n + 1))

            def load_x(n):
                sp.dma_start(xall[:, n * CPB:(n + 1) * CPB, :],
                             x[n * BLK:(n + 1) * BLK, :].rearrange("(c p) d -> p c d", p=P)).then_inc(l_x, 16)
                sp.wait_ge(l_x, 16 * (n + 1))

            load_xT(0)
            load_x(0)
            load_xT(1)
            for n in range(2 * E1):
                sp.wait_ge(stage_used, n + 1)
                sp.dma_start(stage[:, n % 2, :], moe1[:, n * W1C:(n + 1) * W1C]).then_inc(l_stage[n % 2], 16)
                if n < NBLK - 1:
                    load_x(n + 1)
            sp.wait_ge(cst, 4)
            for e in range(E2):
                sp.dma_start(xg[e * CAP:e * CAP + TILE, :].rearrange("(s p) d -> p s d", p=P),
                             zeros[:, :].unsqueeze(1).broadcast_to([P, TILE // P, D])).then_inc(z_done, 16)
            for n in range(2):
                sp.wait_ge(stage_used, 2 * E1 + n + 1)
                sp.dma_start(stage[:, n % 2, :], moe2[0, :, n * W1C:(n + 1) * W1C]).then_inc(l_stage[n % 2], 16)
            for n in range(2, NBLK + 1):
                sp.wait_ge(fdve, at(F_DVE, CPB * (n - 2) + CPB - 1, "x2"))
                load_xT(n)
            def load_expert(e, order):
                for n in range(2):
                    sp.wait_ge(stage_used, 2 * E1 + 2 * order + n + 1)
                    sp.dma_start(stage[:, n, :], moe2[bass.ds(e, 1), :, n * W1C:(n + 1) * W1C]
                                 .rearrange("a p c -> p (a c)")).then_inc(l_stage[n], 16)

            def end_list(e):
                first = sp.value_load(tab[0:1, bass.ds(2 * E2 + e, 1)], min_val=0, max_val=E2 * CAP - TILE)
                sp.dma_start(xg[bass.ds(first, TILE), :].rearrange("(s p) d -> p s d", p=P),
                             zeros[:, :].unsqueeze(1).broadcast_to([P, TILE // P, D])).then_inc(tail_done, 16)

            load_expert(1, 1)
            sp.wait_ge(tab_ready, 1)
            sp.wait_ge(z_done, 16 * E2)
            end_list(0)
            sp.wait_ge(scat, 32 * NCH)

            def expert(e, more):
                nt = sp.value_load(tab[0:1, bass.ds(e, 1)], min_val=1, max_val=NTOK // TILE)
                tb = sp.value_load(tab[0:1, bass.ds(e + E2, 1)], min_val=0, max_val=MOST)
                sp.wait_ge(tail_done, 16 * (e + 1))
                if more:
                    end_list(e + 1)
                with sp.Fori(0, nt) as t:
                    sp.wait_ge(xt_done, tb + t + 1)
                    sp.dma_start(xin[:, :, :], xg[bass.ds(e * CAP + t * TILE, TILE), :]
                                 .rearrange("(s p) d -> p s d", p=P)).then_inc(l_xin, 16)
                if more:
                    load_expert((e + 2) % E2, e + 2)

            with sp.Fori(0, E2 - 1) as e:
                expert(e, True)
            expert(E2 - 1, False)
            ng = sp.value_load(tab[0:1, 3 * E2:3 * E2 + 1], min_val=LEAST, max_val=MOST)
            sp.dma_start(yg[bass.ds(ng * TILE, E2 * TILE), :].rearrange("(s p) d -> p s d", p=P),
                         zeros[:, :].unsqueeze(1).broadcast_to([P, E2 * TILE // P, D])).then_inc(tail_done, 16)
            sp.wait_ge(xt_done, ng + 1)
            sp.dma_start(xin[:, :, :], xg[0:TILE, :].rearrange("(s p) d -> p s d", p=P)).then_inc(l_xin, 16)
            for i, (first, end) in enumerate(GROUPS):
                sp.wait_ge(normed, end)
                sp.dma_start(out[first * P:end * P, :].rearrange("(r p) d -> p r d", p=P), fin[:, i % 2, 0:end - first, :])\
                  .then_inc(fin_out[i % 2], 16)
            for n in range(2):
                sp.wait_ge(fin_out[n], 16 * len(GROUPS[n::2]))

        @block.tensor
        def _(pe):
            pe.sem_inc(rpe, len(R_PE))
            pe.sem_inc(xt_done, 1)
            pe.sem_inc(u2_done, 1)
            mm = nc.tensor.matmul

            def three(outp, wl, xl, first=True, last=True):
                n = len(wl[0])
                for k in range(n):
                    for i, (a, b) in enumerate(((0, 0), (0, 1), (1, 0))):
                        ins = mm(outp, wl[a][k], xl[b][k], start=first and k == 0 and i == 0,
                                 stop=last and k == n - 1 and i == 2, skip_group_check=True)
                return ins

            def ks(t, off=0, n=None):
                return [t[:, k, off:off + n] if n else t[:, k, :] for k in range(KD)]

            def front_pw(q):
                pe.wait_ge(fdve, at(F_DVE, q, "ylo"))
                before_chunk(pe, q, (tdve, T_DVE, "kvt"))
                for eh in range(KD):
                    ins = three(A[1][:, eh * P:(eh + 1) * P],
                                [ks(cols(small_hi, PW, D), eh * P, P), ks(cols(small_lo, PW, D), eh * P, P)],
                                [ks(y_hi), ks(y_lo)])
                ins.then_inc(fpe, 1)

            def front_qkv(q):
                pe.wait_ge(fdve, at(F_DVE, q, "dlo"))
                w = [[t[:, QKV + k * 768:QKV + k * 768 + 512] for k in range(KD)] for t in (small_hi, small_lo)]
                wv = [[t[:, QKV + k * 768 + 512:QKV + (k + 1) * 768] for k in range(KD)] for t in (small_hi, small_lo)]
                three(A[1][:, :], [ks(x2_hi), ks(x2_lo)], w).then_inc(fpe, 1)
                three(A[2][:, 0:D], [ks(x2_hi), ks(x2_lo)], wv).then_inc(fpe, 1)
                three(A[2][:, D:2 * D], [ks(d_hi), ks(d_lo)],
                      [ks(cols(small_hi, WG, D)), ks(cols(small_lo, WG, D))]).then_inc(fpe, 1)
                if not (isinstance(q, int) and q <= 8):
                    pe.wait_ge(rdve, at(R_DVE, q - 9, "cnt"))
                for k in range(KD):
                    ins = nc.tensor.transpose(A[0][:, D + k * P:D + (k + 1) * P], x2T[:, k, 1:CH + 1], ident)
                ins.then_inc(fpe, 1)

            def phit(q):
                before_chunk(pe, q, (tact, T_ACT, "gexp"), (tpool, T_POOL, "clear"))
                pe.wait_ge(fdve, at(F_DVE, q, "klo"))
                for src, bank in ((parts[:, 0:NP], A[1]), (parts[:, NP:2 * NP], A[2])):
                    for g in range(H // 2):
                        nc.tensor.transpose(bank[:, :].bitcast(F16)[:, g * P:(g + 1) * P], src[:, g * P:(g + 1) * P],
                                            ident16[:, :])
                for n in range(KD):
                    ins = nc.tensor.transpose(A[3][:, n * P:(n + 1) * P], phi[:, n * P:(n + 1) * P], ident)
                ins.then_inc(tpe, 1)

            def score(q):
                pe.wait_ge(tact, at(T_ACT, q, "qT"))
                pe.wait_ge(tdve, at(T_DVE, q, "kS"))
                for h in range(H):
                    bank, o, r = (h % 2) * 2 + h // 8, (h % 8) // 2 * CH, (h % 2) * 64
                    ins = mm(A[bank][:, o:o + CH], kS[r:r + 3 * DH, h // 2, :], qS[r:r + 3 * DH, h // 2, :],
                             start=True, stop=True, skip_group_check=True)
                ins.then_inc(tpe, 1)

            def av(q, between):
                for half in range(KD):
                    pe.wait_ge(tdve, at(T_DVE, q, f"mask{half + 2}"))
                    o = half * H // 2 * HE
                    mm(A[0][:, o:o + H // 2 * HE], qTs[:, half, :], state[:, half, :],
                       start=half == 0, stop=False, skip_group_check=True)
                    for h8 in range(H // 2):
                        if between and h8 in (1, 4, 7):
                            next(between)
                        ins = mm(A[0][:, o + h8 * HE:o + (h8 + 1) * HE], sm[:, (h8 % 2) * 2 + half, h8 // 2, :],
                                 vext[:, half * H // 2 + h8, :], start=False, stop=True, skip_group_check=True)
                ins.then_inc(tpe, 1)
                for half in range(KD):
                    ins = mm(A[1][:, half * H // 2 * HE:(half + 1) * H // 2 * HE], phi[:, D + half * P:D + (half + 1) * P],
                             vext[:, half * H // 2:(half + 1) * H // 2, :], start=True, stop=True, skip_group_check=True)
                ins.then_inc(tpe, 1)

            def at_(q):
                pe.wait_ge(tdve, at(T_DVE, q, "attn"))
                for k in range(KD):
                    ins = nc.tensor.transpose(A[2][:, k * P:(k + 1) * P], attn[:, k * P:(k + 1) * P], ident)
                ins.then_inc(tpe, 1)

            def wo(q):
                pe.wait_ge(tdve, at(T_DVE, q, "alo"))
                three(A[3][:, 0:D], [ks(a_hi), ks(a_lo)],
                      [ks(cols(small_hi, WO, D)), ks(cols(small_lo, WO, D))]).then_inc(tpe, 1)

            def ht(q):
                pe.wait_ge(tpool, at(T_POOL, q, "hb"))
                for k in range(KD):
                    ins = nc.tensor.transpose(A[3][:, D + k * P:D + (k + 1) * P], h0[:, k * P:(k + 1) * P], ident)
                ins.then_inc(tpe, 1)

            def lg(q, b, j):
                pe.wait_ge(tdve, at(T_DVE, q, "hlo"))
                s = b % 2
                three(A[3][:, 0:E1], [[t[:, s, k, j * P:(j + 1) * P] for k in range(KD)] for t in (hT_hi, hT_lo)],
                      [ks(cols(small_hi, MG, E1)), ks(cols(small_lo, MG, E1))]).then_inc(tpe, 1)

            def g1(b, n, i):
                e, c, s = n // FC, n % FC, b % 2
                u = i * E1 * FC + n
                if n == 0:
                    pe.wait_ge(tdve, at(T_DVE, i * CPB + CPB - 1, "hlo"))
                if b == 0 and c == 0:
                    pe.wait_ge(w_ready, 2 * (e + 1))
                if not (isinstance(u, int) and u < 2):
                    pe.wait_ge(silu_done, u - 1)
                ws = [[t[:, e, k * FF + c * P:k * FF + (c + 1) * P] for k in range(KD)] for t in (w_hi, w_lo)]
                xs = [ks(hT_hi[:, s]), ks(hT_lo[:, s])]
                for k in range(KD):
                    for m, (wl, xl) in enumerate(((0, 0), (0, 1), (1, 0))):
                        ins = mm(Hb[n % 2][:, :], ws[wl][k], xs[xl][k], start=k == 0 and m == 0,
                                 stop=k == KD - 1 and m == 2, skip_group_check=True)
                        if k == KD - 1 and m == 2:
                            ins.then_inc(g1_done, 1)
                        yield

            def g2_(n, i):
                e, c, s = n // FC, n % FC, n % 4
                u = i * E1 * FC + n
                pe.wait_ge(hlo_done, u + 1)
                if c == 0:
                    pe.wait_ge(b2_dve, 3)
                    if not (isinstance(u, int) and u == 0):
                        pe.wait_ge(comb_done, (i * E1 + e) * CPB)
                    for t in range(CPB):
                        mm(Yb[t // 2][:, (t % 2) * D:(t % 2 + 1) * D], ones[:, :], b2_row[:, e * D:(e + 1) * D],
                           start=t % 2 == 0, stop=False, skip_group_check=True)
                for t in range(CPB):
                    w = [t2[:, e, W1C + c * D:W1C + (c + 1) * D] for t2 in (w_hi, w_lo)]
                    ins = three(Yb[t // 2][:, (t % 2) * D:(t % 2 + 1) * D],
                                [[h_hi[:, s, t * P:(t + 1) * P]], [h_lo[:, s, t * P:(t + 1) * P]]],
                                [[w[0]], [w[1]]], first=False, last=c == FC - 1)
                ins.then_inc(g2_done, 1)

            def post_xt(p):
                pe.wait_ge(rdve, at(R_DVE, p, "x5"))
                for k in range(KD):
                    ins = nc.tensor.transpose(A[0][:, k * P:(k + 1) * P], px5[:, k * P:(k + 1) * P], ident)
                ins.then_inc(rpe, 1)

            def post_rl(p):
                pe.wait_ge(rdve, at(R_DVE, p, "xlo"))
                three(A[0][:, D:D + E2], [ks(px_hi), ks(px_lo)],
                      [ks(cols(small_hi, RT, E2)), ks(cols(small_lo, RT, E2))]).then_inc(rpe, 1)

            def post_rk(p):
                pe.wait_ge(rdve, at(R_DVE, p, "m12"))
                mm(A[0][:, 2 * D - 2 * E2:2 * D - E2], before[:, :], m12[:, :], start=True, stop=True, skip_group_check=True)
                mm(A[0][:, 2 * D - E2:2 * D], ones[:, :], m12[:, :], start=True, stop=True, skip_group_check=True)\
                    .then_inc(rpe, 1)

            def step(b, i, j, ffn=True, att=True, post=True):
                q = (i + 1) * CPB + j
                p = (i - 1) * CPB + j
                for c in range(FC):
                    if att:
                        if c == 0: phit(q)
                        if c == 1: score(q)
                        if c == 2: av(q, g1(b, j * FC + c, i) if ffn else None)
                        if c == 3: at_(q); front_pw(q + 1)
                    if post:
                        if c == 3: post_xt(p)
                        if c == 4: post_rl(p)
                        if c == 5: post_rk(p)
                    if att:
                        if c == 5: front_qkv(q + 1)
                    if ffn and not (att and c == 2):
                        for _ in g1(b, j * FC + c, i):
                            pass
                    if att:
                        if c == 3: wo(q)
                        if c == 5: ht(q)
                        if c == 6: lg(q, b + 1, j)
                    if ffn:
                        n = j * FC + c - 2
                        if n >= 0:
                            g2_(n, i)
                        elif not (isinstance(i, int) and i == 0):
                            g2_(n + E1 * FC, i - 1)

            pe.wait_ge(small_split, 4)
            pe.wait_ge(cst, 9)
            pe.wait_ge(l_const, 16 * 7)
            front_pw(0)
            front_qkv(0)
            for j in range(CPB):
                step(-1, -1, j, ffn=False, post=False)
            for j in range(CPB):
                step(0, 0, j, post=False)
            with pe.Fori(0, (NBLK - 2) // 2) as i:
                for b in (1, 2):
                    for j in range(CPB):
                        step(b, 2 * i + b, j)
            pe.wait_ge(fact, at(F_ACT, NCH, "gt"))
            for j in range(CPB):
                step(NBLK - 1, NBLK - 1, j, att=False)
            for n in (2, 1):
                g2_(E1 * FC - n, NBLK - 1)
            pe.wait_ge(ldve, last(L_DVE, "x5"))
            for j in range(CPB):
                for k in range(KD):
                    ins = nc.tensor.transpose(A[j // 2][:, (j % 2) * D + k * P:(j % 2) * D + (k + 1) * P],
                                              xall[:, p_last + j, k * P:(k + 1) * P], ident)
            ins.then_inc(lpe, 1)
            pe.wait_ge(ldve, last(L_DVE, "xlo1"))
            for j in range(CPB):
                ins = three(A[2][:, j * E2:(j + 1) * E2], [ks(xhi4[:, j]), ks(xlo4[:, j])],
                            [ks(cols(small_hi, RT, E2)), ks(cols(small_lo, RT, E2))])
            ins.then_inc(lpe, 1)
            pe.wait_ge(ldve, last(L_DVE, "m12"))
            for j in range(CPB):
                mm(A[3][:, j * E2:(j + 1) * E2], before[:, :], m12_4[:, j, :], start=True, stop=j == 0, skip_group_check=True)
                for jj in range(j):
                    mm(A[3][:, j * E2:(j + 1) * E2], ones[:, :], m12_4[:, jj, :], start=False, stop=jj == j - 1,
                       skip_group_check=True)
            for jj in range(CPB):
                ins = mm(A[3][:, CPB * E2:(CPB + 1) * E2], ones[:, :], m12_4[:, jj, :], start=jj == 0,
                         stop=jj == CPB - 1, skip_group_check=True)
            ins.then_inc(lpe, 1)

            def transposes(g):
                pe.wait_ge(l_xin, 16 * (g + 1))
                if not (isinstance(g, int) and g == 0):
                    pe.wait_ge(xtlo_done, g)
                for s in range(2):
                    for k in range(KD):
                        ins = nc.tensor.transpose(A[0][:, k * TILE + s * P:k * TILE + (s + 1) * P],
                                                  xin[:, s, k * P:(k + 1) * P], ident)
                ins.then_inc(xt_done, 1)

            transposes(0)
            with pe.Fori(0, E2 // 2) as ep:
                for s in range(2):
                    e = 2 * ep + s
                    nt = pe.value_load(tab[0:1, bass.ds(e, 1)], min_val=1, max_val=NTOK // TILE)
                    tb = pe.value_load(tab[0:1, bass.ds(e + E2, 1)], min_val=0, max_val=MOST)
                    pe.wait_ge(w_ready, 2 * E1 + 2 + 2 * e)
                    pe.sem_inc(passed, 1)
                    with pe.Fori(0, nt) as t:
                        g = pe.snap(tb + t)
                        pe.wait_ge(xthi_done, g + 1)
                        pe.wait_ge(xtlo_done, g + 1)
                        for n in range(FC + 4):
                            if n < FC:
                                if n >= 4:
                                    pe.wait_ge(relu_done, g * FC + n - 3)
                                three(U[n % 4][:, 0:TILE],
                                      [[w[:, s, k * FF + n * P:k * FF + (n + 1) * P] for k in range(KD)] for w in (e_hi, e_lo)],
                                      [ks(xt_hi), ks(xt_lo)]).then_inc(u1_done, 1)
                            if n == 5:
                                transposes(g + 1)
                            if n >= 4:
                                c = n - 4
                                pe.wait_ge(uhi_done, g * FC + c + 1)
                                pe.wait_ge(ulo_done, g * FC + c + 2)
                                if c == 0:
                                    pe.wait_ge(y_done, g + 1)
                                    for r in range(2):
                                        mm(Yb[0][:, r * D:(r + 1) * D], ones[:, :], b2_row[:, bass.ds((e + E1) * D, D)],
                                           start=r == 0, stop=False, skip_group_check=True)
                                w = [[t2[:, s, W1C + c * D:W1C + (c + 1) * D]] for t2 in (e_hi, e_lo)]
                                for r in range(2):
                                    ins = three(Yb[0][:, r * D:(r + 1) * D],
                                                [[u_hi[:, c, r * P:(r + 1) * P]], [u_lo[:, c, r * P:(r + 1) * P]]], w,
                                                first=False, last=c == FC - 1)
                        ins.then_inc(u2_done, 1)

        @block.vector
        def _(dve):
            dve.sem_inc(rdve, len(R_DVE))
            dve.sem_inc(ulo_done, 1)
            dve.sem_inc(y_done, 1)
            V = nc.vector

            def split_lo(out_, in_, hi, scale=1.0):
                return V.scalar_tensor_tensor(out=out_, in0=in_, scalar=scale, in1=hi, op0=ALU.mult, op1=ALU.subtract)

            def front_conv(q, b, j, i):
                xt = xTb[:, b % 2]
                if j == 0:
                    dve.wait_ge(l_xT, 16 * (i + 1))
                for tap in range(3):
                    for k in range(KD):
                        src, w = xt[:, k, j * CH + tap:j * CH + tap + CH], wdw_s[:, k * 3 + tap:k * 3 + tap + 1]
                        if tap == 0:
                            V.tensor_scalar(yT[:, k, :], src, w, None, ALU.mult).then_inc(fdve, 1)
                        else:
                            dve.wait_ge(fdve, at(F_DVE, q, f"conv{tap - 1}{'ab'[k]}"))
                            V.scalar_tensor_tensor(out=yT[:, k, :], in0=src, scalar=w, in1=yT[:, k, :],
                                                   op0=ALU.mult, op1=ALU.add).then_inc(fdve, 1)

            def front_ylo(q):
                dve.wait_ge(fact, at(F_ACT, q, "yhi"))
                split_lo(y_lo[:, :, :], yT[:, :, :], y_hi[:, :, :]).then_inc(fdve, 1)

            def front_x2(q, b, j):
                xt = xTb[:, b % 2]
                if isinstance(q, int) and q == 0:
                    V.memset(x2T[:, :, 0:1], 0.0).then_inc(fdve, 1)
                else:
                    V.tensor_scalar(x2T[:, :, 0:1], x2T[:, :, CH:CH + 1], MO["keep"][:, bass.ds(q, 1)], None,
                                    ALU.mult).then_inc(fdve, 1)
                dve.wait_ge(fpe, at(F_PE, q, "pw"))
                dve.wait_ge(fdve, at(F_DVE, q, "halo"))
                V.scalar_tensor_tensor(out=x2T[:, :, 1:CH + 1], in0=A[1][:, 0:D].rearrange("p (k n) -> p k n", k=KD),
                                       scalar=INV, in1=xt[:, :, 2 + j * CH:2 + j * CH + CH],
                                       op0=ALU.mult, op1=ALU.add).then_inc(fdve, 1)
                dve.wait_ge(fdve, at(F_DVE, q, "x2"))
                V.scalar_tensor_tensor(out=x2T[:, :, 0:1], in0=x2T[:, :, 1:2], scalar=MO["new"][:, bass.ds(q, 1)],
                                       in1=x2T[:, :, 0:1], op0=ALU.mult, op1=ALU.add).then_inc(fdve, 1)
                dve.wait_ge(fdve, at(F_DVE, q, "first"))
                V.tensor_tensor(dT[:, :, :], x2T[:, :, 1:CH + 1], x2T[:, :, 0:CH], ALU.subtract).then_inc(fdve, 1)
                dve.wait_ge(fact, at(F_ACT, q, "x2hi"))
                split_lo(x2_lo[:, :, :], x2T[:, :, 1:CH + 1], x2_hi[:, :, :]).then_inc(fdve, 1)
                dve.wait_ge(fact, at(F_ACT, q, "dhi"))
                split_lo(d_lo[:, :, :], dT[:, :, :], d_hi[:, :, :]).then_inc(fdve, 1)

            def front_phi(q, c):
                cos = rope_s[:, bass.ds(c, 1), 0, :].broadcast_to([P, 2 * H, DH])
                sin = rope_s[:, bass.ds(c, 1), 1, :].broadcast_to([P, 2 * H, DH])
                qk = A[1][:, :].rearrange("p (h d) -> p h d", d=DH)
                dve.wait_ge(fpe, at(F_PE, q, "qk"))
                V.tensor_tensor(r1[:, :].rearrange("p (h d) -> p h d", d=DH), qk, cos, ALU.mult).then_inc(fdve, 1)
                r2v = r2[:, :].rearrange("p (h d) -> p h d", d=DH)
                V.tensor_tensor(r2v[:, :, 0:DH:2], qk[:, :, 1:DH:2], sin[:, :, 0:DH:2], ALU.mult).then_inc(fdve, 1)
                V.tensor_tensor(r2v[:, :, 1:DH:2], qk[:, :, 0:DH:2], sin[:, :, 1:DH:2], ALU.mult).then_inc(fdve, 1)
                dve.wait_ge(fdve, at(F_DVE, q, "rot_sin_b"))
                V.tensor_tensor(rq[:, :], r1[:, :], r2[:, :], ALU.add).then_inc(fdve, 1)
                dve.wait_ge(fdve, at(F_DVE, q, "rot"))
                V.tensor_scalar(phm[:, :], rq[:, :], 0.0, None, ALU.min).then_inc(fdve, 1)

            def front_phi2(q):
                dve.wait_ge(fact, at(F_ACT, q, "vext"))
                V.scalar_tensor_tensor(out=gz[:, :], in0=A[2][:, D:2 * D], scalar=INV, in1=rows_s[:, 0:D],
                                       op0=ALU.mult, op1=ALU.add).then_inc(fdve, 1)
                dve.wait_ge(fact, at(F_ACT, q, "phiexp"))
                V.scalar_tensor_tensor(out=phi[:, :], in0=rq[:, :], scalar=0.0, in1=phe[:, :],
                                       op0=ALU.max, op1=ALU.add).then_inc(fdve, 1)

            def front_lo(q):
                dve.wait_ge(fact, at(F_ACT, q, "khi"))
                for n, (t, lo) in enumerate(((qp, 2), (kp, 1))):
                    split_lo(t[:, :, lo, :], phi[:, n * D:(n + 1) * D].rearrange("p (h d) -> p h d", d=DH), t[:, :, 0, :])\
                        .then_inc(fdve, 1)

            def tail_kS(q):
                dve.wait_ge(tpe, at(T_PE, q, "phit"))
                V.tensor_copy(kS, A[2][:, :].bitcast(F16).rearrange("p (g n) -> p g n", n=CH)).then_inc(tdve, 1)
                V.tensor_scalar(state[:, :, :], state[:, :, :], MO["keep"][:, bass.ds(q, 1)], None,
                                ALU.mult).then_inc(tdve, 1)

            def tail_mask(q):
                dve.wait_ge(tpe, at(T_PE, q, "score"))
                for j in (0, 2, 1, 3):
                    V.tensor_tensor(sm[:, j, :, :], A[j][:, :].rearrange("p (m n) -> p m n", m=4),
                                    causal.unsqueeze(1).broadcast_to([P, 4, CH]), ALU.mult).then_inc(tdve, 1)

            def tail_attn(q):
                o = A[0][:, 0:H * HE].rearrange("p (h e) -> p h e", e=HE)
                dve.wait_ge(tpe, at(T_PE, q, "av"))
                V.tensor_scalar(den[:, :].unsqueeze(2), o[:, :, DH:HE], 1e-6, None, ALU.add).then_inc(tdve, 1)
                dve.wait_ge(tdve, at(T_DVE, q, "den"))
                V.reciprocal(rden[:, :], den[:, :]).then_inc(tdve, 1)
                dve.wait_ge(tdve, at(T_DVE, q, "rden"))
                V.tensor_tensor(attn[:, :].rearrange("p (h d) -> p h d", d=DH), o[:, :, 0:DH],
                                rden[:, :].unsqueeze(2).broadcast_to([P, H, DH]), ALU.mult).then_inc(tdve, 1)
                dve.wait_ge(tpe, at(T_PE, q, "kv"))
                V.tensor_tensor(kvt[:, :, :], A[1][:, 0:H * HE].rearrange("p (k n) -> p k n", k=KD),
                                MO["block"].unsqueeze(1).broadcast_to([P, KD, H // 2 * HE]), ALU.mult).then_inc(tdve, 1)
                dve.wait_ge(tdve, at(T_DVE, q, "kvt"))
                V.tensor_tensor(state[:, :, :], state[:, :, :], kvt[:, :, :], ALU.add).then_inc(tdve, 1)

            def tail_alo(q):
                dve.wait_ge(tact, at(T_ACT, q, "ahi"))
                split_lo(a_lo, A[2][:, 0:D].rearrange("p (k n) -> p k n", k=KD), a_hi).then_inc(tdve, 1)

            def norm(sem_, steps, q, bn_, mv_, src, names):
                V.bn_stats(bn_[:, :], src).then_inc(sem_, 1)
                dve.wait_ge(sem_, at(steps, q, names[0]))
                dve.sem_inc(passed, 1)
                V.bn_aggr(mv_[:, :], bn_[:, :]).then_inc(sem_, 1)

            def tail_x3(q):
                dve.wait_ge(tpe, at(T_PE, q, "wo"))
                V.scalar_tensor_tensor(out=g2[:, :], in0=gt[:, :], scalar=1.0, in1=A[3][:, 0:D],
                                       op0=ALU.add, op1=ALU.mult).then_inc(tdve, 1)
                dve.wait_ge(tdve, at(T_DVE, q, "g2"))
                V.scalar_tensor_tensor(out=x3[:, :], in0=g2[:, :], scalar=0.5 * INV, in1=x2tok[:, :],
                                       op0=ALU.mult, op1=ALU.add).then_inc(tdve, 1)
                dve.wait_ge(tdve, at(T_DVE, q, "x3"))
                norm(tdve, T_DVE, q, bn, mv, x3[:, :], ("bn",))

            def tail_h0(q):
                dve.wait_ge(tpool, at(T_POOL, q, "rstd"))
                V.tensor_scalar(h0[:, :], x3[:, :], mv[:, 0:1], rstd[:, 0:1], ALU.subtract, ALU.mult).then_inc(tdve, 1)

            def tail_hlo(q, b, j):
                dve.wait_ge(tact, at(T_ACT, q, "hhi"))
                split_lo(hT_lo[:, b % 2, :, j * CH:(j + 1) * CH], A[3][:, D:2 * D].rearrange("p (k n) -> p k n", k=KD),
                         hT_hi[:, b % 2, :, j * CH:(j + 1) * CH]).then_inc(tdve, 1)

            def tail_gmax(q):
                dve.wait_ge(tpe, at(T_PE, q, "lg"))
                V.tensor_reduce(gm[:, :], A[3][:, 0:E1], AX.X, ALU.max).then_inc(tdve, 1)
                dve.wait_ge(tdve, at(T_DVE, q, "gmax"))
                V.tensor_scalar(gn[:, :], gm[:, :], -INV, None, ALU.mult).then_inc(tdve, 1)

            def tail_gate(q, b, j):
                dve.wait_ge(tact, at(T_ACT, q, "gexp"))
                V.reciprocal(gr[:, :], gs[:, :]).then_inc(tdve, 1)
                dve.wait_ge(tdve, at(T_DVE, q, "rsum"))
                V.tensor_scalar(gw[:, b % 2, j, :], ge[:, :], gr[:, 0:1], INV, ALU.mult, ALU.mult).then_inc(tdve, 1)

            def split_half_lo(n):
                dve.wait_ge(whi_done, n + 1)
                split_lo(w_lo[:, n // 2, (n % 2) * W1C:(n % 2 + 1) * W1C], stage[:, n % 2, :],
                         w_hi[:, n // 2, (n % 2) * W1C:(n % 2 + 1) * W1C], SCALE).then_inc(w_ready, 1)

            def b2_rows(j):
                nb = (E1 + E2) * D
                if j == 0:
                    dve.wait_ge(b2_act, 2)
                    split_lo(b2_l, b2_f[:, 0:nb], b2_h, SCALE).then_inc(b2_dve, 1)
                    dve.wait_ge(b2_dve, 1)
                    V.tensor_scalar(b2_h, b2_h, b2_f[:, nb:nb + 1], None, ALU.mult).then_inc(b2_dve, 1)
                else:
                    dve.wait_ge(b2_dve, 2)
                    V.scalar_tensor_tensor(out=b2_row[0:2, :], in0=b2_l, scalar=b2_f[:, nb + 1:nb + 2], in1=b2_h,
                                           op0=ALU.mult, op1=ALU.add).then_inc(b2_dve, 1)

            def hlo(n, i):
                u = i * E1 * FC + n
                dve.wait_ge(hhi_done, u + 1)
                V.tensor_tensor(h_lo[:, n % 4, :], s32[:, n % 2, :], h_hi[:, n % 4, :], ALU.subtract).then_inc(hlo_done, 1)

            def comb(e, b, i):
                dve.wait_ge(g2_done, (i * E1 + e + 1) * FC)
                if e == 0:
                    dve.wait_ge(tpool, at(T_POOL, i * CPB + CPB - 1, "xres"))
                    dve.wait_ge(tdve, at(T_DVE, i * CPB + CPB - 1, "gw"))
                else:
                    dve.wait_ge(comb_done, (i * E1 + e) * CPB)
                for t in range(CPB):
                    a = acc[:, b % 2, t, :]
                    V.scalar_tensor_tensor(out=a, in0=Yb[t // 2][:, (t % 2) * D:(t % 2 + 1) * D],
                                           scalar=gw[:, b % 2, t, e:e + 1], in1=a,
                                           op0=ALU.mult, op1=ALU.add).then_inc(comb_done, 1)

            def post_norm(p, b, j, i):
                dve.wait_ge(comb_done, (i * E1 + E1 - 1) * CPB + j + 1)
                norm(rdve, R_DVE, p, pbn, pmv, acc[:, b % 2, j, :], ("bn",))

            def post_x5(p, b, j):
                dve.wait_ge(rpool, at(R_POOL, p, "rstd"))
                before_chunk(dve, p, (rpool, R_POOL, "sent"))
                V.tensor_scalar(px5[:, :], acc[:, b % 2, j, :],
                                pmv[:, 0:1], prstd[:, 0:1], ALU.subtract, ALU.mult).then_inc(rdve, 1)

            def post_xlo(p):
                dve.wait_ge(ract, at(R_ACT, p, "xhi"))
                split_lo(px_lo[:, :, :], A[0][:, 0:D].rearrange("p (k n) -> p k n", k=KD), px_hi[:, :, :]).then_inc(rdve, 1)

            def post_route(p):
                dve.wait_ge(rpe, at(R_PE, p, "rl"))
                V.scalar_tensor_tensor(out=plg[:, :], in0=A[0][:, D:D + E2], scalar=INV, in1=rows_s[:, 3 * D:3 * D + E2],
                                       op0=ALU.mult, op1=ALU.add).then_inc(rdve, 1)
                dve.wait_ge(rdve, at(R_DVE, p, "lg"))
                dve.sem_inc(passed, 1)
                V.max(top8[:, :], plg[:, :]).then_inc(rdve, 1)
                dve.wait_ge(rdve, at(R_DVE, p, "top"))
                dve.sem_inc(passed, 1)
                V.tensor_tensor(dlt[:, bass.ds(p, 1)], top8[:, 1:2], top8[:, 0:1], ALU.subtract).then_inc(rdve, 1)
                V.max_index(topi[:, :], top8[:, :], plg[:, :]).then_inc(rdve, 1)
                dve.wait_ge(rdve, at(R_DVE, p, "topi"))
                V.tensor_scalar(m1[:, :], MO["iota8"], topi[:, 0:1], None, ALU.is_equal).then_inc(rdve, 1)
                V.tensor_scalar(m2[:, :], MO["iota8"], topi[:, 1:2], None, ALU.is_equal).then_inc(rdve, 1)
                dve.wait_ge(rdve, at(R_DVE, p, "m2"))
                V.tensor_tensor(m12[:, :], m1[:, :], m2[:, :], ALU.add).then_inc(rdve, 1)

            def post_rank(p):
                dve.wait_ge(rpe, at(R_PE, p, "rk"))
                V.tensor_tensor(rank[:, :], A[0][:, 2 * D - 2 * E2:2 * D - E2], count[:, :], ALU.add).then_inc(rdve, 1)
                dve.wait_ge(rdve, at(R_DVE, p, "rank"))
                for n, m in enumerate((m1, m2)):
                    V.tensor_tensor_reduce(junk[:, n, :], m[:, :], rank[:, :], 1.0, 0.0, ALU.mult, ALU.add,
                                           posf[:, n:n + 1]).then_inc(rdve, 1)
                V.tensor_tensor(count[:, :], count[:, :], A[0][:, 2 * D - E2:2 * D], ALU.add).then_inc(rdve, 1)
                dve.wait_ge(rdve, at(R_DVE, p, "p2"))
                V.tensor_copy(idx[:, :], posf[:, :]).then_inc(rdve, 1)
                V.tensor_copy(pos[:, bass.ds(p, 1), :].rearrange("p a d -> p (a d)"), posf[:, :]).then_inc(rdve, 1)

            def step(b, i, j, ffn=True, att=True, post=True, w_split=False):
                q = (i + 1) * CPB + j
                nb, nj = b + 1 + (j == CPB - 1), (j + 1) % CPB
                p = (i - 1) * CPB + j
                for c in range(FC):
                    if att and c == 0:
                        tail_kS(q)
                    if ffn and c == 0:
                        if j > 0:
                            hlo(j * FC - 1, i)
                        elif not (isinstance(i, int) and i == 0):
                            hlo(E1 * FC - 1, i - 1)
                    if att and c == 1:
                        tail_mask(q)
                    if ffn and c == 1:
                        hlo(j * FC, i)
                    if att and c == 2:
                        front_ylo(q + 1)
                    if ffn and c == 2:
                        if j > 0:
                            comb(j - 1, b, i)
                        elif not (isinstance(i, int) and i == 0):
                            comb(E1 - 1, b - 1, i - 1)
                    if post and c == 2:
                        post_norm(p, b - 1, j, i - 1)
                        post_x5(p, b - 1, j)
                    if att:
                        if c == 2: tail_attn(q)
                        if c == 3: tail_alo(q); front_x2(q + 1, nb, nj)
                    if post and c == 3:
                        post_xlo(p)
                    if att and c == 3:
                        tail_x3(q)
                    if post and c == 4:
                        post_route(p)
                    if ffn and c == 4:
                        hlo(j * FC + c - 1, i)
                    if att and c == 4 and ffn:
                        tail_h0(q)
                    if post and c == 5:
                        post_rank(p)
                    if att and c == 5:
                        front_phi(q + 1, row_chunk(q + 1))
                        if not ffn:
                            tail_h0(q)
                        tail_hlo(q, b + 1, j)
                    if att:
                        if c == 6:
                            front_phi2(q + 1)
                            tail_gmax(q)
                            front_lo(q + 1)
                            front_conv(q + 2, b + 1 + (j >= CPB - 2), (j + 2) % CPB, i + 1 + (j >= CPB - 2))
                        if c == 7: tail_gate(q, b + 1, j)
                    if w_split:
                        if c == 1: split_half_lo(2 * j); split_half_lo(2 * j + 1)
                        if c == 1 and j < 2: b2_rows(j)
                    if ffn and c not in (0, 3, FC - 1):
                        hlo(j * FC + c, i)

            def row_chunk(q):
                return q % (T // CH)

            V.memset(ones[:, :], 1.0).then_inc(cst, 1)
            V.memset(mhalves[:, :], -0.5).then_inc(cst, 1)
            V.memset(state[:, :, :], 0.0).then_inc(cst, 1)
            V.memset(zeros[:, :], 0.0).then_inc(cst, 1)
            V.memset(b2_row[:, :], 0.0).then_inc(cst, 1)
            V.memset(parts, 0.0).then_inc(cst, 1)
            dve.wait_ge(l_const, 16 * 7)
            V.tensor_tensor(before[:, :], causal, ident, ALU.subtract).then_inc(cst, 1)
            V.tensor_copy(count[:, :], MO["base"]).then_inc(cst, 1)
            V.tensor_copy(ident16[:, :], ident).then_inc(cst, 1)
            dve.wait_ge(cst, 9)
            for n in range(2):
                w = W1C if n == 0 else SMALL - W1C
                dve.wait_ge(small_split, n * 2 + 1)
                split_lo(small_lo[:, n * W1C:n * W1C + w], stage[:, n, 0:w], small_hi[:, n * W1C:n * W1C + w], SCALE)\
                    .then_inc(small_split, 1)
            front_conv(0, 0, 0, 0)
            front_ylo(0)
            front_x2(0, 0, 0)
            front_phi(0, 0)
            front_phi2(0)
            front_lo(0)
            front_conv(1, 0, 1, 0)
            for j in range(CPB):
                step(-1, -1, j, ffn=False, post=False, w_split=True)
            for j in range(CPB):
                step(0, 0, j, post=False)
            dve.wait_ge(z_done, 16 * E2)
            with dve.Fori(0, (NBLK - 2) // 2) as i:
                for b in (1, 2):
                    for j in range(CPB):
                        step(b, 2 * i + b, j)
            for j in range(CPB):
                step(NBLK - 1, NBLK - 1, j, att=False)
            hlo(E1 * FC - 1, NBLK - 1)
            comb(E1 - 1, NBLK - 1, NBLK - 1)
            dve.wait_ge(comb_done, NBLK * E1 * CPB)
            for j in range(CPB):
                ins = V.bn_stats(bn4[:, j, :], acc[:, (NBLK - 1) % 2, j, :])
            ins.then_inc(ldve, 1)
            dve.wait_ge(ldve, last(L_DVE, "bn"))
            dve.sem_inc(passed, 1)
            for j in range(CPB):
                ins = V.bn_aggr(mv4[:, j, :], bn4[:, j, :])
            ins.then_inc(ldve, 1)
            dve.wait_ge(lpool, last(L_POOL, "rstd"))
            for j in range(CPB):
                ins = V.tensor_scalar(xall[:, p_last + j, :], acc[:, (NBLK - 1) % 2, j, :], mv4[:, j, 0:1], rstd4[:, j, 0:1],
                                      ALU.subtract, ALU.mult)
            ins.then_inc(ldve, 1)
            for n in range(2):
                dve.wait_ge(lact, last(L_ACT, f"xhi{n}"))
                split_lo(xlo4[:, 2 * n:2 * n + 2], A[n][:, :].rearrange("p (j k n) -> p j k n", j=2, k=KD),
                         xhi4[:, 2 * n:2 * n + 2]).then_inc(ldve, 1)
            dve.wait_ge(lpe, last(L_PE, "rl"))
            V.scalar_tensor_tensor(out=lg4, in0=A[2][:, 0:CPB * E2].rearrange("p (j e) -> p j e", j=CPB), scalar=INV,
                                   in1=rows_s[:, 3 * D:3 * D + E2].unsqueeze(1).broadcast_to([P, CPB, E2]),
                                   op0=ALU.mult, op1=ALU.add).then_inc(ldve, 1)
            dve.wait_ge(ldve, last(L_DVE, "lg"))
            dve.sem_inc(passed, 1)
            for j in range(CPB):
                ins = V.max(top4[:, j, :], lg4[:, j, :])
            ins.then_inc(ldve, 1)
            dve.wait_ge(ldve, last(L_DVE, "top"))
            dve.sem_inc(passed, 1)
            V.tensor_tensor(dlt[:, p_last:NCH].unsqueeze(2), top4[:, :, 1:2], top4[:, :, 0:1], ALU.subtract).then_inc(ldve, 1)
            for j in range(CPB):
                ins = V.max_index(topi4[:, j, :], top4[:, j, :], lg4[:, j, :])
            ins.then_inc(ldve, 1)
            dve.wait_ge(ldve, last(L_DVE, "topi"))
            for j in range(CPB):
                for n in range(2):
                    ins = V.tensor_scalar(m4[n][:, j, :], MO["iota8"], topi4[:, j, n:n + 1], None, ALU.is_equal)
            ins.then_inc(ldve, 1)
            dve.wait_ge(ldve, last(L_DVE, "m"))
            V.tensor_tensor(m12_4, m4[0], m4[1], ALU.add).then_inc(ldve, 1)
            dve.wait_ge(lpe, last(L_PE, "rk"))
            V.tensor_tensor(rank4, A[3][:, 0:CPB * E2].rearrange("p (j e) -> p j e", j=CPB),
                            count[:, :].unsqueeze(1).broadcast_to([P, CPB, E2]), ALU.add).then_inc(ldve, 1)
            dve.wait_ge(ldve, last(L_DVE, "rank"))
            for j in range(CPB):
                for n in range(2):
                    ins = V.tensor_tensor_reduce(junk4[n][:, j, :], m4[n][:, j, :], rank4[:, j, :], 1.0, 0.0, ALU.mult, ALU.add,
                                                 pos4[:, j, n:n + 1])
            ins.then_inc(ldve, 1)
            V.tensor_tensor(count[:, :], count[:, :], A[3][:, CPB * E2:(CPB + 1) * E2], ALU.add).then_inc(ldve, 1)
            dve.wait_ge(ldve, last(L_DVE, "pos4"))
            V.tensor_copy(idx4, pos4).then_inc(ldve, 1)
            V.tensor_copy(pos[:, p_last:NCH, :], pos4).then_inc(ldve, 1)

            chain = [0]

            def link(ins):
                chain[0] += 1
                ins.then_inc(cnt_chain, 1)
                dve.wait_ge(cnt_chain, chain[0])

            dve.wait_ge(ldve, last(L_DVE, "pos"))
            link(V.tensor_tensor(cf[:, :], count[:, :], MO["base"], ALU.subtract))
            link(V.tensor_scalar(cf[:, :], cf[:, :], float(TILE - 1), None, ALU.add))
            link(V.tensor_copy(ci[:, :], cf[:, :]))
            link(V.tensor_scalar(ct[:, :], ci[:, :], TILE.bit_length() - 1, None, ALU.arith_shift_right))
            link(V.tensor_copy(ctf[:, :], ct[:, :]))
            link(V.tensor_scalar(tabf[:, 0:E2], ctf[:, :], 1.0, None, ALU.max))
            link(V.memset(cf[:, :], 0.0))
            link(V.tensor_tensor_scan(cum[:, :], tabf[:, 0:E2], cf[:, :], 0.0, ALU.add, ALU.add))
            link(V.tensor_tensor(tabf[:, E2:2 * E2], cum[:, :], tabf[:, 0:E2], ALU.subtract))
            link(V.tensor_copy(tabf[:, 2 * E2:3 * E2], count[:, :]))
            link(V.tensor_copy(tabf[:, 3 * E2:3 * E2 + 1], cum[:, E2 - 1:E2]))
            dve.wait_ge(rpool, at(R_POOL, NCH - CPB - 1, "sent"))
            link(V.memset(zeros[:, :], 0.0))
            link(V.tensor_copy(tab[:, :], tabf[:, :]))
            dve.sem_inc(tab_ready, 1)
            link(V.tensor_scalar(shift[:, :], tabf[:, E2:2 * E2], float(TILE), None, ALU.mult))
            link(V.tensor_tensor(shift[:, :], shift[:, :], MO["base"], ALU.subtract))
            link(V.memset(move[:, :, :], 0.0))
            for e in range(1, E2):
                link(V.tensor_tensor(cf[:, 0:1], shift[:, e:e + 1], shift[:, e - 1:e], ALU.subtract))
                link(V.tensor_scalar(moved[:, :, :], pos[:, :, :], float(e * CAP), cf[:, 0:1], ALU.is_ge, ALU.mult))
                link(V.tensor_tensor(move[:, :, :], move[:, :, :], moved[:, :, :], ALU.add))
            link(V.tensor_tensor(posy[:, :, :], pos[:, :, :], move[:, :, :], ALU.add))

            def tile_lo(g):
                dve.wait_ge(xthi_done, g + 1)
                split_lo(xt_lo[:, :, :], A[0][:, :].rearrange("p (k n) -> p k n", k=KD), xt_hi[:, :, :])\
                    .then_inc(xtlo_done, 1)

            dve.wait_ge(tab_ready, 1)
            tile_lo(0)
            with dve.Fori(0, E2) as e:
                nt = dve.value_load(tab[0:1, bass.ds(e, 1)], min_val=1, max_val=NTOK // TILE)
                tb = dve.value_load(tab[0:1, bass.ds(e + E2, 1)], min_val=0, max_val=MOST)
                with dve.Fori(0, nt) as t:
                    g = dve.snap(tb + t)
                    for c in range(FC):
                        dve.wait_ge(uhi_done, g * FC + c + 1)
                        V.tensor_tensor(u_lo[:, c, :], u32t[:, c % 4, :], u_hi[:, c, :], ALU.subtract).then_inc(ulo_done, 1)
                    tile_lo(g + 1)
                    dve.wait_ge(u2_done, g + 2)
                    dve.wait_ge(y_out, 16 * (g + 1))
                    V.tensor_scalar(ysb[:, :, :], Yb[0][:, :].rearrange("p (s d) -> p s d", s=2), INV, None, ALU.mult)\
                        .then_inc(y_done, 1)

            dve.wait_ge(wexp_done, 1)
            link(V.tensor_scalar(wone[:, :], wexp[:, :], 1.0, None, ALU.add))
            link(V.reciprocal(wt[:, 0, :], wone[:, :]))
            link(V.tensor_tensor(wt[:, 1, :], wt[:, 0, :], wexp[:, :], ALU.mult))

            def sums(i):
                first, end = GROUPS[i]
                for n in range(first, end):
                    xr, r = xall[:, n, :], n % NR
                    dve.wait_ge(l_y[r], 32 * (n // NR + 1))
                    for a in range(2):
                        V.scalar_tensor_tensor(out=xr, in0=rows8[:, r, a, :], scalar=wt[:, a, n:n + 1], in1=xr,
                                               op0=ALU.mult, op1=ALU.add).then_inc(sum_done, 1)
                        dve.wait_ge(sum_done, 2 * n + a + 1)
                    V.bn_stats(fbn[:, n - first, :], xr).then_inc(stat_done, 1)
                for n in range(first, end):
                    dve.wait_ge(stat_done, first + n + 1)
                    V.bn_aggr(fmv[:, i % 2, n - first, :], fbn[:, n - first, :]).then_inc(stat_done, 1)

            def norms(i):
                first, end = GROUPS[i]
                dve.wait_ge(frstd, i + 1)
                if i >= 2:
                    dve.wait_ge(fin_out[i % 2], 16 * (i // 2))
                for n in range(first, end):
                    r = n - first
                    V.tensor_scalar(fin[:, i % 2, r, :], xall[:, n, :], fmv[:, i % 2, r, 0:1], frs[:, i % 2, r:r + 1],
                                    ALU.subtract, ALU.mult).then_inc(normed, 1)

            sums(0)
            for i in range(1, len(GROUPS)):
                sums(i)
                norms(i - 1)
            norms(len(GROUPS) - 1)

        @block.scalar
        def _(act):
            act.sem_inc(ract, len(R_ACT))
            act.sem_inc(y_out, 16)
            S = nc.scalar

            def copy(out_, in_, scale=1.0):
                return S.activation(out_, in_, ACT.Copy, scale=scale)

            def front_yhi(q):
                act.wait_ge(fdve, at(F_DVE, q, "conv2b"))
                copy(y_hi[:, :, :], yT[:, :, :]).then_inc(fact, 1)

            def front_x2(q):
                act.wait_ge(fdve, at(F_DVE, q, "x2"))
                copy(x2_hi[:, :, :], x2T[:, :, 1:CH + 1]).then_inc(fact, 1)
                act.wait_ge(fdve, at(F_DVE, q, "delta"))
                copy(d_hi[:, :, :], dT[:, :, :]).then_inc(fact, 1)

            def front_evac(q):
                act.wait_ge(fpe, at(F_PE, q, "x2t"))
                before_chunk(act, q, (tdve, T_DVE, "x3"))
                copy(vext[:, :, 0:DH], A[2][:, 0:D].rearrange("p (h d) -> p h d", d=DH), INV).then_inc(fact, 1)
                copy(x2tok[:, :], A[0][:, D:2 * D]).then_inc(fact, 1)

            def front_exp(q):
                act.wait_ge(fdve, at(F_DVE, q, "phimin"))
                S.activation(phe[:, :], phm[:, :], ACT.Exp).then_inc(fact, 1)

            def front_gt(q):
                act.wait_ge(fdve, at(F_DVE, q, "gz"))
                S.activation(gt[:, :], gz[:, :], ACT.Tanh, scale=0.5).then_inc(fact, 1)

            def front_hi(q):
                act.wait_ge(fdve, at(F_DVE, q, "phi"))
                for n, to in enumerate((qp[:, :, 0:2, :], kp[:, :, 0:3:2, :])):
                    copy(to, phi[:, n * D:(n + 1) * D].rearrange("p (h d) -> p h d", d=DH).unsqueeze(2)
                         .broadcast_to([P, H, 2, DH])).then_inc(fact, 1)

            def tail_T(q):
                act.wait_ge(tpe, at(T_PE, q, "phit"))
                copy(qS, A[1][:, :].bitcast(F16).rearrange("p (g n) -> p g n", n=CH)).then_inc(tact, 1)
                copy(qTs[:, :, :], A[3][:, 0:D].rearrange("p (k n) -> p k n", k=KD)).then_inc(tact, 1)

            def tail_ahi(q):
                act.wait_ge(tpe, at(T_PE, q, "at"))
                copy(a_hi, A[2][:, 0:D].rearrange("p (k n) -> p k n", k=KD)).then_inc(tact, 1)

            def tail_hhi(q, b, j):
                act.wait_ge(tpe, at(T_PE, q, "ht"))
                copy(hT_hi[:, b % 2, :, j * CH:(j + 1) * CH],
                     A[3][:, D:2 * D].rearrange("p (k n) -> p k n", k=KD)).then_inc(tact, 1)

            def tail_gexp(q):
                act.wait_ge(tdve, at(T_DVE, q, "ngmax"))
                S.activation(ge[:, :], A[3][:, 0:E1], ACT.Exp, bias=gn[:, 0:1], scale=INV, accum_out=gs[:, 0:1])\
                    .then_inc(tact, 1)

            def silu(n, i):
                e, c = n // FC, n % FC
                u = i * E1 * FC + n
                act.wait_ge(g1_done, u + 1)
                if not (isinstance(u, int) and u < 2):
                    act.wait_ge(hlo_done, u - 1)
                S.activation(s32[:, n % 2, :], Hb[n % 2][:, :], ACT.Silu, bias=b1_s[:, e * FC + c:e * FC + c + 1],
                             scale=INV).then_inc(silu_done, 1)
                act.wait_ge(silu_done, u + 1)
                if not (isinstance(u, int) and u < 4):
                    act.wait_ge(g2_done, u - 3)
                copy(h_hi[:, n % 4, :], s32[:, n % 2, :]).then_inc(hhi_done, 1)

            def post_xhi(p):
                act.wait_ge(rpe, at(R_PE, p, "xt"))
                copy(px_hi[:, :, :], A[0][:, 0:D].rearrange("p (k n) -> p k n", k=KD)).then_inc(ract, 1)

            def step(b, i, j, ffn=True, att=True, post=True, w_split=False):
                q = (i + 1) * CPB + j
                for c in range(FC):
                    if att:
                        if c == 0: tail_T(q)
                        if c == 3: tail_ahi(q); front_x2(q + 1)
                        if c == 5: front_evac(q + 1)
                        if c == 6: tail_hhi(q, b + 1, j); front_exp(q + 1); front_gt(q + 1); front_hi(q + 1); tail_gexp(q)
                    if post and c == 3:
                        post_xhi((i - 1) * CPB + j)
                    if ffn and c == 0:
                        if j > 0:
                            silu(j * FC - 1, i)
                        elif not (isinstance(i, int) and i == 0):
                            silu(E1 * FC - 1, i - 1)
                    if ffn and c < FC - 1:
                        silu(j * FC + c, i)
                    if att:
                        if c == 7: front_yhi(q + 2)
                    if w_split:
                        if c == 1: split_half_hi(2 * j); split_half_hi(2 * j + 1)
                        if c == 1 and j == 0:
                            copy(b2_h, b2_f[:, 0:(E1 + E2) * D], SCALE).then_inc(b2_act, 1)

            def split_half_hi(n):
                act.wait_ge(l_stage[n % 2], 16 * (n // 2 + 2))
                if n == 4:
                    act.wait_ge(b2_dve, 3)
                copy(w_hi[:, n // 2, (n % 2) * W1C:(n % 2 + 1) * W1C], stage[:, n % 2, :], SCALE).then_inc(whi_done, 1)

            for n in range(2):
                w = W1C if n == 0 else SMALL - W1C
                act.wait_ge(l_stage[n], 16)
                if n:
                    act.wait_ge(small_split, 2)
                copy(small_hi[:, n * W1C:n * W1C + w], stage[:, n, 0:w], SCALE).then_inc(small_split, 1)
            act.wait_ge(l_const, 16 * 7)
            front_yhi(0)
            front_x2(0)
            act.wait_ge(cst, 1)
            copy(vext[:, :, DH:HE], ones[:, 0:H].unsqueeze(2)).then_inc(b2_act, 1)
            front_evac(0)
            front_exp(0)
            front_gt(0)
            front_hi(0)
            front_yhi(1)
            for j in range(CPB):
                step(-1, -1, j, ffn=False, post=False, w_split=True)
            for j in range(CPB):
                step(0, 0, j, post=False)
            with act.Fori(0, (NBLK - 2) // 2) as i:
                for b in (1, 2):
                    for j in range(CPB):
                        step(b, 2 * i + b, j)
            for j in range(CPB):
                step(NBLK - 1, NBLK - 1, j, att=False)
            silu(E1 * FC - 1, NBLK - 1)
            act.wait_ge(lpe, last(L_PE, "xt"))
            for n in range(2):
                copy(xhi4[:, 2 * n:2 * n + 2], A[n][:, :].rearrange("p (j k n) -> p j k n", j=2, k=KD)).then_inc(lact, 1)

            act.wait_ge(ldve, last(L_DVE, "dlt"))
            S.activation(wexp[:, :], dlt[:, :], ACT.Exp).then_inc(wexp_done, 1)

            def tile_hi(g):
                act.wait_ge(xt_done, g + 2)
                if not (isinstance(g, int) and g == 0):
                    act.wait_ge(u1_done, g * FC)
                copy(xt_hi[:, :, :], A[0][:, :].rearrange("p (k n) -> p k n", k=KD)).then_inc(xthi_done, 1)

            act.wait_ge(tab_ready, 1)
            tile_hi(0)
            with act.Fori(0, E2) as e:
                nt = act.value_load(tab[0:1, bass.ds(e, 1)], min_val=1, max_val=NTOK // TILE)
                tb = act.value_load(tab[0:1, bass.ds(e + E2, 1)], min_val=0, max_val=MOST)
                with act.Fori(0, nt) as t:
                    g = act.snap(tb + t)
                    for c in range(FC):
                        act.wait_ge(u1_done, g * FC + c + 1)
                        if c >= 4:
                            act.wait_ge(ulo_done, g * FC + c - 2)
                        else:
                            act.wait_ge(ulo_done, g * FC + 1)
                        S.activation(u32t[:, c % 4, :], U[c % 4][:, 0:TILE], ACT.Relu,
                                     bias=b1r_s[:, bass.ds(e * FC + c, 1)], scale=INV).then_inc(relu_done, 1)
                        act.wait_ge(relu_done, g * FC + c + 1)
                        if c == 0:
                            act.wait_ge(u2_done, g + 1)
                        copy(u_hi[:, c, :], u32t[:, c % 4, :]).then_inc(uhi_done, 1)
                    tile_hi(g + 1)
                    act.wait_ge(y_done, g + 2)
                    row = g.with_bounds(min_val=0, max_val=MOST - 1) * TILE
                    act.dma_start(yg[bass.ds(row, TILE), :].rearrange("(s p) d -> p s d", p=P), ysb[:, :, :])\
                       .then_inc(y_out, 16)

        @block.gpsimd
        def _(pool):
            pool.sem_inc(rpool, len(R_POOL))

            G = nc.gpsimd

            def wait(s, value):
                pool.wait_ge(s, value)
                pool.sem_inc(passed, 1)


            def split(src, hi, lo, n):
                k = 3 * (n - 2 * E1)
                G.tensor_scalar(src, src, SCALE, 1.0, ALU.mult, ALU.mult).then_inc(wch, 1)
                wait(wch, k + 1)
                G.tensor_copy(hi, src).then_inc(wch, 1)
                wait(wch, k + 2)
                G.tensor_tensor(lo, src, hi, ALU.subtract).then_inc(wch, 1)
                wait(wch, k + 3)
                pool.sem_inc(stage_used, 1)
                pool.sem_inc(w_ready, 1)

            def tail(q, b, j):
                wait(tpe, at(T_PE, q, "av"))
                G.memset(parts[:, 0:2 * NP].rearrange("p (h c d) -> p h c d", c=4, d=DH)[:, :, 3, :], 0.0)\
                    .then_inc(tpool, 1)
                wait(tdve, at(T_DVE, q, "x3"))
                G.tensor_tensor(acc[:, b % 2, j, :], xall[:, bass.ds(q, 1), :].rearrange("p a d -> p (a d)"), x3[:, :],
                                ALU.add).then_inc(tpool, 1)
                wait(tdve, at(T_DVE, q, "aggr"))
                G.tensor_scalar(rstd[:, :], mv[:, 1:2], EPS, 1.0, ALU.add, ALU.mult).then_inc(tpool, 1)
                wait(tpool, at(T_POOL, q, "veps"))
                G.tensor_tensor(rstd[:, :], rstd[:, :], mhalf, ALU.pow).then_inc(tpool, 1)
                wait(tdve, at(T_DVE, q, "h0"))
                G.tensor_tensor(h0[:, :], h0[:, :], rows_s[:, D:2 * D], ALU.mult).then_inc(tpool, 1)
                wait(tpool, at(T_POOL, q, "hg"))
                G.tensor_tensor(h0[:, :], h0[:, :], rows_s[:, 2 * D:3 * D], ALU.add).then_inc(tpool, 1)

            def post_rstd(p):
                wait(rdve, at(R_DVE, p, "aggr"))
                G.tensor_scalar(prstd[:, :], pmv[:, 1:2], EPS, 1.0, ALU.add, ALU.mult).then_inc(rpool, 1)
                wait(rpool, at(R_POOL, p, "veps"))
                G.tensor_tensor(prstd[:, :], prstd[:, :], mhalf, ALU.pow).then_inc(rpool, 1)

            def post_keep(p):
                wait(rdve, at(R_DVE, p, "x5"))
                G.tensor_copy(xall[:, bass.ds(p, 1), :].rearrange("p a d -> p (a d)"), px5[:, :]).then_inc(rpool, 1)

            def post_scatter(p):
                wait(rdve, at(R_DVE, p, "idx"))
                for n in range(2):
                    G.indirect_dma_start(xg[:, :], bass.IndirectOffsetOnAxis(idx[:, n:n + 1], 0), px5[:, :], None)\
                        .then_inc(scat, 16)
                wait(scat, 32 * (p + 1))
                pool.sem_inc(rpool, 1)

            def step(b, i, j, ffn=True, att=True, post=True):
                if post:
                    post_rstd((i - 1) * CPB + j)
                    post_keep((i - 1) * CPB + j)
                if att:
                    if j == 0:
                        wait(l_x, 16 * (i + 2))
                    tail((i + 1) * CPB + j, b + 1, j)
                if post:
                    post_scatter((i - 1) * CPB + j)

            def split_half(n):
                wait(l_stage[n % 2], 16 * (n // 2 + 2))
                hi, lo = (w[:, 0, (n % 2) * W1C:(n % 2 + 1) * W1C] for w in (e_hi, e_lo))
                split(stage[:, n % 2, :], hi, lo, n)

            for n in range(2):
                wait(small_split, 2 * (n + 1))
                pool.sem_inc(stage_used, 1)
            wait(cst, 2)
            for j in range(CPB):
                step(-1, -1, j, ffn=False, post=False)
                for n in range(2):
                    wait(w_ready, 2 * j + n + 1)
                    pool.sem_inc(stage_used, 1)
            for j in range(CPB):
                step(0, 0, j, post=False)
            wait(z_done, 16 * E2)
            with pool.Fori(0, (NBLK - 2) // 2) as i:
                for b in (1, 2):
                    for j in range(CPB):
                        step(b, 2 * i + b, j)
            for j in range(CPB):
                step(NBLK - 1, NBLK - 1, j, att=False)
                if j in (1, 2):
                    wait(g2_done, ((NBLK - 1) * E1 + 1) * FC)
                    split_half(2 * E1 + j - 1)
            wait(ldve, last(L_DVE, "aggr"))
            G.tensor_scalar(rstd4, mv4[:, :, 1:2], EPS, 1.0, ALU.add, ALU.mult).then_inc(lpool, 1)
            wait(lpool, last(L_POOL, "veps"))
            G.tensor_tensor(rstd4, rstd4, mhalves[:, 0:CPB].unsqueeze(2), ALU.pow).then_inc(lpool, 1)
            wait(ldve, last(L_DVE, "idx"))
            for j in range(CPB):
                for n in range(2):
                    G.indirect_dma_start(xg[:, :], bass.IndirectOffsetOnAxis(idx4[:, j, n:n + 1], 0), xall[:, p_last + j, :],
                                         None).then_inc(scat, 16)

            wait(tab_ready, 1)
            with pool.Fori(0, E2 // 2) as ep:
                for s in range(2):
                    e = 2 * ep + s
                    tb = pool.value_load(tab[0:1, bass.ds(e + E2, 1)], min_val=0, max_val=MOST)
                    wait(u2_done, tb + 1)
                    if s == 0:
                        wait(g2_done, NBLK * E1 * FC)
                    for n in range(2):
                        wait(l_stage[n], 16 * (E1 + 3 + e))
                        split(stage[:, n, :], *(w[:, 1 - s, n * W1C:(n + 1) * W1C] for w in (e_hi, e_lo)),
                              2 * E1 + 2 + 2 * e + n)

            ng = pool.value_load(tab[0:1, 3 * E2:3 * E2 + 1], min_val=1, max_val=MOST)
            wait(y_out, 16 * (ng + 1))
            wait(tail_done, 16 * (E2 + 1))

            def rstds(i):
                first, end = GROUPS[i]
                n = end - first
                wait(stat_done, 2 * end)
                G.tensor_scalar(frs[:, i % 2, 0:n], fmv[:, i % 2, 0:n, 1], EPS, 1.0, ALU.add, ALU.mult).then_inc(feps, 1)
                wait(feps, i + 1)
                G.tensor_tensor(frs[:, i % 2, 0:n], frs[:, i % 2, 0:n], mhalves[:, 0:n], ALU.pow).then_inc(frstd, 1)

            for i, (first, end) in enumerate(GROUPS):
                for n in range(first, end):
                    if n >= NR:
                        wait(sum_done, 2 * (n - NR + 1))
                    for a in range(2):
                        G.indirect_dma_start(rows8[:, n % NR, a, :], None, yg[0:MOST * TILE, :],
                                             bass.IndirectOffsetOnAxis(posy[:, n, a:a + 1], 0)).then_inc(l_y[n % NR], 16)
                    if i and n == first + 2:
                        rstds(i - 1)
            rstds(len(GROUPS) - 1)


def _layout(a):
    f = {k: np.ascontiguousarray(np.asarray(v)) for k, v in a.items()}
    part = lambda m: m.reshape(KD, P, -1).transpose(1, 0, 2).reshape(P, -1)
    at, ff = "L0_attn_", "L0_ffn_"
    x = f[at + "x"]
    xpad = np.concatenate([np.zeros((B, 2, D), x.dtype), x], axis=1)
    xT = np.ascontiguousarray(xpad.transpose(2, 0, 1).reshape(KD, P, B, T + 2).transpose(1, 0, 2, 3))
    small = np.concatenate([part(f[at + n].T) for n in ("w_pw", "w_qkv", "w_o", "w_gate", "w_moe_gate")]
                           + [part(f[ff + "W_router"])], axis=1)
    wdw = f[at + "w_dw"].reshape(KD, P, 3).transpose(1, 0, 2).reshape(P, -1)
    rows = np.concatenate([f[at + "b_gate"], f[at + "ln_g"], f[at + "ln_b"], f[ff + "b_router"]])
    moe1 = np.concatenate([np.concatenate([part(f[at + "w1"][e].T),
                                           f[at + "w2"][e].T.reshape(FC, P, D).transpose(1, 0, 2).reshape(P, -1)], axis=1)
                           for e in range(E1)], axis=1)
    moe1_b = f[at + "b1"].reshape(E1 * FC, P).T
    moe2 = np.stack([np.concatenate([part(f[ff + "W1"][e]),
                                     f[ff + "W2"][e].reshape(FC, P, D).transpose(1, 0, 2).reshape(P, -1)], axis=1)
                     for e in range(E2)])
    moe2_b = f[ff + "b1"].reshape(E2 * FC, P).T
    b2 = np.concatenate([f[at + "b2"].reshape(-1), f[ff + "b2"].reshape(-1)])
    b2rows = np.concatenate([np.stack([b2, b2]), np.eye(2, dtype=np.float32)], axis=1)
    inv_freq = (1.0 / np.float32(10000.0) ** (np.arange(0, DH, 2, dtype=np.float32) / np.float32(DH))).astype(np.float32)
    theta = np.arange(T, dtype=np.float32)[:, None] * inv_freq[None, :]
    cos, sin = np.cos(theta), np.sin(theta)
    rope = np.stack([np.repeat(cos, 2, axis=1), np.stack([-sin, sin], axis=-1).reshape(T, DH)], axis=1) * INV
    rope = rope.astype(np.float32).reshape(T // P, P, 2, DH).transpose(1, 0, 2, 3)
    p = np.arange(P)
    chunks = np.arange(NCH + 1)
    keep = (chunks % (T // CH) != 0).astype(np.float32)
    masks = np.concatenate([
        np.eye(P), p[:, None] <= p[None, :], (p[:, None] // DH) == (np.arange(H // 2 * HE)[None, :] // HE),
        np.tile(keep, (P, 1)), np.tile(1 - keep, (P, 1)), np.tile(np.arange(E2), (P, 1)),
        np.tile(np.arange(E2) * CAP, (P, 1))], axis=1).astype(np.float32)
    arrays = dict(x=x.reshape(NTOK, D), xT=xT, small=small, wdw=wdw, rows=rows, moe1=moe1, moe1_b=moe1_b, moe2=moe2,
                  moe2_b=moe2_b, b2rows=b2rows, rope=rope, masks=masks)
    return {k: np.ascontiguousarray(v) for k, v in arrays.items()}


def kernel(**inputs):
    import concourse.bacc as bacc
    from concourse.bass_utils import run_bass_kernel_spmd

    nc = bacc.Bacc("TRN2", target_bir_lowering=False, num_devices=1)
    arrays = _layout(inputs)
    args = {k: nc.dram_tensor("in_" + k, a.shape, mybir.dt.from_np(a.dtype), kind="ExternalInput").ap()
            for k, a in arrays.items()}
    out = nc.dram_tensor("out_0", (NTOK, D), F32, kind="ExternalOutput").ap()
    build(nc, out=out, **args)
    r = run_bass_kernel_spmd(nc, [{"in_" + k: a for k, a in arrays.items()}], core_ids=[0])
    return r.results[0]["out_0"].reshape(B, T, D)
```
